# Optimizing a Trainium2 kernel written in Bass

```python
import numpy as np
import jax
import jax.numpy as jnp

def _softmax(x, axis=-1):
    return jax.nn.softmax(x, axis=axis)

def _gelu(x):
    return jax.nn.gelu(x, approximate=True)

def _silu(x):
    return jax.nn.silu(x)

def _sigmoid(x):
    return jax.nn.sigmoid(x)

def _layernorm(x, axis=-1, eps=1e-05):
    m = jnp.mean(x, axis=axis, keepdims=True)
    v = jnp.var(x, axis=axis, keepdims=True)
    return (x - m) / jnp.sqrt(v + eps)

def _scatter_add(tgt, idx, src, axis=0):
    return tgt.at[idx].add(src)

def _segment_sum(src, seg, n):
    return jax.ops.segment_sum(src, seg, n)
kernel_name = 'mk_gnn_resnorm_d4_gnn_r8_ea52d0'

def setup_inputs(seed: int=0):
    np.random.seed(seed)
    _w = jnp.asarray

    def _rec_inputs():
        import jax
        import jax.numpy as jnp
        _gk = jax.random.key(seed)
        x = -0.000202 + 1 * jax.random.normal(jax.random.fold_in(_gk, 1), (6250, 128), jnp.float32)
        _s = jax.random.randint(jax.random.fold_in(_gk, 2), (50000,), 0, 6250, jnp.int32)
        _d = jax.random.randint(jax.random.fold_in(_gk, 3), (50000,), 0, 6250, jnp.int32)
        _loop = jnp.arange(6250, dtype=jnp.int32)
        src = jnp.concatenate([_s, _d, _loop])
        dst = jnp.concatenate([_d, _s, _loop])
        _o = jnp.argsort(dst, stable=True)
        src = src[_o]
        dst = dst[_o]
        edge_attr_4 = -0.000107899 + 1.00008 * jax.random.normal(jax.random.fold_in(_gk, 11), (106250, 4), jnp.float32)
        edge_attr_8 = jax.random.uniform(jax.random.fold_in(_gk, 12), (106250, 8), jnp.float32, 0.0, 1)
        return (x, src, dst, edge_attr_4, edge_attr_8)
    x, src, dst, edge_attr_4, edge_attr_8 = _rec_inputs()

    def _L0_gnn_setup():
        import jax, jax.numpy as jnp
        import numpy as np
        N_NODES = 6250
        N_EDGES = 100000
        DIM = 128
        BN_EPS = 1e-05
        key = jax.random.key(seed)
        ks = jax.random.split(key, 12)
        d = DIM
        s = 1.0 / np.sqrt(d)
        x = jax.random.normal(ks[0], (N_NODES, d), dtype=jnp.float32)
        edge_index = jax.random.randint(ks[1], (2, N_EDGES), 0, N_NODES, dtype=jnp.int64)
        W_msg = jax.random.uniform(ks[2], (d, d), jnp.float32, -s, s)
        b_msg = jax.random.uniform(ks[3], (d,), jnp.float32, -s, s)
        sa = 1.0 / np.sqrt(2 * d)
        W_att = jax.random.uniform(ks[4], (2 * d, 1), jnp.float32, -sa, sa)
        b_att = jax.random.uniform(ks[5], (1,), jnp.float32, -sa, sa)
        W_ih = jax.random.uniform(ks[6], (3 * d, d), jnp.float32, -s, s)
        b_ih = jax.random.uniform(ks[7], (3 * d,), jnp.float32, -s, s)
        W_hh = jax.random.uniform(ks[8], (3 * d, d), jnp.float32, -s, s)
        b_hh = jax.random.uniform(ks[9], (3 * d,), jnp.float32, -s, s)
        gamma = jnp.ones((d,), jnp.float32)
        beta = jnp.zeros((d,), jnp.float32)
        return {'x': x, 'edge_index': edge_index, 'W_msg': W_msg, 'b_msg': b_msg, 'W_att': W_att, 'b_att': b_att, 'W_ih': W_ih, 'b_ih': b_ih, 'W_hh': W_hh, 'b_hh': b_hh, 'gamma': gamma, 'beta': beta}
    _L0_gnn_all = _L0_gnn_setup()
    _L0_gnn_in = {k: v for k, v in _L0_gnn_all.items() if k in ('W_msg', 'b_msg', 'W_att', 'b_att', 'W_ih', 'b_ih', 'W_hh', 'b_hh', 'gamma', 'beta')}
    del _L0_gnn_all

    def _L1_gnn_setup():
        import jax, jax.numpy as jnp
        import numpy as np
        N_NODES = 6250
        N_EDGES = 80000
        D = 128
        L = 3

        def _transformer_conv(x, src, dst, Wq, bq, Wk, bk, Wv, bv, Ws, bs):
            n = x.shape[0]
            d = Wq.shape[1]
            q = x @ Wq + bq
            k = x @ Wk + bk
            v = x @ Wv + bv
            skip = x @ Ws + bs
            logits = jnp.sum(q[dst] * k[src], axis=-1) * (1.0 / jnp.sqrt(jnp.asarray(d, x.dtype)))
            m = jax.ops.segment_max(logits, dst, num_segments=n)
            e = jnp.exp(logits - m[dst])
            z = jax.ops.segment_sum(e, dst, num_segments=n)
            alpha = e / jnp.maximum(z[dst], 1e-16)
            agg = jax.ops.segment_sum(alpha[:, None] * v[src], dst, num_segments=n)
            return agg + skip
        key = jax.random.key(seed)
        ks = jax.random.split(key, 10)
        s = 1.0 / np.sqrt(D)
        inp = {'x': jax.random.normal(ks[0], (N_NODES, D), dtype=jnp.float32), 'edge_index': jax.random.randint(ks[1], (2, N_EDGES), 0, N_NODES, dtype=jnp.int32), 'Wq': jax.random.normal(ks[2], (L, D, D), dtype=jnp.float32) * s, 'bq': jax.random.normal(ks[3], (L, D), dtype=jnp.float32) * 0.02, 'Wk': jax.random.normal(ks[4], (L, D, D), dtype=jnp.float32) * s, 'bk': jax.random.normal(ks[5], (L, D), dtype=jnp.float32) * 0.02, 'Wv': jax.random.normal(ks[6], (L, D, D), dtype=jnp.float32) * s, 'bv': jax.random.normal(ks[7], (L, D), dtype=jnp.float32) * 0.02, 'Ws': jax.random.normal(ks[8], (L, D, D), dtype=jnp.float32) * s, 'bs': jax.random.normal(ks[9], (L, D), dtype=jnp.float32) * 0.02}
        return inp
    _L1_gnn_all = _L1_gnn_setup()
    _L1_gnn_in = {k: v for k, v in _L1_gnn_all.items() if k in ('Wq', 'bq', 'Wk', 'bk', 'Wv', 'bv', 'Ws', 'bs')}
    del _L1_gnn_all

    def _L2_gnn_setup():
        import jax, jax.numpy as jnp
        import numpy as np
        N_NODES = 12500
        N_EDGES = 400000
        D = 128
        key = jax.random.key(seed)
        ks = jax.random.split(key, 8)
        scale = 1.0 / np.sqrt(D)
        inp = {'x': jax.random.normal(ks[0], (N_NODES, D), jnp.float32), 'edge_index': jax.random.randint(ks[1], (2, N_EDGES), 0, N_NODES, jnp.int64)}
        for i in range(3):
            inp[f'W_l{i}'] = jax.random.normal(ks[2 + 2 * i], (D, D), jnp.float32) * scale
            inp[f'b{i}'] = jnp.zeros((D,), jnp.float32)
            inp[f'W_r{i}'] = jax.random.normal(ks[3 + 2 * i], (D, D), jnp.float32) * scale
        return inp
    _L2_gnn_all = _L2_gnn_setup()
    _L2_gnn_in = {k: v for k, v in _L2_gnn_all.items() if k in ('W_l0', 'b0', 'W_r0', 'W_l1', 'b1', 'W_r1', 'W_l2', 'b2', 'W_r2')}
    del _L2_gnn_all

    def _L3_gnn_setup():
        import jax, jax.numpy as jnp
        import numpy as np
        MUL = 32
        N_NODES = 6250
        N_EDGES = 100000
        R3 = np.sqrt(3.0).astype(np.float32)
        key = jax.random.key(seed)
        ks = jax.random.split(key, 12)
        inp = {}
        inp['node_feats'] = jax.random.normal(ks[0], (N_NODES, 4 * MUL), dtype=jnp.float32)
        inp['edge_attrs'] = jax.random.normal(ks[1], (N_EDGES, 4), dtype=jnp.float32)
        inp['edge_feats'] = jax.random.uniform(ks[2], (N_EDGES, 8), dtype=jnp.float32)
        inp['edge_index'] = jax.random.randint(ks[3], (2, N_EDGES), 0, N_NODES)
        inp['W_up_s'] = jax.random.normal(ks[4], (MUL, MUL), dtype=jnp.float32)
        inp['W_up_v'] = jax.random.normal(ks[5], (MUL, MUL), dtype=jnp.float32)
        inp['A1'] = jax.random.normal(ks[6], (8, 64), dtype=jnp.float32) / np.sqrt(8.0)
        inp['b1'] = jnp.zeros((64,), dtype=jnp.float32)
        inp['A2'] = jax.random.normal(ks[7], (64, 64), dtype=jnp.float32) / np.sqrt(64.0)
        inp['b2'] = jnp.zeros((64,), dtype=jnp.float32)
        inp['A3'] = jax.random.normal(ks[8], (64, 4 * MUL), dtype=jnp.float32) * (10.0 * np.sqrt(6.0 / (64 + 4 * MUL)))
        inp['W_out_s'] = jax.random.normal(ks[9], (2 * MUL, MUL), dtype=jnp.float32)
        inp['W_out_v'] = jax.random.normal(ks[10], (2 * MUL, MUL), dtype=jnp.float32)
        return inp
    _L3_gnn_all = _L3_gnn_setup()
    _L3_gnn_in = {k: v for k, v in _L3_gnn_all.items() if k in ('W_up_s', 'W_up_v', 'A1', 'b1', 'A2', 'b2', 'A3', 'W_out_s', 'W_out_v')}
    del _L3_gnn_all
    return {'x': x, 'src': src, 'dst': dst, 'edge_attr_4': edge_attr_4, 'edge_attr_8': edge_attr_8, 'L0_gnn_W_msg': _L0_gnn_in['W_msg'], 'L0_gnn_b_msg': _L0_gnn_in['b_msg'], 'L0_gnn_W_att': _L0_gnn_in['W_att'], 'L0_gnn_b_att': _L0_gnn_in['b_att'], 'L0_gnn_W_ih': _L0_gnn_in['W_ih'], 'L0_gnn_b_ih': _L0_gnn_in['b_ih'], 'L0_gnn_W_hh': _L0_gnn_in['W_hh'], 'L0_gnn_b_hh': _L0_gnn_in['b_hh'], 'L0_gnn_gamma': _L0_gnn_in['gamma'], 'L0_gnn_beta': _L0_gnn_in['beta'], 'L1_gnn_Wq': _L1_gnn_in['Wq'], 'L1_gnn_bq': _L1_gnn_in['bq'], 'L1_gnn_Wk': _L1_gnn_in['Wk'], 'L1_gnn_bk': _L1_gnn_in['bk'], 'L1_gnn_Wv': _L1_gnn_in['Wv'], 'L1_gnn_bv': _L1_gnn_in['bv'], 'L1_gnn_Ws': _L1_gnn_in['Ws'], 'L1_gnn_bs': _L1_gnn_in['bs'], 'L2_gnn_W_l0': _L2_gnn_in['W_l0'], 'L2_gnn_b0': _L2_gnn_in['b0'], 'L2_gnn_W_r0': _L2_gnn_in['W_r0'], 'L2_gnn_W_l1': _L2_gnn_in['W_l1'], 'L2_gnn_b1': _L2_gnn_in['b1'], 'L2_gnn_W_r1': _L2_gnn_in['W_r1'], 'L2_gnn_W_l2': _L2_gnn_in['W_l2'], 'L2_gnn_b2': _L2_gnn_in['b2'], 'L2_gnn_W_r2': _L2_gnn_in['W_r2'], 'L3_gnn_W_up_s': _L3_gnn_in['W_up_s'], 'L3_gnn_W_up_v': _L3_gnn_in['W_up_v'], 'L3_gnn_A1': _L3_gnn_in['A1'], 'L3_gnn_b1': _L3_gnn_in['b1'], 'L3_gnn_A2': _L3_gnn_in['A2'], 'L3_gnn_b2': _L3_gnn_in['b2'], 'L3_gnn_A3': _L3_gnn_in['A3'], 'L3_gnn_W_out_s': _L3_gnn_in['W_out_s'], 'L3_gnn_W_out_v': _L3_gnn_in['W_out_v']}

def reference(x, src, dst, edge_attr_4, edge_attr_8, L0_gnn_W_msg, L0_gnn_b_msg, L0_gnn_W_att, L0_gnn_b_att, L0_gnn_W_ih, L0_gnn_b_ih, L0_gnn_W_hh, L0_gnn_b_hh, L0_gnn_gamma, L0_gnn_beta, L1_gnn_Wq, L1_gnn_bq, L1_gnn_Wk, L1_gnn_bk, L1_gnn_Wv, L1_gnn_bv, L1_gnn_Ws, L1_gnn_bs, L2_gnn_W_l0, L2_gnn_b0, L2_gnn_W_r0, L2_gnn_W_l1, L2_gnn_b1, L2_gnn_W_r1, L2_gnn_W_l2, L2_gnn_b2, L2_gnn_W_r2, L3_gnn_W_up_s, L3_gnn_W_up_v, L3_gnn_A1, L3_gnn_b1, L3_gnn_A2, L3_gnn_b2, L3_gnn_A3, L3_gnn_W_out_s, L3_gnn_W_out_v):
    import jax
    import jax.numpy as jnp

    def _L0_gnn_ref(x, edge_index, W_msg, b_msg, W_att, b_att, W_ih, b_ih, W_hh, b_hh, gamma, beta):
        import jax, jax.numpy as jnp
        import numpy as np
        N_NODES = 6250
        N_EDGES = 100000
        DIM = 128
        BN_EPS = 1e-05
        num_nodes, d = x.shape
        src = edge_index[0]
        dst = edge_index[1]
        xs = x[src]
        xd = x[dst]
        att = jax.nn.sigmoid(xs @ W_att[:d] + xd @ W_att[d:] + b_att)
        messages = (xs @ W_msg + b_msg) * att
        aggregated = jax.ops.segment_sum(messages, dst, num_segments=num_nodes)
        gi = aggregated @ W_ih.T + b_ih
        gh = x @ W_hh.T + b_hh
        i_r, i_z, i_n = jnp.split(gi, 3, axis=1)
        h_r, h_z, h_n = jnp.split(gh, 3, axis=1)
        r = jax.nn.sigmoid(i_r + h_r)
        z = jax.nn.sigmoid(i_z + h_z)
        n = jnp.tanh(i_n + r * h_n)
        h_new = (1.0 - z) * n + z * x
        mean = jnp.mean(h_new, axis=0)
        var = jnp.var(h_new, axis=0)
        return gamma * (h_new - mean) * jax.lax.rsqrt(var + BN_EPS) + beta

    def _L1_gnn_ref(x, edge_index, Wq, bq, Wk, bk, Wv, bv, Ws, bs):
        import jax, jax.numpy as jnp
        import numpy as np
        N_NODES = 6250
        N_EDGES = 80000
        D = 128
        L = 3

        def _transformer_conv(x, src, dst, Wq, bq, Wk, bk, Wv, bv, Ws, bs):
            n = x.shape[0]
            d = Wq.shape[1]
            q = x @ Wq + bq
            k = x @ Wk + bk
            v = x @ Wv + bv
            skip = x @ Ws + bs
            logits = jnp.sum(q[dst] * k[src], axis=-1) * (1.0 / jnp.sqrt(jnp.asarray(d, x.dtype)))
            m = jax.ops.segment_max(logits, dst, num_segments=n)
            e = jnp.exp(logits - m[dst])
            z = jax.ops.segment_sum(e, dst, num_segments=n)
            alpha = e / jnp.maximum(z[dst], 1e-16)
            agg = jax.ops.segment_sum(alpha[:, None] * v[src], dst, num_segments=n)
            return agg + skip
        src = edge_index[0]
        dst = edge_index[1]
        n_layers = Wq.shape[0]
        h = x
        for l in range(n_layers):
            h = _transformer_conv(h, src, dst, Wq[l], bq[l], Wk[l], bk[l], Wv[l], bv[l], Ws[l], bs[l])
            if l < n_layers - 1:
                h = jax.nn.relu(h)
        return h

    def _L2_gnn_ref(x, edge_index, W_l0, b0, W_r0, W_l1, b1, W_r1, W_l2, b2, W_r2):
        import jax, jax.numpy as jnp
        import numpy as np
        N_NODES = 12500
        N_EDGES = 400000
        D = 128
        src, dst = (edge_index[0], edge_index[1])
        n = x.shape[0]
        deg = jax.ops.segment_sum(jnp.ones(src.shape[0], x.dtype), dst, num_segments=n)
        inv_deg = (1.0 / jnp.maximum(deg, 1.0))[:, None]

        def sage_conv(h, Wl, b, Wr):
            agg = jax.ops.segment_sum(h[src], dst, num_segments=n) * inv_deg
            return agg @ Wl + b + h @ Wr
        h = jax.nn.relu(sage_conv(x, W_l0, b0, W_r0))
        h = jax.nn.relu(sage_conv(h, W_l1, b1, W_r1))
        return sage_conv(h, W_l2, b2, W_r2)

    def _L3_gnn_ref(node_feats, edge_attrs, edge_feats, W_up_s, W_up_v, A1, b1, A2, b2, A3, W_out_s, W_out_v, edge_index):
        import jax, jax.numpy as jnp
        import numpy as np
        MUL = 32
        N_NODES = 6250
        N_EDGES = 100000
        R3 = np.sqrt(3.0).astype(np.float32)
        num_nodes = node_feats.shape[0]
        sender, receiver = (edge_index[0], edge_index[1])
        s = node_feats[:, :MUL]
        v = node_feats[:, MUL:].reshape(num_nodes, MUL, 3)
        inv = 1.0 / np.sqrt(MUL).astype(np.float32)
        s = s @ W_up_s * inv
        v = jnp.einsum('nui,uw->nwi', v, W_up_v) * inv
        h = jax.nn.silu(edge_feats @ A1 + b1)
        h = jax.nn.silu(h @ A2 + b2)
        tpw = h @ A3
        w0, w1, w2, w3 = jnp.split(tpw, 4, axis=1)
        ss = s[sender]
        vs = v[sender]
        y_s = edge_attrs[:, :1]
        y_v = edge_attrs[:, 1:4]
        out_s0 = ss * y_s * w0
        out_s3 = jnp.einsum('eui,ei->eu', vs, y_v) / R3 * w3
        out_v1 = ss[:, :, None] * y_v[:, None, :] * w1[:, :, None]
        out_v2 = vs * y_s[:, :, None] * w2[:, :, None]
        E = ss.shape[0]
        mji = jnp.concatenate([out_s0, out_s3, out_v1.reshape(E, 3 * MUL), out_v2.reshape(E, 3 * MUL)], axis=1)
        message = jax.ops.segment_sum(mji, receiver, num_segments=num_nodes) / 10.0
        ms = message[:, :2 * MUL]
        mv = message[:, 2 * MUL:].reshape(num_nodes, 2 * MUL, 3)
        inv2 = 1.0 / np.sqrt(2 * MUL).astype(np.float32)
        out_s = ms @ W_out_s * inv2
        out_v = jnp.einsum('nui,uw->nwi', mv, W_out_v) * inv2
        return jnp.concatenate([out_s, out_v.reshape(num_nodes, 3 * MUL)], axis=1)
    edge_index = jnp.stack([src, dst])
    x = _layernorm(x + _L0_gnn_ref(x, edge_index, L0_gnn_W_msg, L0_gnn_b_msg, L0_gnn_W_att, L0_gnn_b_att, L0_gnn_W_ih, L0_gnn_b_ih, L0_gnn_W_hh, L0_gnn_b_hh, L0_gnn_gamma, L0_gnn_beta), axis=-1)
    x = _layernorm(x + _L1_gnn_ref(x, edge_index, L1_gnn_Wq, L1_gnn_bq, L1_gnn_Wk, L1_gnn_bk, L1_gnn_Wv, L1_gnn_bv, L1_gnn_Ws, L1_gnn_bs), axis=-1)
    x = _layernorm(x + _L2_gnn_ref(x, edge_index, L2_gnn_W_l0, L2_gnn_b0, L2_gnn_W_r0, L2_gnn_W_l1, L2_gnn_b1, L2_gnn_W_r1, L2_gnn_W_l2, L2_gnn_b2, L2_gnn_W_r2), axis=-1)
    x = _layernorm(x + _L3_gnn_ref(x, edge_attr_4, edge_attr_8, L3_gnn_W_up_s, L3_gnn_W_up_v, L3_gnn_A1, L3_gnn_b1, L3_gnn_A2, L3_gnn_b2, L3_gnn_A3, L3_gnn_W_out_s, L3_gnn_W_out_v, edge_index), axis=-1)
    return x

_drawn_inputs = setup_inputs


def setup_inputs(seed=0):
    import zlib

    import numpy as np

    out = dict(_drawn_inputs(seed))
    spreads = {'L0_gnn_gamma': (1.0, 0.2),
     'L0_gnn_beta': (0.0, 0.1),
     'L2_gnn_b0': (0.0, 0.1),
     'L2_gnn_b1': (0.0, 0.1),
     'L2_gnn_b2': (0.0, 0.1),
     'L3_gnn_b1': (0.0, 0.1),
     'L3_gnn_b2': (0.0, 0.1)}
    factors = {'L0_gnn_b_ih': 5.565, 'L0_gnn_b_hh': 6.571, 'L1_gnn_bq': 22.647, 'L1_gnn_bk': 64.0}
    for name, (base, spread) in spreads.items():
        noise = np.random.default_rng([zlib.crc32(name.encode()), seed]).standard_normal(out[name].shape)
        drawn = base * np.exp(spread * noise) if base else spread * noise
        out[name] = jnp.asarray(drawn.astype(out[name].dtype))
    for name, factor in factors.items():
        out[name] = (out[name] * factor).astype(out[name].dtype)
    return out
```

```python
from contextlib import ExitStack

import numpy as np

import concourse.bass as bass
from concourse import mybir

F32 = mybir.dt.float32
I32 = mybir.dt.int32
ALU = mybir.AluOpType
ACT = mybir.ActivationFunctionType
AX = mybir.AxisListType

DVE, PE = mybir.EngineType.DVE, mybir.EngineType.PE
P = 128
NODES = 6250
EDGES = 106250
D = 128
BLOCKS = -(-NODES // P)
NP = BLOCKS * P
NW = NP + P
SLOTS = 16
QUAD = 4
QUADS = SLOTS // QUAD
HALF = SLOTS // 2
TURNS = -(-EDGES // (P * SLOTS))
TILES = TURNS * SLOTS
EP = TILES * P
LINES = EP // (8 * P)
LINE = EP // LINES
CHUNK = NP // 14
HEADS_L1 = 3
MUL = 32
HID = 64
FEATS = 8
NO_NODE = 1 << 20
EPS = 1e-5
BIG = 1e38

assert CHUNK * 14 == NP and CHUNK <= 512 and LINE == 8 * P and LINES <= P and TILES % 8 == 0


class Count:

    def __init__(self, sem, value=0):
        self.sem, self.value = sem, value


class Program:
    def __init__(self, nc, ctx):
        self.nc, self.ctx = nc, ctx
        self.engines = {"pe": nc.tensor, "act": nc.scalar, "dve": nc.vector, "pool": nc.gpsimd, "sp": nc.sync}
        self.done = {k: self.count(f"done_{k}") for k in self.engines}
        self.lanes = [self.count(f"lane{i}") for i in range(8)]
        self.lane_at = 0

    def sbuf(self, name, shape, dt=F32):
        return self.ctx.enter_context(self.nc.sbuf_tensor(name, shape, dt))

    def count(self, name):
        return Count(self.ctx.enter_context(self.nc.semaphore(name)))

    def wait(self, engine, *marks):
        for m in marks:
            if m is not None:
                self.engines[engine].wait_ge(m[0].sem, m[1])

    def mark(self, engine, instruction):
        c = self.done[engine]
        c.value += 1
        instruction.then_inc(c.sem, 1)
        return c, c.value

    def dma(self, engine, out, in_):
        lane = self.lanes[self.lane_at % len(self.lanes)]
        self.lane_at += 1
        if lane.value:
            self.engines[engine].wait_ge(lane.sem, lane.value)
        lane.value += 16
        self.engines[engine].dma_start(out, in_).then_inc(lane.sem, 16)
        return lane, lane.value

    def all_dmas(self, engine):
        for lane in self.lanes:
            if lane.value:
                self.engines[engine].wait_ge(lane.sem, lane.value)

    def barrier(self):
        self.all_dmas("sp")
        self.nc.all_engine_barrier()


def build_program(nc, a, out):
    with ExitStack() as ctx:
        pr = Program(nc, ctx)
        sb, wait, mark, dma = pr.sbuf, pr.wait, pr.mark, pr.dma
        pe, act, dve, pool, sp = nc.tensor, nc.scalar, nc.vector, nc.gpsimd, nc.sync
        bank = [ctx.enter_context(nc.psum_tensor(f"bank{i}", [P, 512], F32)) for i in range(8)]

        def dram(name, shape):
            return nc.dram_tensor(name, shape, F32, kind="Internal").ap()

        table_gated = dram("table_gated", (NP, D + 1))
        table_kv = dram("table_kv", (NP, 2 * D))
        table = [dram(f"table_h{i}", (NP, D)) for i in range(2)]
        stash = dram("stash", (2 * TURNS, P, HALF * D))

        ident = sb("ident", [P, P])
        ramp = sb("ramp", [P, P])
        ones = sb("ones", [P, P])
        src_idx = sb("src_idx", [P, TILES + SLOTS], I32)
        start = sb("start", [P, TILES], I32)
        place = sb("place", [P, TILES])
        same_prev = sb("same_prev", [P, LINE])
        clamp_prev = sb("clamp_prev", [P, LINE])
        clamp_next = sb("clamp_next", [P, LINE])
        rows = sb("rows", [1, 6, P])
        cols = sb("cols", [P, 8])
        xT = sb("xT", [P, NP])
        hT = sb("hT", [P, NP])
        qT = sb("qT", [P, NW])
        sums = sb("sums", [P, 2, NW])
        aggT = sums[:, 0, :]
        spare = sums[:, 1, :]
        logit = sb("logit", [P, TILES])
        weight = sb("weight", [P, TILES])
        wts = sb("wts", [P, 6 * D])
        rowsW = sb("rowsW", [1, 2 * D])
        biasc = sb("biasc", [P, 8])
        small = sb("small", [P, 16])

        G = sb("G", [P, SLOTS, 2 * D])
        OH = sb("OH", [P, SLOTS, P])
        KT = sb("KT", [P, SLOTS, P])
        idx = sb("idx", [P, SLOTS], I32)
        per_slot = sb("per_slot", [P, 3, SLOTS])
        stats = sb("stats", [P, BLOCKS, 6])
        moments = sb("moments", [P, BLOCKS, 2])

        m_in = [dma("sp", src_idx[:], a["src_tile"]), dma("sp", start[:], a["dst_first"].rearrange("(a t) -> a t", a=1).to_broadcast([P, TILES]))]
        dst_i = logit[:].bitcast(I32)
        m_dst = dma("sp", dst_i, a["dst_tile"])
        lines = [spare[0:LINES, k * LINE:(k + 1) * LINE].bitcast(I32) for k in range(3)]
        m_lines = [dma("sp", lines[k], a["dst_line"][k:k + EP].rearrange("(i r) -> i r", i=LINES)) for k in range(3)]
        m_x = []
        xN = hT[:].rearrange("p (b d) -> p b d", d=D)
        for b0 in range(0, BLOCKS, 7):
            m_x.append(dma("act", xN[:, b0:b0 + 7, :], a["x"].rearrange("(b p) d -> p b d", p=P)[:, b0:b0 + 7, :]))
        m_ramp = mark("pool", pool.iota(ramp[:], [[1, P]], base=0, channel_multiplier=0, allow_small_or_imprecise_dtypes=True))
        m = mark("pool", pool.memset(ident[:], 0.0))
        wait("pool", m)
        m_ident = mark("pool", pool.affine_select(out=ident[:], in_=ident[:], compare_op=ALU.not_equal, fill=1.0, base=0, pattern=[[-1, P]], channel_multiplier=1))
        m_ones = mark("dve", dve.memset(ones[:], 1.0))
        wait("dve", *m_in, m_dst)
        m1 = mark("dve", dve.tensor_scalar(start[:], start[:], float(NODES - 1), None, ALU.min))
        m2 = mark("dve", dve.tensor_copy(weight[:], dst_i))
        wait("dve", m1, m2)
        m3 = mark("dve", dve.tensor_tensor(place[:], weight[:], start[:], ALU.subtract))
        wait("dve", *m_lines)
        before, here, after = lines
        eq_next = spare[0:LINES, 3 * LINE:4 * LINE]
        m4 = mark("dve", dve.tensor_tensor(same_prev[0:LINES, :], here, before, ALU.is_equal))
        m5 = mark("dve", dve.tensor_tensor(eq_next, here, after, ALU.is_equal))
        wait("dve", m4, m5)
        dve.tensor_scalar(clamp_prev[0:LINES, :], same_prev[0:LINES, :], 2 * BIG, -BIG, ALU.mult, ALU.add)
        m6 = mark("dve", dve.tensor_scalar(clamp_next[0:LINES, :], eq_next, 2 * BIG, -BIG, ALU.mult, ALU.add))
        wait("dve", m6)
        dve.tensor_reduce(cols[0:LINES, 0:1], same_prev[0:LINES, :], AX.X, ALU.min)
        dve.tensor_reduce(cols[0:LINES, 1:2], clamp_prev[0:LINES, :], AX.X, ALU.min)
        m7 = mark("dve", dve.tensor_reduce(cols[0:LINES, 2:3], clamp_next[0:LINES, :], AX.X, ALU.min))
        wait("pe", m7, m_ident)
        for k in range(3):
            m8 = mark("pe", pe.matmul(bank[0][0:1, k * P:k * P + LINES], cols[0:LINES, k:k + 1], ident[0:LINES, 0:LINES], start=True, stop=True))
        wait("dve", m8)
        for k in range(3):
            m9 = mark("dve", dve.tensor_copy(rows[0:1, k, 0:LINES], bank[0][0:1, k * P:k * P + LINES]))
        ROW_SAME, ROW_PREV, ROW_NEXT, ROW_END, ROW_CARRY = range(5)

        free = [None] * 8
        free[0] = m9

        def transpose_blocks(dstT, srcN, ready):
            last = None
            for g, b0 in enumerate(range(0, BLOCKS, QUAD)):
                nb = min(QUAD, BLOCKS - b0)
                k = g % 8
                wait("pe", free[k], *ready)
                for j in range(nb):
                    m = pe.transpose(bank[k][:, j * P:(j + 1) * P], srcN[:, b0 + j, :], ident[:])
                m = mark("pe", m)
                who, e = (("act", act), ("dve", dve))[g % 2]
                wait(who, m)
                free[k] = last = mark(who, (e.copy if who == "act" else e.tensor_copy)(dstT[:, b0 * P:(b0 + nb) * P], bank[k][:, 0:nb * P]))
            return last

        def nodes_T(dstT, terms, func, bias):
            for c in range(14):
                k = c % 8
                cut = slice(c * CHUNK, (c + 1) * CHUNK)
                wait("pe", free[k])
                for n, (w, nodesT) in enumerate(terms):
                    m = pe.matmul(bank[k][:, 0:CHUNK], w, nodesT[:, cut], start=n == 0, stop=n == len(terms) - 1)
                m = mark("pe", m)
                wait("act", m)
                free[k] = mark("act", act.activation(dstT[:, cut], bank[k][:, 0:CHUNK], func, bias=bias))

        def nodes_N(block_done, terms, width, bias_row):
            for b in range(BLOCKS):
                k = b % 8
                wait("pe", free[k])
                if bias_row is not None:
                    pe.matmul(bank[k][:, 0:width], ones[0:1, :], bias_row, start=True, stop=False)
                for n, (nodesT, w) in enumerate(terms):
                    m = pe.matmul(bank[k][:, 0:width], nodesT[:, b * P:(b + 1) * P], w, start=n == 0 and bias_row is None, stop=n == len(terms) - 1)
                free[k] = block_done(b, k, mark("pe", m))

        stage_at = [0]
        stage_free = [None] * 8

        def make_table(dst, terms, width, bias_row, func=ACT.Copy, scale=1.0):
            stage = G[:, 0:SLOTS // 2, :] if width > D + 1 else G[:, 0:SLOTS // 2, :]

            def done(b, k, m):
                s = stage_at[0] % 8
                stage_at[0] += 1
                wait("act", m, stage_free[s])
                r = mark("act", act.activation(stage[:, s, 0:width], bank[k][:, 0:width], func, scale=scale))
                wait("sp", r)
                stage_free[s] = dma("sp", dst[b * P:(b + 1) * P, :], stage[:, s, 0:width])
                return r
            nodes_N(done, terms, width, bias_row)

        def layer_norm(dstN, terms, bias_row):
            def done(b, k, m):
                wait("dve", m)
                s = mark("dve", dve.bn_stats(stats[:, b, :], bank[k][:, 0:D]))
                wait("act", s)
                return mark("act", act.copy(dstN[:, b, :], bank[k][:, 0:D]))
            nodes_N(done, terms, D, bias_row)
            wait("dve", (pr.done["dve"], pr.done["dve"].value), (pr.done["act"], pr.done["act"].value))
            for b in range(BLOCKS):
                m = mark("dve", dve.bn_aggr(moments[:, b, :], stats[:, b, :]))
            wait("dve", m)
            var = moments[:, :, 1]
            m = mark("dve", dve.tensor_scalar(var, var, EPS, None, ALU.add))
            wait("act", m)
            m = mark("act", act.activation(var, var, ACT.Sqrt))
            wait("dve", m)
            m = mark("dve", dve.reciprocal(var, var))
            wait("dve", m)
            for b in range(BLOCKS):
                m = mark("dve", dve.tensor_scalar(dstN[:, b, :], dstN[:, b, :], moments[:, b, 0:1], moments[:, b, 1:2], ALU.subtract, ALU.mult))
            return m

        def load_weights(parts):
            return [dma("sp", o, i) for o, i in parts]

        def zero_sums(whole=False):
            return mark("pool", pool.memset(sums[:, :, :] if whole else aggT, 0.0))

        def segments(values, result, kind):
            pr.barrier()
            line = spare[0:LINES, 0:LINE]
            fwd = spare[0:LINES, LINE:2 * LINE]
            back = spare[0:LINES, 2 * LINE:3 * LINE]
            lowest = -BIG if kind == "max" else 0.0
            keep = clamp_prev[0:LINES, :] if kind == "max" else same_prev[0:LINES, :]
            op_keep, op_take = (ALU.min, ALU.max) if kind == "max" else (ALU.mult, ALU.add)
            v = values.rearrange("p (i j) -> p j i", j=8)
            for j in range(8):
                m = mark("pe", pe.transpose(bank[j // 4][0:LINES, (j % 4) * P:(j % 4 + 1) * P], v[:, j, :], ident[:]))
            wait("dve", m)
            for h in range(2):
                m = mark("dve", dve.tensor_copy(line[:, h * 512:(h + 1) * 512], bank[h][0:LINES, :]))

            def carried(row_keep, end, reverse, lowest, op_keep, op_take, m_end):
                wait("pe", m_end)
                m = mark("pe", pe.matmul(bank[2][0:1, 0:LINES], end, ident[0:LINES, 0:LINES], start=True, stop=True))
                wait("dve", m)
                m = mark("dve", dve.tensor_copy(rows[0:1, ROW_END, 0:LINES], bank[2][0:1, 0:LINES]))
                carry = rows[0:1, ROW_CARRY, :]
                m0 = mark("dve", dve.memset(carry, lowest))
                wait("dve", m, m0)
                k, x = rows[0:1, row_keep, 0:LINES], rows[0:1, ROW_END, 0:LINES]
                if reverse:
                    m = mark("dve", dve.tensor_tensor_scan(carry[:, 0:LINES - 1][:, ::-1], k[:, 1:][:, ::-1], x[:, 1:][:, ::-1], lowest, op_keep, op_take))
                else:
                    m = mark("dve", dve.tensor_tensor_scan(carry[:, 1:LINES], k[:, 0:LINES - 1], x[:, 0:LINES - 1], lowest, op_keep, op_take))
                wait("pe", m)
                m = mark("pe", pe.matmul(bank[3][0:LINES, 0:1], carry[:, 0:LINES], ones[0:1, 0:1], start=True, stop=True))
                wait("dve", m)
                m = mark("dve", dve.tensor_copy(cols[0:LINES, 3:4], bank[3][0:LINES, 0:1]))
                wait("dve", m)

            wait("dve", m)
            m = mark("dve", dve.tensor_tensor_scan(fwd, keep, line, lowest, op_keep, op_take))
            carried(ROW_PREV if kind == "max" else ROW_SAME, fwd[:, LINE - 1:LINE], False, lowest, op_keep, op_take, m)
            m = mark("dve", dve.tensor_tensor_scan(fwd, keep, line, cols[0:LINES, 3:4], op_keep, op_take))
            wait("dve", m)
            m = mark("dve", dve.tensor_tensor_scan(back[:, ::-1], clamp_next[0:LINES, ::-1], fwd[:, ::-1], -BIG, ALU.min, ALU.max))
            carried(ROW_NEXT, back[:, 0:1], True, -BIG, ALU.min, ALU.max, m)
            m = mark("dve", dve.tensor_tensor_scan(back[:, ::-1], clamp_next[0:LINES, ::-1], fwd[:, ::-1], cols[0:LINES, 3:4], ALU.min, ALU.max))
            wait("pe", m)
            for j in range(8):
                m = mark("pe", pe.transpose(bank[4 + j // 4][:, (j % 4) * P:(j % 4) * P + LINES], back[:, j * P:(j + 1) * P], ident[0:LINES, 0:LINES]))
            r = result.rearrange("p (i j) -> p j i", j=8)
            wait("dve", m)
            for h in range(2):
                m = mark("dve", dve.tensor_copy(r[:, 4 * h:4 * h + 4, :], bank[4 + h][:, :].rearrange("p (j i) -> p j i", j=4)[:, :, 0:LINES]))
            wait("dve", m)
            free[:] = [None] * 8

        c_gather = [pr.count(f"gather{s}") for s in range(SLOTS)]
        c_idx = pr.count("idx_ready")
        c_issue = pr.count("pool_issue")
        c_rows = pr.count("rows_used")
        c_added = pr.count("added")
        c_onehot = pr.count("onehot_ready")
        c_z = pr.count("gate_in")
        c_gate = pr.count("gate_ready")
        c_bd = pr.count("dst_part")
        c_turned = pr.count("turned")
        c_kt = pr.count("kt_ready")
        c_scores = pr.count("scores")
        c_picked = pr.count("picked")
        c_kept = pr.count("kept")
        c_stored = [pr.count(f"stored{h}") for h in range(2)]
        c_loaded = [pr.count(f"loaded{q}") for q in range(QUADS)]
        c_ef = [pr.count(f"ef{h}") for h in range(2)]
        c_h1 = pr.count("h1_psum")
        c_h1s = pr.count("h1_ready")
        c_h2 = pr.count("h2_psum")
        c_h2s = pr.count("h2_ready")
        c_tp = pr.count("tp_psum")
        c_far = pr.count("distance")
        c_step = pr.count("msg_step")
        c_msg = pr.count("msg_ready")
        sp.sem_inc(c_rows.sem, QUADS)
        sp.sem_inc(c_added.sem, SLOTS)
        sp.sem_inc(c_turned.sem, QUADS)
        sp.sem_inc(c_scores.sem, QUADS)
        sp.sem_inc(c_kt.sem, QUADS)
        sp.sem_inc(c_picked.sem, QUADS)
        for h in range(2):
            sp.sem_inc(c_stored[h].sem, 16)
            c_stored[h].value = 16
        c_rows.value = c_turned.value = c_scores.value = c_kt.value = c_picked.value = QUADS
        c_added.value = SLOTS
        for c in (c_h1s, c_h2s, c_tp, c_h1, c_h2, c_msg):
            sp.sem_inc(c.sem, QUADS)
            c.value = QUADS

        def at(eng, c, turn, per_turn, n):
            eng.wait_ge(c.sem, turn * per_turn + (c.value + n))

        def quad(buf, q):
            return buf[:, q * QUAD:(q + 1) * QUAD]

        def load_idx_loop(c_free):
            act.copy(idx[:], src_idx[:, 0:SLOTS]).then_inc(c_idx.sem, QUADS)

            def quad_idx(i, q):
                at(act, c_free, i, QUADS, q + 1)
                act.copy(quad(idx, q), src_idx[:, bass.ds((i + 1) * SLOTS + q * QUAD, QUAD)]).then_inc(c_idx.sem, 1)
            return quad_idx

        def gather_loop(tab, width, stashed=False):
            with pool.Fori(0, TURNS) as i:
                for q in range(QUADS):
                    at(pool, c_idx, i, QUADS, q + 1)
                    if stashed:
                        at(pool, c_stored[q // 2], i, 16, 0)
                    pool.sem_inc(c_issue.sem, 1)
                    for s in range(q * QUAD, (q + 1) * QUAD):
                        pool.indirect_dma_start(G[:, s, 0:width], None, tab,
                                                bass.IndirectOffsetOnAxis(ap=idx[:, s:s + 1], axis=0)).then_inc(c_gather[s].sem, 16)

        def finish(counts):
            for c, n in counts:
                c.value += n
            free[:] = [None] * 8

        def windows_of(kind, i, q, n=QUAD):
            _, values = nc.values_load_multi_w_load_instructions(
                start[0:1, bass.ds(i * SLOTS + q * QUAD, n)], engines=(kind,), min_val=0, max_val=NODES - 1,
                skip_runtime_bounds_check_because="starts are dst values, clamped to the nodes")
            return values

        def make_onehot(i, q, weights, dynamic):
            at(dve, c_rows, i, QUADS, q + 1 - QUADS)
            for s in range(q * QUAD, (q + 1) * QUAD):
                w = weights[:, bass.ds(i * SLOTS + s, 1)] if dynamic else weights[:, s:s + 1]
                ins = dve.tensor_scalar(OH[:, s, :], ramp[:], place[:, bass.ds(i * SLOTS + s, 1)], w, ALU.is_equal, ALU.mult)
            ins.then_inc(c_onehot.sem, 1)

        def add_windows(i, q):
            windows = windows_of(DVE, i, q)
            at(dve, c_rows, i, QUADS, q + 1)
            for s in range(q * QUAD, (q + 1) * QUAD):
                w = aggT[:, bass.ds(windows[s % QUAD], P)]
                at(dve, c_added, i, SLOTS, s)
                dve.tensor_tensor(w, w, bank[q][:, (s % QUAD) * P:(s % QUAD + 1) * P], ALU.add).then_inc(c_added.sem, 1)

        def pe_sums(i, q, rows_ready, view):
            at(pe, c_onehot, i, QUADS, q + 1)
            at(pe, c_added, i, SLOTS, (q + 1) * QUAD - SLOTS)
            for s in range(q * QUAD, (q + 1) * QUAD):
                rows_ready(i, s)
                ins = pe.matmul(bank[q][:, (s % QUAD) * P:(s % QUAD + 1) * P], view[:, s, :], OH[:, s, :], start=True, stop=True)
            ins.then_inc(c_rows.sem, 1)

        def slot_landed(i, s):
            at(pe, c_gather[s], i, 16, 16)

        def aggregate(tab, weights):
            pr.barrier()
            view = G[:, :, 0:D] if tab is not None else G[:].rearrange("p s d -> p (s d)")[:, 0:SLOTS * D].rearrange("p (s d) -> p s d", d=D)
            with nc.Block() as block:
                if tab is not None:
                    @block.gpsimd
                    def _(_e):
                        gather_loop(tab, D)

                    @block.scalar
                    def _(_e):
                        quad_idx = load_idx_loop(c_rows)
                        with act.Fori(0, TURNS) as i:
                            for q in range(QUADS):
                                quad_idx(i, q)
                else:
                    @block.sync
                    def _(_e):
                        with sp.Fori(0, TURNS) as i:
                            for q in range(QUADS):
                                at(sp, c_rows, i, QUADS, q + 1 - QUADS)
                                part = q % 2 * QUAD * D
                                sp.dma_start(view[:, q * QUAD:(q + 1) * QUAD, :].rearrange("p s d -> p (s d)"),
                                             stash[bass.ds(i * 2 + q // 2, 1), :, part:part + QUAD * D].rearrange("a p d -> (a p) d")).then_inc(c_loaded[q].sem, 16)

                @block.tensor
                def _(_e):
                    def landed(i, s):
                        if tab is not None:
                            slot_landed(i, s)
                        elif s % QUAD == 0:
                            at(pe, c_loaded[s // QUAD], i, 16, 16)
                    with pe.Fori(0, TURNS) as i:
                        for q in range(QUADS):
                            pe_sums(i, q, landed, view)

                @block.vector
                def _(_e):
                    with dve.Fori(0, TURNS) as i:
                        for q in range(QUADS + 1):
                            if q < QUADS:
                                make_onehot(i, q, weights, True)
                            if q:
                                add_windows(i, q - 1)
            if tab is not None:
                finish([(c, 16 * TURNS) for c in c_gather] + [(c_idx, QUADS * (TURNS + 1))])
            else:
                finish([(c, 16 * TURNS) for c in c_loaded])
            finish([(c_rows, QUADS * TURNS), (c_onehot, QUADS * TURNS), (c_added, SLOTS * TURNS)])

        def aggregate_gated():
            dst_part, gate_in, gate = (per_slot[:, k, :] for k in range(3))
            pr.barrier()
            with nc.Block() as block:
                @block.gpsimd
                def _(_e):
                    gather_loop(table_gated, D + 1)

                @block.scalar
                def _(_e):
                    quad_idx = load_idx_loop(c_rows)
                    with act.Fori(0, TURNS) as i:
                        for q in range(QUADS + 1):
                            if q < QUADS:
                                at(act, c_z, i, QUADS, q + 1)
                                act.activation(quad(gate, q), quad(gate_in, q), ACT.Sigmoid).then_inc(c_gate.sem, 1)
                            if q:
                                quad_idx(i, q - 1)

                @block.tensor
                def _(_e):
                    with pe.Fori(0, TURNS) as i:
                        for q in range(QUADS):
                            pe_sums(i, q, slot_landed, G[:, :, 0:D])

                @block.vector
                def _(_e):
                    def gates(i, q):
                        windows = windows_of(DVE, i, q)
                        for s in range(q * QUAD, (q + 1) * QUAD):
                            w = qT[:, bass.ds(windows[s % QUAD], P)]
                            ins = dve.scalar_tensor_tensor(KT[:, s, :], ramp[:], place[:, bass.ds(i * SLOTS + s, 1)], w,
                                                           ALU.is_equal, ALU.mult, accum_out=dst_part[:, s:s + 1])
                        ins.then_inc(c_bd.sem, 1)
                        for s in range(q * QUAD, (q + 1) * QUAD):
                            at(dve, c_gather[s], i, 16, 16)
                        at(dve, c_bd, i, QUADS, q + 1)
                        dve.tensor_tensor(quad(gate_in, q), quad(dst_part, q), G[:, q * QUAD:(q + 1) * QUAD, D], ALU.add).then_inc(c_z.sem, 1)

                    def onehot(i, q):
                        at(dve, c_gate, i, QUADS, q + 1)
                        make_onehot(i, q, gate, False)

                    with dve.Fori(0, TURNS) as i:
                        for q in range(QUADS + 2):
                            if q < QUADS:
                                gates(i, q)
                            if 1 <= q <= QUADS:
                                onehot(i, q - 1)
                            if q >= 2:
                                add_windows(i, q - 2)
            finish([(c, 16 * TURNS) for c in c_gather] + [(c_idx, QUADS * (TURNS + 1))])
            finish([(c, QUADS * TURNS) for c in (c_rows, c_onehot, c_z, c_gate, c_bd)] + [(c_added, SLOTS * TURNS)])

        def scores_pass():
            pr.barrier()
            with nc.Block() as block:
                @block.gpsimd
                def _(_e):
                    gather_loop(table_kv, 2 * D, stashed=True)

                @block.sync
                def _(_e):
                    with sp.Fori(0, TURNS) as i:
                        for h in range(2):
                            at(sp, c_turned, i, QUADS, 2 * h + 2)
                            sp.dma_start(stash[bass.ds(i * 2 + h, 1)].rearrange("a p (s d) -> (a p) s d", d=D),
                                         G[:, h * HALF:(h + 1) * HALF, D:2 * D]).then_inc(c_stored[h].sem, 16)
                    for h in range(2):
                        sp.wait_ge(c_stored[h].sem, c_stored[h].value + 16 * TURNS)

                @block.scalar
                def _(_e):
                    quad_idx = load_idx_loop(c_turned)
                    with act.Fori(0, TURNS) as i:
                        for q in range(QUADS):
                            at(act, c_turned, i, QUADS, q + 1)
                            at(act, c_scores, i, QUADS, q + 1 - QUADS)
                            act.copy(quad(KT, q).rearrange("p s d -> p (s d)"), bank[q][:, :]).then_inc(c_kt.sem, 1)
                            quad_idx(i, q)

                @block.tensor
                def _(_e):
                    def turn(i, q):
                        at(pe, c_kt, i, QUADS, q + 1 - QUADS)
                        for s in range(q * QUAD, (q + 1) * QUAD):
                            slot_landed(i, s)
                            ins = pe.transpose(bank[q][:, (s % QUAD) * P:(s % QUAD + 1) * P], G[:, s, 0:D], ident[:])
                        ins.then_inc(c_turned.sem, 1)

                    def scores(i, q):
                        windows = windows_of(PE, i, q)
                        at(pe, c_kt, i, QUADS, q + 1)
                        at(pe, c_picked, i, QUADS, q + 1 - QUADS)
                        for s in range(q * QUAD, (q + 1) * QUAD):
                            w = qT[:, bass.ds(windows[s % QUAD], P)]
                            ins = pe.matmul(bank[4 + q][:, (s % QUAD) * P:(s % QUAD + 1) * P], KT[:, s, :], w, start=True, stop=True)
                        ins.then_inc(c_scores.sem, 1)

                    with pe.Fori(0, TURNS) as i:
                        for q in range(QUADS + 1):
                            if q < QUADS:
                                turn(i, q)
                            if q:
                                scores(i, q - 1)

                @block.vector
                def _(_e):
                    picked = per_slot[:, 0, :]
                    with dve.Fori(0, TURNS) as i:
                        for q in range(QUADS):
                            at(dve, c_scores, i, QUADS, q + 1)
                            for s in range(q * QUAD, (q + 1) * QUAD):
                                ins = dve.scalar_tensor_tensor(OH[:, s, :], ramp[:], place[:, bass.ds(i * SLOTS + s, 1)],
                                                               bank[4 + q][:, (s % QUAD) * P:(s % QUAD + 1) * P],
                                                               ALU.is_equal, ALU.mult, accum_out=picked[:, s:s + 1])
                            ins.then_inc(c_picked.sem, 1)
                        at(dve, c_picked, i, QUADS, QUADS)
                        dve.tensor_scalar(logit[:, bass.ds(i * SLOTS, SLOTS)], picked, float(D) ** -0.5, None, ALU.mult).then_inc(c_kept.sem, 1)
                        at(dve, c_kept, i, 1, 1)
            finish([(c, 16 * TURNS) for c in c_gather + c_stored] + [(c_idx, QUADS * (TURNS + 1)), (c_kept, TURNS)])
            finish([(c, QUADS * TURNS) for c in (c_turned, c_kt, c_scores, c_picked)])

        wm = wts[:, 0:D + 1]
        wrep = wts[:, 2 * D:3 * D]
        ws = load_weights([(wm[:, 0:D], a["W_msg"]), (wm[:, D:D + 1], a["W_att"][0:D, :]), (small[:, 0:1], a["W_att"][D:2 * D, :]),
                           (rowsW[0:1, 0:D], a["b_msg"]), (rowsW[0:1, D:D + 1], a["b_att"]),
                           (biasc[:, 0:3], a["b_ih"]), (biasc[:, 3:6], a["b_hh"]), (small[:, 1:3], a["bn"])])
        wait("dve", *ws, m_ones)
        m_rep = mark("dve", dve.tensor_scalar(wrep, ones[:], small[:, 0:1], None, ALU.mult))
        m_br = mark("dve", dve.tensor_tensor(small[:, 4:6], biasc[:, 0:2], biasc[:, 3:5], ALU.add))
        m_tail = mark("dve", dve.memset(qT[:, NP:NW], 0.0))
        m_xT = transpose_blocks(xT, xN, m_x + [m_ident])
        pr.barrier()
        zero_sums()
        nodes_T(qT, [(wrep, xT)], ACT.Identity, 0.0)
        make_table(table_gated, [(xT, wm)], D + 1, rowsW[0:1, 0:D + 1])
        aggregate_gated()

        w_ih, w_hh = wts[:, 0:3 * D], wts[:, 3 * D:6 * D]
        pr.barrier()
        ws = load_weights([(w_ih, a["W_ih"]), (w_hh, a["W_hh"])])
        wait("pe", *ws)
        gate_r, gate_z, mix = (spare[:, k * 2 * CHUNK:(k + 1) * 2 * CHUNK].rearrange("p (j c) -> p j c", j=2) for k in range(3))
        for c in range(14):
            j, k = c % 2, 4 * (c % 2)
            cut = slice(c * CHUNK, (c + 1) * CHUNK)
            r_p, z_p, in_p, hn_p = (bank[k + n][:, 0:CHUNK] for n in range(4))
            wait("pe", free[k], free[k + 3])
            for o, g, both in ((r_p, 0, True), (z_p, 1, True)):
                pe.matmul(o, w_ih[:, g * D:(g + 1) * D], aggT[:, cut], start=True, stop=False)
                pe.matmul(o, w_hh[:, g * D:(g + 1) * D], xT[:, cut], start=False, stop=True)
            pe.matmul(in_p, w_ih[:, 2 * D:3 * D], aggT[:, cut], start=True, stop=True)
            m = mark("pe", pe.matmul(hn_p, w_hh[:, 2 * D:3 * D], xT[:, cut], start=True, stop=True))
            wait("act", m)
            m_r = mark("act", act.activation(gate_r[:, j, :], r_p, ACT.Sigmoid, bias=small[:, 4:5]))
            m_z = mark("act", act.activation(gate_z[:, j, :], z_p, ACT.Sigmoid, bias=small[:, 5:6]))
            wait("dve", m_r)
            m = mark("dve", dve.scalar_tensor_tensor(mix[:, j, :], hn_p, biasc[:, 5:6], gate_r[:, j, :], ALU.add, ALU.mult))
            wait("dve", m)
            m = mark("dve", dve.tensor_tensor(mix[:, j, :], mix[:, j, :], in_p, ALU.add))
            wait("act", m)
            m = mark("act", act.activation(mix[:, j, :], mix[:, j, :], ACT.Tanh, bias=biasc[:, 2:3]))
            wait("dve", m, m_z)
            m = mark("dve", dve.tensor_tensor(gate_r[:, j, :], xT[:, cut], mix[:, j, :], ALU.subtract))
            wait("dve", m)
            m = mark("dve", dve.tensor_tensor(gate_r[:, j, :], gate_r[:, j, :], gate_z[:, j, :], ALU.mult))
            wait("dve", m)
            m = mark("dve", dve.tensor_tensor(hT[:, cut], gate_r[:, j, :], mix[:, j, :], ALU.add))
            free[k] = free[k + 3] = m
        wait("dve", m)
        BN = 250
        assert NODES % BN == 0 and NODES // BN <= BLOCKS
        for c in range(NODES // BN):
            m = mark("dve", dve.bn_stats(stats[:, c, :], hT[:, c * BN:(c + 1) * BN]))
        wait("dve", m)
        m = mark("dve", dve.bn_aggr(moments[:, 0, :], stats[:, 0:NODES // BN, :].rearrange("p c s -> p (c s)")))
        wait("dve", m)
        m = mark("dve", dve.tensor_scalar(small[:, 6:7], moments[:, 0, 1:2], EPS, None, ALU.add))
        wait("act", m)
        m = mark("act", act.activation(small[:, 6:7], small[:, 6:7], ACT.Sqrt))
        wait("dve", m)
        m = mark("dve", dve.reciprocal(small[:, 6:7], small[:, 6:7]))
        wait("dve", m)
        m = mark("dve", dve.tensor_scalar(small[:, 6:7], small[:, 6:7], small[:, 1:2], None, ALU.mult))
        wait("dve", m)
        m = mark("dve", dve.tensor_scalar(hT[:], hT[:], moments[:, 0, 0:1], small[:, 6:7], ALU.subtract, ALU.mult))
        m_b = dma("sp", rowsW[0:1, 0:D], a["beta"])
        wait("pe", m, m_b)
        nextN = qT[:, 0:NP].rearrange("p (b d) -> p b d", d=D)
        free[:] = [None] * 8
        m = layer_norm(nextN, [(xT, ident[:]), (hT, ident[:])], rowsW[0:1, 0:D])
        m_x = transpose_blocks(xT, nextN, [m])

        wq, wkv, wskip = wts[:, 0:D], wts[:, D:3 * D], wts[:, 3 * D:4 * D]
        for l in range(HEADS_L1):
            last = l == HEADS_L1 - 1
            pr.barrier()
            inT = xT if l == 0 else hT
            ws = load_weights([(wq, a["Wq"][l]), (wkv[:, 0:D], a["Wk"][l]), (wkv[:, D:2 * D], a["Wv"][l]), (wskip, a["Ws"][l]),
                               (biasc[:, 0:1], a["bq"][l]), (biasc[:, 1:2], a["bs_col"][l]),
                               (rowsW[0:1, 0:D], a["bk"][l:l + 1, :]), (rowsW[0:1, D:2 * D], a["bv"][l:l + 1, :])])
            wait("pe", *ws)
            wait("act", *ws)
            zero_sums()
            if l == 0:
                mark("dve", dve.memset(qT[:, NP:NW], 0.0))
            nodes_T(qT, [(wq, inT)], ACT.Identity, biasc[:, 0:1])
            make_table(table_kv, [(inT, wkv)], 2 * D, rowsW[0:1, 0:2 * D])
            scores_pass()
            segments(logit[:], weight[:], "max")
            m = mark("dve", dve.tensor_tensor(logit[:], logit[:], weight[:], ALU.subtract))
            wait("act", m)
            m = mark("act", act.activation(logit[:], logit[:], ACT.Exp))
            segments(logit[:], weight[:], "sum")
            m = mark("dve", dve.tensor_scalar(weight[:], weight[:], 1e-16, None, ALU.max))
            wait("dve", m)
            m = mark("dve", dve.reciprocal(weight[:], weight[:]))
            wait("dve", m)
            m = mark("dve", dve.tensor_tensor(weight[:], weight[:], logit[:], ALU.mult))
            wait("dve", m)
            aggregate(None, weight)
            pr.barrier()
            if not last:
                nodes_T(hT, [(ident[:], aggT), (wskip, inT)], ACT.Relu, biasc[:, 1:2])
        m_b = dma("sp", rowsW[0:1, 0:D], a["bs"][HEADS_L1 - 1:HEADS_L1, :])
        wait("pe", m_b)
        m = layer_norm(nextN, [(xT, ident[:]), (aggT, ident[:]), (hT, wskip)], rowsW[0:1, 0:D])
        wait("sp", m)
        dma("sp", table[0].rearrange("(b p) d -> p b d", p=P), nextN)
        transpose_blocks(xT, nextN, [m])

        mark("dve", dve.memset(logit[:], 1.0))
        segments(logit[:], weight[:], "sum")
        m = mark("dve", dve.tensor_scalar(weight[:], weight[:], 1.0, None, ALU.max))
        wait("dve", m)
        m = mark("dve", dve.reciprocal(weight[:], weight[:]))
        wait("dve", m)
        for l in range(3):
            inT = (xT, hT, qT)[l]
            outT = (hT, qT, None)[l]
            pr.barrier()
            wl, wr = wts[:, 0:D], wts[:, D:2 * D]
            ws = load_weights([(wl, a[f"W_l{l}"]), (wr, a[f"W_r{l}"]), (biasc[:, 0:1], a["b_sage_col"][l]), (rowsW[0:1, 0:D], a["b_sage"][l:l + 1, :])])
            zero_sums()
            aggregate(table[l % 2], weight)
            pr.barrier()
            if l < 2:
                make_table(table[(l + 1) % 2], [(aggT, wl), (inT, wr)], D, rowsW[0:1, 0:D], func=ACT.Relu)
                nodes_T(outT, [(wl, aggT), (wr, inT)], ACT.Relu, biasc[:, 0:1])
        nextN = hT[:].rearrange("p (b d) -> p b d", d=D)
        m = layer_norm(nextN, [(xT, ident[:]), (aggT, wl), (qT, wr)], rowsW[0:1, 0:D])
        transpose_blocks(xT, nextN, [m])
        pr.barrier()

        wup = wts[:, 0:D]
        wout = [wts[:, D:2 * D], wts[:, 2 * D:3 * D]]
        A3, A2, A1 = wts[:, 3 * D:4 * D], wts[:, 4 * D:5 * D], wts[0:2 * FEATS, 5 * D:6 * D]
        m = mark("dve", dve.memset(wts[:], 0.0))
        wait("sp", m)
        up = wup.rearrange("p (g w) -> p g w", g=4)
        parts = [(up[0:MUL, 0, :], a["W_up_s"])]
        for k in range(2):
            hid = slice(k * HID, (k + 1) * HID)
            parts += [(A1[k * FEATS:(k + 1) * FEATS, hid], a["A1"]), (A2[hid, hid], a["A2"]), (A3[hid, :], a["A3"]),
                      (biasc[hid, 0:1], a["b1"]), (biasc[hid, 1:2], a["b2"])]
        for i in range(3):
            parts.append((up[:, 1 + i, :], a["W_up_v"][i]))
        outv = [w[:, MUL:D].rearrange("p (w i) -> p i w", i=3) for w in wout]
        parts.append((wout[0][0:2 * MUL, 0:MUL], a["W_out_s"]))
        vec = sb("vec", [P, MUL])
        parts.append((vec[0:2 * MUL, :], a["W_out_v"]))
        parts.append((vec[2 * MUL:P, :], a["W_out_v"]))
        ws = load_weights(parts)
        wait("dve", *ws)
        scale_out = 0.1 * float(2 * MUL) ** -0.5
        m = mark("dve", dve.tensor_scalar(wout[0][0:2 * MUL, 0:MUL], wout[0][0:2 * MUL, 0:MUL], scale_out, None, ALU.mult))
        for w, axis_lo, axis_hi in ((outv[0], None, 0), (outv[1], 1, 2)):
            if axis_lo is not None:
                m = mark("dve", dve.tensor_scalar(w[0:2 * MUL, axis_lo, :], vec[0:2 * MUL, :], scale_out, None, ALU.mult))
            m = mark("dve", dve.tensor_scalar(w[2 * MUL:P, axis_hi, :], vec[2 * MUL:P, :], scale_out, None, ALU.mult))
        zero_sums(whole=True)
        pr.barrier()
        make_table(table[0], [(xT, wup)], D, None, scale=float(MUL) ** -0.5)
        pr.barrier()
        msg = qT[:, 0:SLOTS * 2 * D].rearrange("p (s m) -> p s m", m=2 * D)
        PAIR = 2 * QUAD * P // 2
        ef = hT[0:2 * FEATS, 0:2 * PAIR].rearrange("p (h e) -> p h e", h=2)
        H1, H2 = (hT[:, (2 + 2 * k) * PAIR:(4 + 2 * k) * PAIR].rearrange("p (h e) -> p h e", h=2) for k in range(2))
        tmp = KT[:].rearrange("p s d -> p (s d)")
        ea = qT[:, SLOTS * 2 * D:SLOTS * 2 * D + 2 * HALF * 4].rearrange("p (h s c) -> p h s c", h=2, c=4)
        c_ea = c_loaded[0:2]
        with nc.Block() as block:
            @block.gpsimd
            def _(_e):
                gather_loop(table[0], D)

            @block.sync
            def _(_e):
                def features(h, column):
                    sp.dma_start(ef[:, h, :], a["edge_feats"][:, bass.ds(column, PAIR)]).then_inc(c_ef[h].sem, 16)

                features(0, 0)
                with sp.Fori(0, TURNS) as i:
                    for h in range(2):
                        at(sp, c_msg, i, QUADS, 2 * h + 2 - QUADS)
                        sp.dma_start(ea[:, h, :, :].rearrange("p s c -> p (s c)"),
                                     a["edge_attrs"][:, bass.ds(i * SLOTS * 4 + h * HALF * 4, HALF * 4)]).then_inc(c_ea[h].sem, 16)
                        at(sp, c_h1, i, 2, h)
                        features(1 - h, (i * 2 + (h + 1)) * PAIR)

            @block.scalar
            def _(_e):
                quad_idx = load_idx_loop(c_rows)

                def layer1(i, h):
                    at(act, c_h1, i, 2, h + 1)
                    at(act, c_h2, i, 2, h - 1)
                    act.activation(H1[:, h, :], bank[0][:, :], ACT.Silu, bias=biasc[:, 0:1]).then_inc(c_h1s.sem, 1)

                def layer2(i, h):
                    at(act, c_h2, i, 2, h + 1)
                    at(act, c_tp, i, QUADS, 2 * h - 2)
                    act.activation(H2[:, h, :], bank[1][:, :], ACT.Silu, bias=biasc[:, 1:2]).then_inc(c_h2s.sem, 1)

                def onehot(i, q):
                    at(act, c_rows, i, QUADS, q + 1 - QUADS)
                    for s in range(q * QUAD, (q + 1) * QUAD):
                        ins = act.activation(OH[:, s, :], ramp[:], ACT.Abs, bias=place[:, bass.ds(i * SLOTS + s, 1)], scale=-1.0)
                    ins.then_inc(c_far.sem, 1)
                    at(act, c_far, i, QUADS, q + 1)
                    act.activation(quad(OH, q), quad(OH, q), ACT.Relu, bias=1.0, scale=-1.0).then_inc(c_onehot.sem, 1)

                with act.Fori(0, TURNS) as i:
                    layer1(i, 0)
                    onehot(i, 0)
                    layer2(i, 0)
                    layer1(i, 1)
                    onehot(i, 1)
                    layer2(i, 1)
                    onehot(i, 2)
                    quad_idx(i, 0)
                    onehot(i, 3)
                    for q in range(1, QUADS):
                        quad_idx(i, q)

            @block.tensor
            def _(_e):
                def product1(h):
                    pe.matmul(bank[0][:, :], A1, ef[:, h, :], start=True, stop=True).then_inc(c_h1.sem, 1)

                def product2(i, h):
                    at(pe, c_h1s, i, 2, h + 1)
                    at(pe, c_h2s, i, 2, h)
                    pe.matmul(bank[1][:, :], A2, H1[:, h, :], start=True, stop=True).then_inc(c_h2.sem, 1)

                def product3(i, q):
                    h, j = q // 2, q % 2
                    hid = slice(j * HID, (j + 1) * HID)
                    at(pe, c_h2s, i, 2, h + 1)
                    at(pe, c_msg, i, QUADS, q - 1)
                    for t in range(QUAD):
                        ins = pe.matmul(bank[2 + j][:, t * P:(t + 1) * P], H2[hid, h, t * P:(t + 1) * P], A3[hid, :], start=True, stop=True)
                    ins.then_inc(c_tp.sem, 1)

                def sum_up(i, q):
                    at(pe, c_msg, i, QUADS, q + 1)
                    at(pe, c_onehot, i, QUADS, q + 1)
                    at(pe, c_added, i, SLOTS, (q - 1) * QUAD)
                    for s in range(q * QUAD, (q + 1) * QUAD):
                        for part in range(2):
                            o = bank[4 + 2 * (q % 2) + (s % QUAD) // 2][:, ((s % 2) * 2 + part) * P:((s % 2) * 2 + part + 1) * P]
                            ins = pe.matmul(o, msg[:, s, part * D:(part + 1) * D], OH[:, s, :], start=True, stop=True)
                    ins.then_inc(c_rows.sem, 1)

                pe.wait_ge(c_ef[0].sem, c_ef[0].value + 16)
                product1(0)
                with pe.Fori(0, TURNS) as i:
                    product2(i, 0)
                    at(pe, c_ef[1], i, 16, 16)
                    product1(1)
                    product3(i, 0)
                    product3(i, 1)
                    product2(i, 1)
                    at(pe, c_ef[0], i, 16, 32)
                    product1(0)
                    sum_up(i, 0)
                    product3(i, 2)
                    sum_up(i, 1)
                    product3(i, 3)
                    sum_up(i, 2)
                    sum_up(i, 3)

            @block.vector
            def _(_e):
                def messages(i, q):
                    j, h = q % 2, q // 2
                    at(dve, c_rows, i, QUADS, q + 1 - QUADS)
                    for s in range(q * QUAD, (q + 1) * QUAD):
                        at(dve, c_gather[s], i, 16, 16)
                    if q % 2 == 0:
                        at(dve, c_ea[h], i, 16, 16)
                    at(dve, c_tp, i, QUADS, q + 1)
                    w = bank[2 + j][:, :].rearrange("p (s g u) -> p s g u", s=QUAD, g=4)
                    g = G[:, q * QUAD:(q + 1) * QUAD, 0:D].rearrange("p s (g u) -> p s g u", g=4)
                    y = ea[:, h, (q % 2) * QUAD:(q % 2 + 1) * QUAD, :]
                    mq = msg[:, q * QUAD:(q + 1) * QUAD, :]
                    ys = y[:, :, 0:1].to_broadcast([P, QUAD, MUL])
                    yv = y[:, :, 1:4].unsqueeze(3).to_broadcast([P, QUAD, 3, MUL])
                    n = QUAD * MUL
                    ss_w0, ss_w1, ys_w2, dot = (tmp[:, (8 * j + k) * n:(8 * j + k + 1) * n].rearrange("p (s u) -> p s u", u=MUL) for k in range(4))
                    prod = tmp[:, (8 * j + 4) * n:(8 * j + 7) * n].rearrange("p (s i u) -> p s i u", s=QUAD, i=3)
                    v1 = mq[:, :, 2 * MUL:].rearrange("p s (i k u) -> p s i k u", i=3, k=2)
                    dve.tensor_tensor(ss_w0, g[:, :, 0, :], w[:, :, 0, :], ALU.mult)
                    dve.tensor_tensor(ss_w1, g[:, :, 0, :], w[:, :, 1, :], ALU.mult)
                    dve.tensor_tensor(ys_w2, ys, w[:, :, 2, :], ALU.mult)
                    dve.tensor_tensor(prod, g[:, :, 1:4, :], yv, ALU.mult).then_inc(c_step.sem, 1)
                    at(dve, c_step, i, 3 * QUADS, 3 * q + 1)
                    dve.tensor_tensor(dot, prod[:, :, 0, :], prod[:, :, 1, :], ALU.add).then_inc(c_step.sem, 1)
                    dve.tensor_tensor(mq[:, :, 0:MUL], ss_w0, ys, ALU.mult)
                    at(dve, c_step, i, 3 * QUADS, 3 * q + 2)
                    dve.tensor_tensor(dot, dot, prod[:, :, 2, :], ALU.add).then_inc(c_step.sem, 1)
                    dve.tensor_tensor(v1[:, :, :, 0, :], ss_w1.unsqueeze(2).to_broadcast([P, QUAD, 3, MUL]), yv, ALU.mult)
                    dve.tensor_tensor(v1[:, :, :, 1, :], g[:, :, 1:4, :], ys_w2.unsqueeze(2).to_broadcast([P, QUAD, 3, MUL]), ALU.mult)
                    at(dve, c_step, i, 3 * QUADS, 3 * q + 3)
                    dve.scalar_tensor_tensor(mq[:, :, MUL:2 * MUL], dot, float(3.0 ** -0.5), w[:, :, 3, :], ALU.mult, ALU.mult).then_inc(c_msg.sem, 1)

                def add_pairs(i, q):
                    windows = windows_of(DVE, i, q)
                    at(dve, c_rows, i, QUADS, q + 1)
                    for s in range(q * QUAD, (q + 1) * QUAD):
                        w = sums[:, :, bass.ds(windows[s % QUAD], P)]
                        o = bank[4 + 2 * (q % 2) + (s % QUAD) // 2][:, (s % 2) * 2 * P:((s % 2) * 2 + 2) * P].rearrange("p (k n) -> p k n", k=2)
                        at(dve, c_added, i, SLOTS, s)
                        dve.tensor_tensor(w, w, o, ALU.add).then_inc(c_added.sem, 1)

                with dve.Fori(0, TURNS) as i:
                    for q in range(QUADS + 1):
                        if q < QUADS:
                            messages(i, q)
                        if q:
                            add_pairs(i, q - 1)
        finish([(c, 16 * TURNS) for c in c_gather + c_ef + c_ea] + [(c_idx, QUADS * (TURNS + 1)), (c_added, SLOTS * TURNS)])
        pr.barrier()
        nextN = hT[:].rearrange("p (b d) -> p b d", d=D)
        m = layer_norm(nextN, [(xT, ident[:]), (aggT, wout[0]), (spare, wout[1])], None)
        wait("sp", m)
        dma("sp", out.rearrange("(b p) d -> p b d", p=P), nextN)
        pr.all_dmas("sp")


def kernel(**inputs):
    import concourse.bacc as bacc
    from concourse.bass_utils import run_bass_kernel_spmd

    x = {k: np.asarray(v) for k, v in inputs.items()}

    def padded(v, rows, fill=0):
        return np.concatenate([v, np.full((rows - v.shape[0],) + v.shape[1:], fill, v.dtype)])

    def tiles(v):
        return np.swapaxes(v.reshape((TILES, P) + v.shape[1:]), 0, 1)

    src, dst = padded(x["src"], EP), padded(x["dst"], EP, NO_NODE)
    up_v = np.zeros((3, D, MUL), np.float32)
    for i in range(3):
        up_v[i, MUL + i::3, :] = x["L3_gnn_W_up_v"]
    arrays = {
        "x": padded(x["x"], NP),
        "src_tile": np.concatenate([tiles(src), np.zeros((P, SLOTS), src.dtype)], axis=1),
        "dst_tile": tiles(dst),
        "dst_first": dst[::P],
        "dst_line": np.concatenate([np.full(1, -1, dst.dtype), dst, np.full(1, 2 * NO_NODE, dst.dtype)]),
        "edge_attrs": tiles(padded(x["edge_attr_4"], EP)).reshape(P, TILES * 4),
        "edge_feats": padded(padded(x["edge_attr_8"], EP).reshape(2 * TURNS, 2, QUAD * P, FEATS), 2 * TURNS + 1)
        .transpose(1, 3, 0, 2).reshape(2 * FEATS, (2 * TURNS + 1) * QUAD * P),
        "W_msg": x["L0_gnn_W_msg"], "W_att": x["L0_gnn_W_att"],
        "b_msg": x["L0_gnn_b_msg"].reshape(1, D), "b_att": x["L0_gnn_b_att"].reshape(1, 1),
        "W_ih": x["L0_gnn_W_ih"].T, "W_hh": x["L0_gnn_W_hh"].T,
        "b_ih": x["L0_gnn_b_ih"].reshape(3, D).T, "b_hh": x["L0_gnn_b_hh"].reshape(3, D).T,
        "bn": np.stack([x["L0_gnn_gamma"], x["L0_gnn_beta"]], axis=1), "beta": x["L0_gnn_beta"].reshape(1, D),
        "Wq": x["L1_gnn_Wq"], "Wk": x["L1_gnn_Wk"], "Wv": x["L1_gnn_Wv"], "Ws": x["L1_gnn_Ws"],
        "bq": x["L1_gnn_bq"].reshape(HEADS_L1, D, 1), "bk": x["L1_gnn_bk"], "bv": x["L1_gnn_bv"], "bs": x["L1_gnn_bs"], "bs_col": x["L1_gnn_bs"].reshape(HEADS_L1, D, 1),
        "b_sage": np.stack([x[f"L2_gnn_b{l}"] for l in range(3)]),
        "b_sage_col": np.stack([x[f"L2_gnn_b{l}"] for l in range(3)]).reshape(3, D, 1),
        "W_up_s": x["L3_gnn_W_up_s"], "W_up_v": up_v,
        "A1": x["L3_gnn_A1"], "A2": x["L3_gnn_A2"], "A3": x["L3_gnn_A3"],
        "b1": x["L3_gnn_b1"].reshape(HID, 1), "b2": x["L3_gnn_b2"].reshape(HID, 1),
        "W_out_s": x["L3_gnn_W_out_s"], "W_out_v": x["L3_gnn_W_out_v"],
    }
    for l in range(3):
        arrays[f"W_l{l}"], arrays[f"W_r{l}"] = x[f"L2_gnn_W_l{l}"], x[f"L2_gnn_W_r{l}"]
    arrays = {f"in_{k}": np.ascontiguousarray(v) for k, v in arrays.items()}

    nc = bacc.Bacc("TRN2", target_bir_lowering=False, num_devices=1)
    drams = {k[3:]: nc.dram_tensor(k, v.shape, mybir.dt.from_np(v.dtype), kind="ExternalInput").ap() for k, v in arrays.items()}
    out = nc.dram_tensor("out", (NP, D), F32, kind="ExternalOutput").ap()
    build_program(nc, drams, out)
    result = run_bass_kernel_spmd(nc, [arrays], core_ids=[0])
    return result.results[0]["out"][:NODES]
```

```python
from contextlib import ExitStack

import numpy as np

import concourse.bass as bass
from concourse import mybir

F32 = mybir.dt.float32
I32 = mybir.dt.int32
ALU = mybir.AluOpType
ACT = mybir.ActivationFunctionType
AX = mybir.AxisListType

DVE, PE = mybir.EngineType.DVE, mybir.EngineType.PE
P = 128
NODES = 6250
EDGES = 106250
D = 128
BLOCKS = -(-NODES // P)
NP = BLOCKS * P
NW = NP + P
SLOTS = 16
QUAD = 4
QUADS = SLOTS // QUAD
HALF = SLOTS // 2
TURNS = -(-EDGES // (P * SLOTS))
TILES = TURNS * SLOTS
EP = TILES * P
LINES = EP // (8 * P)
LINE = EP // LINES
PIECE_TURNS = 4
PIECES = TURNS // PIECE_TURNS
PT = PIECE_TURNS * SLOTS
LAG = PIECE_TURNS + 3
CHUNK = NP // 14
HEADS_L1 = 3
MUL = 32
HID = 64
FEATS = 8
NO_NODE = 1 << 20
EPS = 1e-5
BIG = 1e38

assert CHUNK * 14 == NP and CHUNK <= 512 and LINE == 8 * P and LINES <= P and TILES % 8 == 0
assert PIECES * PIECE_TURNS == TURNS and PT <= P and PIECES <= 14


class Count:

    def __init__(self, sem, value=0):
        self.sem, self.value = sem, value


class Program:
    def __init__(self, nc, ctx):
        self.nc, self.ctx = nc, ctx
        self.engines = {"pe": nc.tensor, "act": nc.scalar, "dve": nc.vector, "pool": nc.gpsimd, "sp": nc.sync}
        self.done = {k: self.count(f"done_{k}") for k in self.engines}
        self.lanes = [self.count(f"lane{i}") for i in range(8)]
        self.lane_at = 0

    def sbuf(self, name, shape, dt=F32):
        return self.ctx.enter_context(self.nc.sbuf_tensor(name, shape, dt))

    def count(self, name):
        return Count(self.ctx.enter_context(self.nc.semaphore(name)))

    def wait(self, engine, *marks):
        for m in marks:
            if m is not None:
                self.engines[engine].wait_ge(m[0].sem, m[1])

    def mark(self, engine, instruction):
        c = self.done[engine]
        c.value += 1
        instruction.then_inc(c.sem, 1)
        return c, c.value

    def dma(self, engine, out, in_):
        lane = self.lanes[self.lane_at % len(self.lanes)]
        self.lane_at += 1
        if lane.value:
            self.engines[engine].wait_ge(lane.sem, lane.value)
        lane.value += 16
        self.engines[engine].dma_start(out, in_).then_inc(lane.sem, 16)
        return lane, lane.value

    def all_dmas(self, engine):
        for lane in self.lanes:
            if lane.value:
                self.engines[engine].wait_ge(lane.sem, lane.value)

    def barrier(self):
        self.all_dmas("sp")
        self.nc.all_engine_barrier()


def build_program(nc, a, out):
    with ExitStack() as ctx:
        pr = Program(nc, ctx)
        sb, wait, mark, dma = pr.sbuf, pr.wait, pr.mark, pr.dma
        pe, act, dve, pool, sp = nc.tensor, nc.scalar, nc.vector, nc.gpsimd, nc.sync
        bank = [ctx.enter_context(nc.psum_tensor(f"bank{i}", [P, 512], F32)) for i in range(8)]

        def dram(name, shape):
            return nc.dram_tensor(name, shape, F32, kind="Internal").ap()

        table_gated = dram("table_gated", (NP, D + 1))
        table_kv = dram("table_kv", (NP, 2 * D))
        table = [dram(f"table_h{i}", (NP, D)) for i in range(2)]
        stash = dram("stash", (2 * TURNS, P, HALF * D))

        ident = sb("ident", [P, P])
        ramp = sb("ramp", [P, P])
        ones = sb("ones", [P, P])
        src_idx = sb("src_idx", [P, TILES + SLOTS], I32)
        start = sb("start", [P, TILES], I32)
        place = sb("place", [P, TILES])
        same_prev = sb("same_prev", [PT, PIECES * P])
        same_next = sb("same_next", [PT, PIECES * P])
        rows = sb("rows", [1, 6, P])
        cols = sb("cols", [P, 8])
        xT = sb("xT", [P, NP])
        hT = sb("hT", [P, NP])
        qT = sb("qT", [P, NW])
        sums = sb("sums", [P, 2, NW])
        aggT = sums[:, 0, :]
        spare = sums[:, 1, :]
        inv_degree = sb("inv_degree", [P, TILES])
        weight = sb("weight", [P, TILES])
        wts = sb("wts", [P, 6 * D])
        rowsW = sb("rowsW", [1, 2 * D])
        biasc = sb("biasc", [P, 8])
        small = sb("small", [P, 16])

        G = sb("G", [P, SLOTS, 2 * D])
        OH = sb("OH", [P, SLOTS, P])
        KT = sb("KT", [P, SLOTS, P])
        idx = sb("idx", [P, SLOTS], I32)
        per_slot = sb("per_slot", [P, 3, SLOTS])
        stats = sb("stats", [P, BLOCKS, 6])
        moments = sb("moments", [P, BLOCKS, 2])

        m_in = [dma("sp", src_idx[:], a["src_tile"]), dma("sp", start[:], a["dst_first"].rearrange("(a t) -> a t", a=1).to_broadcast([P, TILES]))]
        dst_i = inv_degree[:].bitcast(I32)
        m_dst = dma("sp", dst_i, a["dst_tile"])
        lines = [spare[0:LINES, k * LINE:(k + 1) * LINE].bitcast(I32) for k in range(3)]
        m_lines = [dma("sp", lines[k], a["dst_line"][k:k + EP].rearrange("(i r) -> i r", i=LINES)) for k in range(3)]
        m_x = []
        xN = hT[:].rearrange("p (b d) -> p b d", d=D)
        for b0 in range(0, BLOCKS, 7):
            m_x.append(dma("act", xN[:, b0:b0 + 7, :], a["x"].rearrange("(b p) d -> p b d", p=P)[:, b0:b0 + 7, :]))
        m_ramp = mark("pool", pool.iota(ramp[:], [[1, P]], base=0, channel_multiplier=0, allow_small_or_imprecise_dtypes=True))
        m = mark("pool", pool.memset(ident[:], 0.0))
        wait("pool", m)
        m_ident = mark("pool", pool.affine_select(out=ident[:], in_=ident[:], compare_op=ALU.not_equal, fill=1.0, base=0, pattern=[[-1, P]], channel_multiplier=1))
        m_ones = mark("dve", dve.memset(ones[:], 1.0))
        wait("dve", *m_in, m_dst)
        m1 = mark("dve", dve.tensor_scalar(start[:], start[:], float(NODES - 1), None, ALU.min))
        m2 = mark("dve", dve.tensor_copy(weight[:], dst_i))
        wait("dve", m1, m2)
        m3 = mark("dve", dve.tensor_tensor(place[:], weight[:], start[:], ALU.subtract))
        wait("dve", *m_lines)
        before, here, after = lines
        eq_next = spare[0:LINES, 3 * LINE:4 * LINE]
        line_same, line_next, fwd, back = (qT[0:LINES, k * LINE:(k + 1) * LINE] for k in range(4))
        m4 = mark("dve", dve.tensor_tensor(line_same, here, before, ALU.is_equal))
        m5 = mark("dve", dve.tensor_tensor(eq_next, here, after, ALU.is_equal))
        wait("dve", m4, m5)
        m6 = mark("dve", dve.tensor_scalar(line_next, eq_next, 2 * BIG, -BIG, ALU.mult, ALU.add))
        wait("dve", m6)
        dve.tensor_reduce(cols[0:LINES, 0:1], line_same, AX.X, ALU.min)
        m7 = mark("dve", dve.tensor_reduce(cols[0:LINES, 1:2], line_next, AX.X, ALU.min))
        wait("pe", m7, m_ident)
        for k in range(2):
            m8 = mark("pe", pe.matmul(bank[0][0:1, k * P:k * P + LINES], cols[0:LINES, k:k + 1], ident[0:LINES, 0:LINES], start=True, stop=True))
        wait("dve", m8)
        for k in range(2):
            m9 = mark("dve", dve.tensor_copy(rows[0:1, k, 0:LINES], bank[0][0:1, k * P:k * P + LINES]))
        ROW_SAME, ROW_NEXT, ROW_END, ROW_CARRY = range(4)

        def carried(row_keep, end, reverse, lowest, op_keep, op_take, m_end):
            wait("pe", m_end)
            m = mark("pe", pe.matmul(bank[2][0:1, 0:LINES], end, ident[0:LINES, 0:LINES], start=True, stop=True))
            wait("dve", m)
            m = mark("dve", dve.tensor_copy(rows[0:1, ROW_END, 0:LINES], bank[2][0:1, 0:LINES]))
            carry = rows[0:1, ROW_CARRY, :]
            m0 = mark("dve", dve.memset(carry, lowest))
            wait("dve", m, m0)
            k, x = rows[0:1, row_keep, 0:LINES], rows[0:1, ROW_END, 0:LINES]
            if reverse:
                m = mark("dve", dve.tensor_tensor_scan(carry[:, 0:LINES - 1][:, ::-1], k[:, 1:][:, ::-1], x[:, 1:][:, ::-1], lowest, op_keep, op_take))
            else:
                m = mark("dve", dve.tensor_tensor_scan(carry[:, 1:LINES], k[:, 0:LINES - 1], x[:, 0:LINES - 1], lowest, op_keep, op_take))
            wait("pe", m)
            m = mark("pe", pe.matmul(bank[3][0:LINES, 0:1], carry[:, 0:LINES], ones[0:1, 0:1], start=True, stop=True))
            wait("dve", m)
            m = mark("dve", dve.tensor_copy(cols[0:LINES, 3:4], bank[3][0:LINES, 0:1]))
            wait("dve", m)

        each = spare[0:LINES, 0:LINE]
        m = mark("dve", dve.memset(each, 1.0))
        wait("dve", m, m9)
        m = mark("dve", dve.tensor_tensor_scan(fwd, line_same, each, 0.0, ALU.mult, ALU.add))
        carried(ROW_SAME, fwd[:, LINE - 1:LINE], False, 0.0, ALU.mult, ALU.add, m)
        m = mark("dve", dve.tensor_tensor_scan(fwd, line_same, each, cols[0:LINES, 3:4], ALU.mult, ALU.add))
        wait("dve", m)
        m = mark("dve", dve.tensor_tensor_scan(back[:, ::-1], line_next[:, ::-1], fwd[:, ::-1], -BIG, ALU.min, ALU.max))
        carried(ROW_NEXT, back[:, 0:1], True, -BIG, ALU.min, ALU.max, m)
        m = mark("dve", dve.tensor_tensor_scan(back[:, ::-1], line_next[:, ::-1], fwd[:, ::-1], cols[0:LINES, 3:4], ALU.min, ALU.max))
        wait("pe", m)
        for j in range(8):
            m = mark("pe", pe.transpose(bank[4 + j // 4][:, (j % 4) * P:(j % 4) * P + LINES], back[:, j * P:(j + 1) * P], ident[0:LINES, 0:LINES]))
        degree = inv_degree[:].rearrange("p (i j) -> p j i", j=8)
        wait("dve", m)
        for h in range(2):
            m = mark("dve", dve.tensor_scalar(degree[:, 4 * h:4 * h + 4, :], bank[4 + h][:, :].rearrange("p (j i) -> p j i", j=4)[:, :, 0:LINES], 1.0, None, ALU.max))
        wait("dve", m)
        m_degree = mark("dve", dve.reciprocal(inv_degree[:], inv_degree[:]))

        free = [None] * 8
        free[0] = free[2] = free[3] = free[4] = free[5] = m_degree

        def transpose_blocks(dstT, srcN, ready):
            last = None
            for g, b0 in enumerate(range(0, BLOCKS, QUAD)):
                nb = min(QUAD, BLOCKS - b0)
                k = g % 8
                wait("pe", free[k], *ready)
                for j in range(nb):
                    m = pe.transpose(bank[k][:, j * P:(j + 1) * P], srcN[:, b0 + j, :], ident[:])
                m = mark("pe", m)
                who, e = (("act", act), ("dve", dve))[g % 2]
                wait(who, m)
                free[k] = last = mark(who, (e.copy if who == "act" else e.tensor_copy)(dstT[:, b0 * P:(b0 + nb) * P], bank[k][:, 0:nb * P]))
            return last

        def nodes_T(dstT, terms, func, bias):
            for c in range(14):
                k = c % 8
                cut = slice(c * CHUNK, (c + 1) * CHUNK)
                wait("pe", free[k])
                for n, (w, nodesT) in enumerate(terms):
                    m = pe.matmul(bank[k][:, 0:CHUNK], w, nodesT[:, cut], start=n == 0, stop=n == len(terms) - 1)
                m = mark("pe", m)
                wait("act", m)
                free[k] = mark("act", act.activation(dstT[:, cut], bank[k][:, 0:CHUNK], func, bias=bias))

        def nodes_N(block_done, terms, width, bias_row):
            for b in range(BLOCKS):
                k = b % 8
                wait("pe", free[k])
                if bias_row is not None:
                    pe.matmul(bank[k][:, 0:width], ones[0:1, :], bias_row, start=True, stop=False)
                for n, (nodesT, w) in enumerate(terms):
                    m = pe.matmul(bank[k][:, 0:width], nodesT[:, b * P:(b + 1) * P], w, start=n == 0 and bias_row is None, stop=n == len(terms) - 1)
                free[k] = block_done(b, k, mark("pe", m))

        stage_at = [0]
        stage_free = [None] * 8

        def make_table(dst, terms, width, bias_row, func=ACT.Copy, scale=1.0):
            stage = G[:, 0:SLOTS // 2, :] if width > D + 1 else G[:, 0:SLOTS // 2, :]

            def done(b, k, m):
                s = stage_at[0] % 8
                stage_at[0] += 1
                wait("act", m, stage_free[s])
                r = mark("act", act.activation(stage[:, s, 0:width], bank[k][:, 0:width], func, scale=scale))
                wait("sp", r)
                stage_free[s] = dma("sp", dst[b * P:(b + 1) * P, :], stage[:, s, 0:width])
                return r
            nodes_N(done, terms, width, bias_row)

        def layer_norm(dstN, terms, bias_row):
            def done(b, k, m):
                wait("dve", m)
                s = mark("dve", dve.bn_stats(stats[:, b, :], bank[k][:, 0:D]))
                wait("act", s)
                return mark("act", act.copy(dstN[:, b, :], bank[k][:, 0:D]))
            nodes_N(done, terms, D, bias_row)
            wait("dve", (pr.done["dve"], pr.done["dve"].value), (pr.done["act"], pr.done["act"].value))
            for b in range(BLOCKS):
                m = mark("dve", dve.bn_aggr(moments[:, b, :], stats[:, b, :]))
            wait("dve", m)
            var = moments[:, :, 1]
            m = mark("dve", dve.tensor_scalar(var, var, EPS, None, ALU.add))
            wait("act", m)
            m = mark("act", act.activation(var, var, ACT.Sqrt))
            wait("dve", m)
            m = mark("dve", dve.reciprocal(var, var))
            wait("dve", m)
            for b in range(BLOCKS):
                m = mark("dve", dve.tensor_scalar(dstN[:, b, :], dstN[:, b, :], moments[:, b, 0:1], moments[:, b, 1:2], ALU.subtract, ALU.mult))
            return m

        def load_weights(parts):
            return [dma("sp", o, i) for o, i in parts]

        def zero_sums(whole=False):
            return mark("pool", pool.memset(sums[:, :, :] if whole else aggT, 0.0))

        v_rows = spare[:, 0:SLOTS * D].rearrange("p (s d) -> p s d", d=D)
        scratch = spare[:, SLOTS * D:(SLOTS + QUAD) * D].rearrange("p (s d) -> p s d", d=D)
        SOFTMAX_AT = (SLOTS + QUAD) * D
        fwd, back, expo, clamp_prev, clamp_next = (spare[:, SOFTMAX_AT + k * P:SOFTMAX_AT + (k + 1) * P] for k in range(5))
        picked = spare[:, SOFTMAX_AT + 5 * P:SOFTMAX_AT + 6 * P]
        row_at = SOFTMAX_AT + 6 * P
        same_row, clamp_row, clamp_next_row = (spare[0:1, row_at + k * TILES:row_at + (k + 1) * TILES] for k in range(3))
        max_row, behind_row, sum_row, whole_row, carry, next_row = (rows[0:1, k, :] for k in range(6))
        rescale = cols[:, 7:8]

        c_gather = [pr.count(f"gather{s}") for s in range(SLOTS)]
        c_idx = pr.count("idx_ready")
        c_issue = pr.count("pool_issue")
        c_sp_issue = pr.count("sp_issue")
        c_rows = pr.count("rows_used")
        c_added = pr.count("added")
        c_onehot = pr.count("onehot_ready")
        c_z = pr.count("gate_in")
        c_gate = pr.count("gate_ready")
        c_bd = pr.count("dst_part")
        c_turned = pr.count("turned")
        c_kt = pr.count("kt_ready")
        c_scores = pr.count("scores")
        c_picked = pr.count("picked")
        c_stored = [pr.count(f"stored{h}") for h in range(2)]
        c_loaded = [pr.count(f"loaded{q}") for q in range(QUADS)]
        c_link = pr.count("softmax_link")
        c_hop = pr.count("softmax_hop")
        c_exp = pr.count("softmax_exp")
        c_ef = [pr.count(f"ef{h}") for h in range(2)]
        c_h1 = pr.count("h1_psum")
        c_h1s = pr.count("h1_ready")
        c_h2 = pr.count("h2_psum")
        c_h2s = pr.count("h2_ready")
        c_tp = pr.count("tp_psum")
        c_far = pr.count("distance")
        c_step = pr.count("msg_step")
        c_msg = pr.count("msg_ready")
        sp.sem_inc(c_rows.sem, QUADS)
        sp.sem_inc(c_added.sem, SLOTS)
        sp.sem_inc(c_turned.sem, QUADS)
        sp.sem_inc(c_scores.sem, QUADS)
        sp.sem_inc(c_kt.sem, QUADS)
        sp.sem_inc(c_picked.sem, QUADS)
        for h in range(2):
            sp.sem_inc(c_stored[h].sem, 16)
            c_stored[h].value = 16
        c_rows.value = c_turned.value = c_scores.value = c_kt.value = c_picked.value = QUADS
        c_added.value = SLOTS
        for c in (c_h1s, c_h2s, c_tp, c_h1, c_h2, c_msg):
            sp.sem_inc(c.sem, QUADS)
            c.value = QUADS

        def at(eng, c, turn, per_turn, n):
            eng.wait_ge(c.sem, turn * per_turn + (c.value + n))

        def quad(buf, q):
            return buf[:, q * QUAD:(q + 1) * QUAD]

        def load_idx_loop(c_free):
            act.copy(idx[:], src_idx[:, 0:SLOTS]).then_inc(c_idx.sem, QUADS)

            def quad_idx(i, q):
                at(act, c_free, i, QUADS, q + 1)
                act.copy(quad(idx, q), src_idx[:, bass.ds((i + 1) * SLOTS + q * QUAD, QUAD)]).then_inc(c_idx.sem, 1)
            return quad_idx

        def gather_loop(tab, width, stashed=False):
            with pool.Fori(0, TURNS) as i:
                for q in range(QUADS):
                    at(pool, c_idx, i, QUADS, q + 1)
                    if stashed:
                        at(pool, c_stored[q // 2], i, 16, 0)
                    pool.sem_inc(c_issue.sem, 1)
                    for s in range(q * QUAD, (q + 1) * QUAD):
                        pool.indirect_dma_start(G[:, s, 0:width], None, tab,
                                                bass.IndirectOffsetOnAxis(ap=idx[:, s:s + 1], axis=0)).then_inc(c_gather[s].sem, 16)

        def finish(counts):
            for c, n in counts:
                c.value += n
            free[:] = [None] * 8

        def windows_of(kind, i, q, n=QUAD):
            _, values = nc.values_load_multi_w_load_instructions(
                start[0:1, bass.ds(i * SLOTS + q * QUAD, n)], engines=(kind,), min_val=0, max_val=NODES - 1,
                skip_runtime_bounds_check_because="starts are dst values, clamped to the nodes")
            return values

        def turns(engine, body):
            with engine.Fori(0, TURNS - 1) as i:
                body(i, False)
            body(TURNS - 1, True)

        def slots_of(q):
            return [q % QUADS * QUAD + k for k in range(QUAD)]

        def onehot_and_add(i, q_onehot, weights, q_add, c_weights=None, banks=range(4)):
            windows = windows_of(DVE, i, q_add) if q_add is not None else None
            for k in range(QUAD):
                if q_onehot is not None:
                    s = slots_of(q_onehot)[k]
                    tile = bass.ds(i * SLOTS + (q_onehot * QUAD + k), 1)
                    if k == 0:
                        if c_weights is not None:
                            at(dve, c_weights, i, QUADS, q_onehot + 1)
                        at(dve, c_rows, i, QUADS, q_onehot + 1 - QUADS)
                    w = weights[:, tile] if weights.shape[1] == TILES else weights[:, s:s + 1]
                    ins = dve.tensor_scalar(OH[:, s, :], ramp[:], place[:, tile], w, ALU.is_equal, ALU.mult)
                    if k == QUAD - 1:
                        ins.then_inc(c_onehot.sem, 1)
                if q_add is not None:
                    if k == 0:
                        at(dve, c_rows, i, QUADS, q_add + 1)
                    w = aggT[:, bass.ds(windows[k], P)]
                    at(dve, c_added, i, SLOTS, q_add * QUAD + k)
                    dve.tensor_tensor(w, w, bank[banks[q_add % len(banks)]][:, k * P:(k + 1) * P], ALU.add).then_inc(c_added.sem, 1)

        def pe_sums(i, q, rows_ready, view, banks=range(4)):
            at(pe, c_onehot, i, QUADS, q + 1)
            at(pe, c_added, i, SLOTS, (q + 1 - len(banks)) * QUAD)
            for s in range(q * QUAD, (q + 1) * QUAD):
                rows_ready(i, s)
                ins = pe.matmul(bank[banks[q % len(banks)]][:, (s % QUAD) * P:(s % QUAD + 1) * P], view[:, s, :], OH[:, s, :], start=True, stop=True)
            ins.then_inc(c_rows.sem, 1)

        def slot_landed(i, s):
            at(pe, c_gather[s], i, 16, 16)

        def quad_loaded(i, s):
            if s % QUAD == 0:
                at(pe, c_loaded[s // QUAD], i, 16, 16)

        def aggregate(tab, weights):
            pr.barrier()
            with nc.Block() as block:
                @block.gpsimd
                def _(_e):
                    gather_loop(tab, D)

                @block.scalar
                def _(_e):
                    quad_idx = load_idx_loop(c_rows)
                    with act.Fori(0, TURNS) as i:
                        for q in range(QUADS):
                            quad_idx(i, q)

                @block.tensor
                def _(_e):
                    with pe.Fori(0, TURNS) as i:
                        for q in range(QUADS):
                            pe_sums(i, q, slot_landed, G[:, :, 0:D])

                @block.vector
                def _(_e):
                    for q in range(2):
                        onehot_and_add(0, q, weights, None)

                    def turn(i, last):
                        for q in range(QUADS):
                            onehot_and_add(i, None if last and q + 2 >= QUADS else q + 2, weights, q)
                    turns(dve, turn)
            finish([(c, 16 * TURNS) for c in c_gather] + [(c_idx, QUADS * (TURNS + 1))])
            finish([(c_rows, QUADS * TURNS), (c_onehot, QUADS * TURNS), (c_added, SLOTS * TURNS)])

        def aggregate_gated():
            dst_part, gate_in, gate = (per_slot[:, k, :] for k in range(3))
            pr.barrier()
            with nc.Block() as block:
                @block.gpsimd
                def _(_e):
                    gather_loop(table_gated, D + 1)

                @block.scalar
                def _(_e):
                    quad_idx = load_idx_loop(c_rows)
                    act.activation(small[:, 3:4], ones[:, 0:1], ACT.Sigmoid)

                    def sigmoid(i, q):
                        at(act, c_z, i, QUADS, q + 1)
                        act.activation(quad(gate, q % QUADS), quad(gate_in, q % QUADS), ACT.Sigmoid).then_inc(c_gate.sem, 1)

                    sigmoid(0, 0)
                    sigmoid(0, 1)

                    def turn(i, last):
                        for q in range(QUADS):
                            if not last or q + 2 < QUADS:
                                sigmoid(i, q + 2)
                            quad_idx(i, q)
                    turns(act, turn)

                @block.tensor
                def _(_e):
                    with pe.Fori(0, TURNS) as i:
                        for q in range(QUADS):
                            pe_sums(i, q, slot_landed, G[:, :, 0:D])

                @block.vector
                def _(_e):
                    def dst_parts(i, q):
                        windows = windows_of(DVE, i, q)
                        for k, s in enumerate(slots_of(q)):
                            ins = dve.scalar_tensor_tensor(KT[:, s, :], ramp[:], place[:, bass.ds(i * SLOTS + (q * QUAD + k), 1)],
                                                           qT[:, bass.ds(windows[k], P)],
                                                           ALU.is_equal, ALU.mult, accum_out=dst_part[:, s:s + 1])
                        ins.then_inc(c_bd.sem, 1)

                    def gate_inputs(i, q):
                        for s in slots_of(q):
                            at(dve, c_gather[s], i, 16, 16 * (1 + q // QUADS))
                        at(dve, c_bd, i, QUADS, q + 1)
                        a, b = slots_of(q)[0], slots_of(q)[-1] + 1
                        dve.tensor_tensor(gate_in[:, a:b], dst_part[:, a:b], G[:, a:b, D], ALU.add).then_inc(c_z.sem, 1)

                    for q in range(2):
                        dst_parts(0, q)
                        gate_inputs(0, q)
                    onehot_and_add(0, 0, gate, None, c_gate)

                    def turn(i, last):
                        for q in range(QUADS):
                            ahead = not last or q + 2 < QUADS
                            if ahead:
                                dst_parts(i, q + 2)
                            onehot_and_add(i, q + 1 if not last or q + 1 < QUADS else None, gate, q, c_gate)
                            if ahead:
                                gate_inputs(i, q + 2)
                    turns(dve, turn)
            finish([(c, 16 * TURNS) for c in c_gather] + [(c_idx, QUADS * (TURNS + 1))])
            finish([(c, QUADS * TURNS) for c in (c_rows, c_onehot, c_z, c_gate, c_bd)] + [(c_added, SLOTS * TURNS)])

        def prepare_softmax():
            pr.barrier()
            temp = [hT[0:PT, k * PIECES * P:(k + 1) * PIECES * P].bitcast(I32) for k in range(3)]
            ms = [dma("sp", temp[k].rearrange("t (c p) -> t c p", p=P), a["dst_line"][k:k + EP].rearrange("(c t p) -> t c p", t=PT, p=P)) for k in range(3)]
            m0 = mark("dve", dve.memset(spare[:, SOFTMAX_AT:], 0.0))
            wait("dve", *ms, m0)
            m1 = mark("dve", dve.tensor_tensor(same_prev[:], temp[1], temp[0], ALU.is_equal))
            m2 = mark("dve", dve.tensor_tensor(same_next[:], temp[1], temp[2], ALU.is_equal))
            wait("dve", m1, m2)
            whole = picked[0:PT, 0:2 * PIECES].rearrange("p (k c) -> p k c", k=2)
            for k, same in enumerate((same_prev, same_next)):
                m = mark("dve", dve.tensor_reduce(whole[:, k, :], same[:].rearrange("t (c p) -> t c p", p=P), AX.X, ALU.min))
            wait("pe", m)
            for k in range(2):
                for c in range(PIECES):
                    b, col = 2 * k + c // 7, c % 7 * PT
                    m = mark("pe", pe.matmul(bank[b][0:1, col:col + PT], picked[:, k * PIECES + c:k * PIECES + c + 1], ident[:, 0:PT], start=True, stop=True))
            wait("dve", m)
            for b, (lo, hi) in enumerate(((0, 7 * PT), (7 * PT, TILES))):
                m = mark("dve", dve.tensor_copy(same_row[:, lo:hi], bank[b][0:1, 0:hi - lo]))
                m = mark("dve", dve.tensor_scalar(clamp_row[:, lo:hi], bank[b][0:1, 0:hi - lo], 2 * BIG, -BIG, ALU.mult, ALU.add))
                m = mark("dve", dve.tensor_scalar(clamp_next_row[:, lo:hi], bank[2 + b][0:1, 0:hi - lo], 2 * BIG, -BIG, ALU.mult, ALU.add))
            free[:] = [None] * 8

        DVE_LINKS = (2, 2, 5, 3, 3, 7, 4, 1)
        LINKS_TO = [sum(DVE_LINKS[:k + 1]) for k in range(len(DVE_LINKS))]
        LINKS, HOPS, EXPS = LINKS_TO[-1], 6, 2
        DVE_AT = {0: 0, 2: 1, 4: 2, 5: 3, 7: 4, 9: 5, 11: 6}
        PE_AT = {1: 0, 3: 1, 5: 2, 8: 3, 10: 4, 12: 5}

        def attention():
            pr.barrier()
            m0 = mark("dve", dve.memset(rows[:], 0.0))
            wait("dve", m0)
            dve.memset(max_row[:, 0:1], -BIG)
            m0 = mark("dve", dve.memset(behind_row[:, PT - 1:PT], -BIG))
            wait("dve", m0)
            scale = float(D) ** -0.5

            def phases(c, j):
                t = c * PIECE_TURNS + j
                if isinstance(c, int):
                    return t, t < TURNS, 0 <= t - LAG < TURNS, 1 <= c <= PIECES
                return t, True, True, True

            def pieces(engine, body):
                body(0)
                body(1)
                with engine.Fori(0, PIECES - 2) as i:
                    body(i + 2)
                body(PIECES)
                body(PIECES + 1)

            with nc.Block() as block:
                @block.gpsimd
                def _(_e):
                    gather_loop(table_kv, 2 * D, stashed=True)

                @block.sync
                def _(_e):
                    def store(t, h):
                        at(sp, c_turned, t, QUADS, 2 * h + 2)
                        sp.sem_inc(c_sp_issue.sem, 1)
                        sp.dma_start(stash[bass.ds(t * 2 + h, 1)].rearrange("a p (s d) -> (a p) s d", d=D),
                                     G[:, h * HALF:(h + 1) * HALF, D:2 * D]).then_inc(c_stored[h].sem, 16)

                    def load(t, q):
                        at(sp, c_stored[q // 2], t, 16, 16)
                        sp.sem_inc(c_sp_issue.sem, 1)
                        at(sp, c_rows, t, QUADS, q + 1 - QUADS)
                        sp.sem_inc(c_sp_issue.sem, 1)
                        part = q % 2 * QUAD * D
                        sp.dma_start(v_rows[:, q * QUAD:(q + 1) * QUAD, :].rearrange("p s d -> p (s d)"),
                                     stash[bass.ds(t * 2 + q // 2, 1), :, part:part + QUAD * D].rearrange("a p d -> (a p) d")).then_inc(c_loaded[q].sem, 16)

                    with sp.Fori(0, LAG - 1) as i:
                        store(i, 0)
                        store(i, 1)
                    with sp.Fori(0, TURNS - LAG + 1) as i:
                        for q in range(QUADS):
                            if q % 2:
                                store(i + (LAG - 1), q // 2)
                            load(i, q)
                    with sp.Fori(0, LAG - 1) as i:
                        for q in range(QUADS):
                            load(i + (TURNS - LAG + 1), q)

                @block.scalar
                def _(_e):
                    quad_idx = load_idx_loop(c_turned)

                    def piece(c):
                        for j in range(PIECE_TURNS):
                            t, scores_on, _, softmax_on = phases(c, j)
                            if softmax_on and j == 0:
                                if not isinstance(c, int) or c > 1:
                                    at(act, c_link, c - 2, LINKS, LINKS)
                                act.copy(next_row[:, 0:PT], clamp_next_row[:, bass.ds((c - 1) * PT, PT)])
                                edges = bass.ds((c - 1) * P, P)
                                act.activation(clamp_prev[0:PT, :], same_prev[:, edges], ACT.Copy, bias=-BIG, scale=2 * BIG)
                                act.activation(clamp_next[0:PT, :], same_next[:, edges], ACT.Copy, bias=-BIG, scale=2 * BIG).then_inc(c_exp.sem, 1)
                            for q in range(QUADS):
                                if scores_on:
                                    at(act, c_turned, t, QUADS, q + 1)
                                    at(act, c_scores, t, QUADS, q + 1 - QUADS)
                                    act.copy(quad(KT, q).rearrange("p s d -> p (s d)"), bank[q % 2][:, :]).then_inc(c_kt.sem, 1)
                                    quad_idx(t, q)
                                if softmax_on and j == 0 and q == 2:
                                    at(act, c_link, c - 1, LINKS, LINKS_TO[2])
                                    act.activation(expo[0:PT, :], fwd[0:PT, :], ACT.Exp, scale=scale)
                                    act.activation(carry[:, 1:2], carry[:, 0:1], ACT.Exp, scale=scale).then_inc(c_exp.sem, 1)
                    pieces(act, piece)

                @block.tensor
                def _(_e):
                    def turn(t, q):
                        at(pe, c_kt, t, QUADS, q - 1)
                        for s in range(q * QUAD, (q + 1) * QUAD):
                            slot_landed(t, s)
                            ins = pe.transpose(bank[q % 2][:, (s % QUAD) * P:(s % QUAD + 1) * P], G[:, s, 0:D], ident[:])
                        ins.then_inc(c_turned.sem, 1)

                    def scores(t, q):
                        windows = windows_of(PE, t, q)
                        at(pe, c_kt, t, QUADS, q + 1)
                        at(pe, c_picked, t, QUADS, q - 1)
                        for s in range(q * QUAD, (q + 1) * QUAD):
                            w = qT[:, bass.ds(windows[s % QUAD], P)]
                            ins = pe.matmul(bank[2 + q % 2][:, (s % QUAD) * P:(s % QUAD + 1) * P], KT[:, s, :], w, start=True, stop=True)
                        ins.then_inc(c_scores.sem, 1)

                    def hop(c, k):
                        if k == 0:
                            at(pe, c_picked, c * PIECE_TURNS, QUADS, 0)
                            ins = pe.transpose(bank[6][:, 0:P], picked, ident[:])
                        else:
                            at(pe, c_link, c - 1, LINKS, LINKS_TO[k - 1 if k < 3 else k])
                            if k in (1, 3):
                                pe.matmul(bank[7][0:1, 0:PT], back[:, P - 1:P], ident[:, 0:PT], start=True, stop=True)
                                ins = pe.matmul(bank[7][0:1, PT:2 * PT], back[:, 0:1], ident[:, 0:PT], start=True, stop=True)
                            elif k in (2, 4):
                                pe.matmul(bank[7][0:PT, P:P + 1], (max_row if k == 2 else sum_row)[:, 0:PT], ones[0:1, 0:1], start=True, stop=True)
                                ins = pe.matmul(bank[7][0:PT, P + 1:P + 2], behind_row[:, 0:PT], ones[0:1, 0:1], start=True, stop=True)
                            else:
                                pe.transpose(bank[6][:, 0:P], fwd, ident[:])
                                ins = pe.matmul(bank[7][:, P + 2:P + 3], ones[0:1, :], carry[:, 2:3], start=True, stop=True)
                        ins.then_inc(c_hop.sem, 1)

                    def piece(c):
                        for j in range(PIECE_TURNS):
                            t, scores_on, sums_on, softmax_on = phases(c, j)
                            for q in range(QUADS):
                                if scores_on:
                                    turn(t, q)
                                if q and scores_on:
                                    scores(t, q - 1)
                                elif not q and phases(c, j - 1)[1] and (not isinstance(c, int) or t > 0):
                                    scores(t - 1, QUADS - 1)
                                if softmax_on and 8 * j + 2 * q in PE_AT:
                                    hop(c, PE_AT[8 * j + 2 * q])
                                if sums_on:
                                    pe_sums(t - LAG, q, quad_loaded, v_rows, (4, 5))
                                if softmax_on and 8 * j + 2 * q + 1 in PE_AT:
                                    hop(c, PE_AT[8 * j + 2 * q + 1])
                    pieces(pe, piece)

                @block.vector
                def _(_e):
                    def pick(c, j, q):
                        t = phases(c, j)[0]
                        at(dve, c_scores, t, QUADS, q + 1)
                        at(dve, c_picked, t, QUADS, q)
                        if j == 0 and q == 0 and (not isinstance(c, int) or c > 0):
                            at(dve, c_hop, c - 1, HOPS, 1)
                        for s in range(q * QUAD, (q + 1) * QUAD):
                            ins = dve.scalar_tensor_tensor(scratch[:, s % QUAD, :], ramp[:], place[:, bass.ds(t * SLOTS + s, 1)],
                                                           bank[2 + q % 2][:, (s % QUAD) * P:(s % QUAD + 1) * P],
                                                           ALU.is_equal, ALU.mult, accum_out=picked[:, j * SLOTS + s:j * SLOTS + s + 1])
                        ins.then_inc(c_picked.sem, 1)

                    def softmax_steps(c):
                        taken = [0]
                        now = bass.ds((c - 1) * PT, PT)
                        edges = bass.ds((c - 1) * P, P)

                        def link(ins):
                            taken[0] += 1
                            ins.then_inc(c_link.sem, 1)

                        def linked():
                            at(dve, c_link, c - 1, LINKS, taken[0])

                        def hopped(k):
                            at(dve, c_hop, c - 1, HOPS, k + 1)

                        def forward(keep, values, first, ops):
                            link(dve.tensor_tensor_scan(fwd[0:PT, :], keep, values, first, *ops))
                            linked()

                        def backward(first):
                            link(dve.tensor_tensor_scan(back[0:PT, ::-1], clamp_next[0:PT, ::-1], fwd[0:PT, ::-1], first, ALU.min, ALU.max))

                        def carries_behind(values):
                            link(dve.tensor_tensor_scan(behind_row[:, 0:PT - 1][:, ::-1], next_row[:, 1:PT][:, ::-1],
                                                        values[:, 1:PT][:, ::-1], -BIG, ALU.min, ALU.max))

                        def both_carries():
                            link(dve.tensor_copy(cols[0:PT, 0:2], bank[7][0:PT, P:P + 2]))
                            linked()

                        top, add = (ALU.min, ALU.max), (ALU.mult, ALU.add)
                        logits = bank[6][0:PT, 0:P]
                        ends, begins = bank[7][0:1, 0:PT], bank[7][0:1, PT:2 * PT]

                        def step(k):
                            if k == 0:
                                hopped(0)
                                at(dve, c_exp, c - 1, EXPS, 1)
                                forward(clamp_prev[0:PT, :], logits, -BIG, top)
                                backward(-BIG)
                            elif k == 1:
                                hopped(1)
                                link(dve.tensor_tensor_scan(max_row[:, 1:PT + 1], clamp_row[:, now], ends, max_row[:, 0:1], *top))
                                carries_behind(begins)
                            elif k == 2:
                                hopped(2)
                                both_carries()
                                link(dve.tensor_tensor_scan(fwd[0:PT, :], clamp_prev[0:PT, :], back[0:PT, :], cols[0:PT, 0:1], *top))
                                linked()
                                backward(cols[0:PT, 1:2])
                                linked()
                                link(dve.tensor_tensor(fwd[0:PT, :], logits, back[0:PT, :], ALU.subtract))
                                link(dve.tensor_scalar(carry[:, 0:1], max_row[:, 0:1], back[0:1, 0:1], 0.0, ALU.subtract, ALU.min))
                            elif k == 3:
                                at(dve, c_exp, c - 1, EXPS, 2)
                                link(dve.tensor_tensor(sum_row[:, 0:1], sum_row[:, 0:1], carry[:, 1:2], ALU.mult))
                                forward(same_prev[:, edges], expo[0:PT, :], 0.0, add)
                                backward(-BIG)
                            elif k == 4:
                                hopped(3)
                                link(dve.tensor_tensor_scan(sum_row[:, 1:PT + 1], same_row[:, now], ends, sum_row[:, 0:1], *add))
                                linked()
                                link(dve.tensor_tensor(whole_row[:, 0:PT], begins, sum_row[:, 0:PT], ALU.add))
                                linked()
                                carries_behind(whole_row)
                            elif k == 5:
                                hopped(4)
                                both_carries()
                                forward(same_prev[:, edges], expo[0:PT, :], cols[0:PT, 0:1], add)
                                backward(cols[0:PT, 1:2])
                                linked()
                                link(dve.tensor_scalar(back[0:PT, :], back[0:PT, :], 1e-16, None, ALU.max))
                                linked()
                                link(dve.reciprocal(back[0:PT, :], back[0:PT, :]))
                                linked()
                                link(dve.tensor_tensor(fwd[0:PT, :], expo[0:PT, :], back[0:PT, :], ALU.mult))
                                link(dve.tensor_tensor(carry[:, 2:3], sum_row[:, 0:1], back[0:1, 0:1], ALU.mult))
                            elif k == 6:
                                hopped(5)
                                link(dve.tensor_copy(weight[:, now], bank[6][:, 0:PT]))
                                link(dve.tensor_copy(rescale, bank[7][:, P + 2:P + 3]))
                                link(dve.tensor_copy(max_row[:, 0:1], max_row[:, PT:PT + 1]))
                                link(dve.tensor_copy(sum_row[:, 0:1], sum_row[:, PT:PT + 1]))
                            else:
                                windows = windows_of(DVE, (c - 1) * PIECE_TURNS, 0, 1)
                                at(dve, c_added, (c - 1) * PIECE_TURNS, SLOTS, 0)
                                column = aggT[:, bass.ds(windows[0], 1)]
                                link(dve.tensor_scalar(column, column, rescale, None, ALU.mult))
                            assert taken[0] == LINKS_TO[k]
                        return step, linked

                    def piece(c):
                        step, linked = softmax_steps(c)
                        for j in range(PIECE_TURNS):
                            t, scores_on, _, softmax_on = phases(c, j)
                            i = t - LAG
                            for q in range(QUADS):
                                if softmax_on and q == 0 and j == 3:
                                    step(7)
                                if softmax_on and q == 0 and j >= 2:
                                    linked()
                                if scores_on:
                                    pick(c, j, q)
                                if softmax_on and 8 * j + 2 * q in DVE_AT:
                                    step(DVE_AT[8 * j + 2 * q])
                                q_onehot, q_add = q + 2, q
                                if isinstance(c, int):
                                    q_onehot = q_onehot if 0 <= i * QUADS + q_onehot < TURNS * QUADS else None
                                    q_add = q_add if 0 <= i < TURNS else None
                                if q_onehot is not None or q_add is not None:
                                    onehot_and_add(i, q_onehot, weight, q_add, banks=(4, 5))
                                if softmax_on and 8 * j + 2 * q + 1 in DVE_AT:
                                    step(DVE_AT[8 * j + 2 * q + 1])
                    pieces(dve, piece)
            finish([(c, 16 * TURNS) for c in c_gather + c_stored + c_loaded] + [(c_idx, QUADS * (TURNS + 1)), (c_added, SLOTS * TURNS)])
            finish([(c, QUADS * TURNS) for c in (c_turned, c_kt, c_scores, c_picked, c_rows, c_onehot)])
            finish([(c_link, LINKS * PIECES), (c_hop, HOPS * PIECES), (c_exp, EXPS * PIECES)])

        wm = wts[:, 0:D + 1]
        wrep = wts[:, 2 * D:3 * D]
        ws = load_weights([(wm[:, 0:D], a["W_msg"]), (wm[:, D:D + 1], a["W_att"][0:D, :]), (small[:, 0:1], a["W_att"][D:2 * D, :]),
                           (rowsW[0:1, 0:D], a["b_msg"]), (rowsW[0:1, D:D + 1], a["b_att"]),
                           (biasc[:, 0:3], a["b_ih"]), (biasc[:, 3:6], a["b_hh"]), (small[:, 1:3], a["bn"])])
        wait("dve", *ws, m_ones)
        m_rep = mark("dve", dve.tensor_scalar(wrep, ones[:], small[:, 0:1], None, ALU.mult))
        m_br = mark("dve", dve.tensor_tensor(small[:, 4:6], biasc[:, 0:2], biasc[:, 3:5], ALU.add))
        m_tail = mark("dve", dve.memset(qT[:, NP:NW], 0.0))
        m_xT = transpose_blocks(xT, xN, m_x + [m_ident])
        pr.barrier()
        zero_sums()
        nodes_T(qT, [(wrep, xT)], ACT.Identity, 0.0)
        make_table(table_gated, [(xT, wm)], D + 1, rowsW[0:1, 0:D + 1])
        aggregate_gated()

        w_ih, w_hh = wts[:, 0:3 * D], wts[:, 3 * D:6 * D]
        pr.barrier()
        ws = load_weights([(w_ih, a["W_ih"]), (w_hh, a["W_hh"])])
        wait("pe", *ws)
        gate_r, gate_z, mix = (spare[:, k * 2 * CHUNK:(k + 1) * 2 * CHUNK].rearrange("p (j c) -> p j c", j=2) for k in range(3))
        for c in range(14):
            j, k = c % 2, 4 * (c % 2)
            cut = slice(c * CHUNK, (c + 1) * CHUNK)
            r_p, z_p, in_p, hn_p = (bank[k + n][:, 0:CHUNK] for n in range(4))
            wait("pe", free[k], free[k + 3])
            for o, g, both in ((r_p, 0, True), (z_p, 1, True)):
                pe.matmul(o, w_ih[:, g * D:(g + 1) * D], aggT[:, cut], start=True, stop=False)
                pe.matmul(o, w_hh[:, g * D:(g + 1) * D], xT[:, cut], start=False, stop=True)
            pe.matmul(in_p, w_ih[:, 2 * D:3 * D], aggT[:, cut], start=True, stop=True)
            m = mark("pe", pe.matmul(hn_p, w_hh[:, 2 * D:3 * D], xT[:, cut], start=True, stop=True))
            wait("act", m)
            m_r = mark("act", act.activation(gate_r[:, j, :], r_p, ACT.Sigmoid, bias=small[:, 4:5]))
            m_z = mark("act", act.activation(gate_z[:, j, :], z_p, ACT.Sigmoid, bias=small[:, 5:6]))
            wait("dve", m_r)
            m = mark("dve", dve.scalar_tensor_tensor(mix[:, j, :], hn_p, biasc[:, 5:6], gate_r[:, j, :], ALU.add, ALU.mult))
            wait("dve", m)
            m = mark("dve", dve.tensor_tensor(mix[:, j, :], mix[:, j, :], in_p, ALU.add))
            wait("act", m)
            m = mark("act", act.activation(mix[:, j, :], mix[:, j, :], ACT.Tanh, bias=biasc[:, 2:3]))
            wait("dve", m, m_z)
            m = mark("dve", dve.tensor_tensor(gate_r[:, j, :], xT[:, cut], mix[:, j, :], ALU.subtract))
            wait("dve", m)
            m = mark("dve", dve.tensor_tensor(gate_r[:, j, :], gate_r[:, j, :], gate_z[:, j, :], ALU.mult))
            wait("dve", m)
            m = mark("dve", dve.tensor_tensor(hT[:, cut], gate_r[:, j, :], mix[:, j, :], ALU.add))
            free[k] = free[k + 3] = m
        wait("dve", m)
        BN = 250
        assert NODES % BN == 0 and NODES // BN <= BLOCKS
        for c in range(NODES // BN):
            m = mark("dve", dve.bn_stats(stats[:, c, :], hT[:, c * BN:(c + 1) * BN]))
        wait("dve", m)
        m = mark("dve", dve.bn_aggr(moments[:, 0, :], stats[:, 0:NODES // BN, :].rearrange("p c s -> p (c s)")))
        wait("dve", m)
        m = mark("dve", dve.tensor_scalar(small[:, 6:7], moments[:, 0, 1:2], EPS, None, ALU.add))
        wait("act", m)
        m = mark("act", act.activation(small[:, 6:7], small[:, 6:7], ACT.Sqrt))
        wait("dve", m)
        m = mark("dve", dve.reciprocal(small[:, 6:7], small[:, 6:7]))
        wait("dve", m)
        m = mark("dve", dve.tensor_scalar(small[:, 6:7], small[:, 6:7], small[:, 1:2], None, ALU.mult))
        wait("dve", m)
        m = mark("dve", dve.tensor_scalar(hT[:], hT[:], moments[:, 0, 0:1], small[:, 6:7], ALU.subtract, ALU.mult))
        m_b = dma("sp", rowsW[0:1, 0:D], a["beta"])
        wait("pe", m, m_b)
        nextN = qT[:, 0:NP].rearrange("p (b d) -> p b d", d=D)
        free[:] = [None] * 8
        m = layer_norm(nextN, [(xT, ident[:]), (hT, ident[:])], rowsW[0:1, 0:D])
        m_x = transpose_blocks(xT, nextN, [m])

        wq, wkv, wskip = wts[:, 0:D], wts[:, D:3 * D], wts[:, 3 * D:4 * D]
        prepare_softmax()
        for l in range(HEADS_L1):
            last = l == HEADS_L1 - 1
            pr.barrier()
            inT = xT if l == 0 else hT
            ws = load_weights([(wq, a["Wq"][l]), (wkv[:, 0:D], a["Wk"][l]), (wkv[:, D:2 * D], a["Wv"][l]), (wskip, a["Ws"][l]),
                               (biasc[:, 0:1], a["bq"][l]), (biasc[:, 1:2], a["bs_col"][l]),
                               (rowsW[0:1, 0:D], a["bk"][l:l + 1, :]), (rowsW[0:1, D:2 * D], a["bv"][l:l + 1, :])])
            wait("pe", *ws)
            wait("act", *ws)
            zero_sums()
            if l == 0:
                mark("dve", dve.memset(qT[:, NP:NW], 0.0))
            nodes_T(qT, [(wq, inT)], ACT.Identity, biasc[:, 0:1])
            make_table(table_kv, [(inT, wkv)], 2 * D, rowsW[0:1, 0:2 * D])
            attention()
            pr.barrier()
            if not last:
                nodes_T(hT, [(ident[:], aggT), (wskip, inT)], ACT.Relu, biasc[:, 1:2])
        m_b = dma("sp", rowsW[0:1, 0:D], a["bs"][HEADS_L1 - 1:HEADS_L1, :])
        wait("pe", m_b)
        m = layer_norm(nextN, [(xT, ident[:]), (aggT, ident[:]), (hT, wskip)], rowsW[0:1, 0:D])
        wait("sp", m)
        dma("sp", table[0].rearrange("(b p) d -> p b d", p=P), nextN)
        transpose_blocks(xT, nextN, [m])

        for l in range(3):
            inT = (xT, hT, qT)[l]
            outT = (hT, qT, None)[l]
            pr.barrier()
            wl, wr = wts[:, 0:D], wts[:, D:2 * D]
            ws = load_weights([(wl, a[f"W_l{l}"]), (wr, a[f"W_r{l}"]), (biasc[:, 0:1], a["b_sage_col"][l]), (rowsW[0:1, 0:D], a["b_sage"][l:l + 1, :])])
            zero_sums()
            aggregate(table[l % 2], inv_degree)
            pr.barrier()
            if l < 2:
                make_table(table[(l + 1) % 2], [(aggT, wl), (inT, wr)], D, rowsW[0:1, 0:D], func=ACT.Relu)
                nodes_T(outT, [(wl, aggT), (wr, inT)], ACT.Relu, biasc[:, 0:1])
        nextN = hT[:].rearrange("p (b d) -> p b d", d=D)
        m = layer_norm(nextN, [(xT, ident[:]), (aggT, wl), (qT, wr)], rowsW[0:1, 0:D])
        transpose_blocks(xT, nextN, [m])
        pr.barrier()

        wup = wts[:, 0:D]
        wout = [wts[:, D:2 * D], wts[:, 2 * D:3 * D]]
        A3, A2, A1 = wts[:, 3 * D:4 * D], wts[:, 4 * D:5 * D], wts[0:2 * FEATS, 5 * D:6 * D]
        m = mark("dve", dve.memset(wts[:], 0.0))
        wait("sp", m)
        up = wup.rearrange("p (g w) -> p g w", g=4)
        parts = [(up[0:MUL, 0, :], a["W_up_s"])]
        for k in range(2):
            hid = slice(k * HID, (k + 1) * HID)
            parts += [(A1[k * FEATS:(k + 1) * FEATS, hid], a["A1"]), (A2[hid, hid], a["A2"]), (A3[hid, :], a["A3"]),
                      (biasc[hid, 0:1], a["b1"]), (biasc[hid, 1:2], a["b2"])]
        for i in range(3):
            parts.append((up[:, 1 + i, :], a["W_up_v"][i]))
        outv = [w[:, MUL:D].rearrange("p (w i) -> p i w", i=3) for w in wout]
        parts.append((wout[0][0:2 * MUL, 0:MUL], a["W_out_s"]))
        vec = sb("vec", [P, MUL])
        parts.append((vec[0:2 * MUL, :], a["W_out_v"]))
        parts.append((vec[2 * MUL:P, :], a["W_out_v"]))
        ws = load_weights(parts)
        wait("dve", *ws)
        scale_out = 0.1 * float(2 * MUL) ** -0.5
        m = mark("dve", dve.tensor_scalar(wout[0][0:2 * MUL, 0:MUL], wout[0][0:2 * MUL, 0:MUL], scale_out, None, ALU.mult))
        for w, axis_lo, axis_hi in ((outv[0], None, 0), (outv[1], 1, 2)):
            if axis_lo is not None:
                m = mark("dve", dve.tensor_scalar(w[0:2 * MUL, axis_lo, :], vec[0:2 * MUL, :], scale_out, None, ALU.mult))
            m = mark("dve", dve.tensor_scalar(w[2 * MUL:P, axis_hi, :], vec[2 * MUL:P, :], scale_out, None, ALU.mult))
        zero_sums(whole=True)
        pr.barrier()
        make_table(table[0], [(xT, wup)], D, None, scale=float(MUL) ** -0.5)
        pr.barrier()
        msg = qT[:, 0:SLOTS * 2 * D].rearrange("p (s m) -> p s m", m=2 * D)
        PAIR = 2 * QUAD * P // 2
        ef = hT[0:2 * FEATS, 0:2 * PAIR].rearrange("p (h e) -> p h e", h=2)
        H1, H2 = (hT[:, (2 + 2 * k) * PAIR:(4 + 2 * k) * PAIR].rearrange("p (h e) -> p h e", h=2) for k in range(2))
        tmp = KT[:].rearrange("p s d -> p (s d)")
        ea = qT[:, SLOTS * 2 * D:SLOTS * 2 * D + 2 * HALF * 4].rearrange("p (h s c) -> p h s c", h=2, c=4)
        c_ea = c_loaded[0:2]
        with nc.Block() as block:
            @block.gpsimd
            def _(_e):
                gather_loop(table[0], D)

            @block.sync
            def _(_e):
                def features(h, column):
                    sp.dma_start(ef[:, h, :], a["edge_feats"][:, bass.ds(column, PAIR)]).then_inc(c_ef[h].sem, 16)

                features(0, 0)
                features(1, PAIR)

                def turn(i, last):
                    for h in range(2):
                        at(sp, c_msg, i, QUADS, 2 * h + 2 - QUADS)
                        sp.dma_start(ea[:, h, :, :].rearrange("p s c -> p (s c)"),
                                     a["edge_attrs"][:, bass.ds(i * SLOTS * 4 + h * HALF * 4, HALF * 4)]).then_inc(c_ea[h].sem, 16)
                        if not last:
                            at(sp, c_h1, i, 2, h + 1)
                            features(h, (i * 2 + (h + 2)) * PAIR)
                turns(sp, turn)

            @block.scalar
            def _(_e):
                quad_idx = load_idx_loop(c_rows)

                def layer1(i, h):
                    at(act, c_h1, i, 2, h + 1)
                    at(act, c_h2, i, 2, h - 1)
                    act.activation(H1[:, h % 2, :], bank[0][:, :], ACT.Silu, bias=biasc[:, 0:1]).then_inc(c_h1s.sem, 1)

                def layer2(i, h):
                    at(act, c_h2, i, 2, h + 1)
                    at(act, c_tp, i, QUADS, 2 * h - 2)
                    act.activation(H2[:, h % 2, :], bank[1][:, :], ACT.Silu, bias=biasc[:, 1:2]).then_inc(c_h2s.sem, 1)

                def onehot(i, q):
                    at(act, c_rows, i, QUADS, q + 1 - QUADS)
                    for k, s in enumerate(slots_of(q)):
                        ins = act.activation(OH[:, s, :], ramp[:], ACT.Abs, bias=place[:, bass.ds(i * SLOTS + (q * QUAD + k), 1)], scale=-1.0)
                    ins.then_inc(c_far.sem, 1)
                    at(act, c_far, i, QUADS, q + 1)
                    act.activation(quad(OH, q % QUADS), quad(OH, q % QUADS), ACT.Relu, bias=1.0, scale=-1.0).then_inc(c_onehot.sem, 1)

                layer1(0, 0)
                layer2(0, 0)
                onehot(0, 0)
                onehot(0, 1)

                def turn(i, last):
                    layer1(i, 1)
                    onehot(i, 2)
                    layer2(i, 1)
                    quad_idx(i, 0)
                    if not last:
                        layer1(i, 2)
                    onehot(i, 3)
                    if not last:
                        layer2(i, 2)
                        onehot(i, 4)
                    quad_idx(i, 1)
                    if not last:
                        onehot(i, 5)
                    quad_idx(i, 2)
                    quad_idx(i, 3)
                turns(act, turn)

            @block.tensor
            def _(_e):
                def product1(i, h):
                    at(pe, c_ef[h % 2], i, 16, 16 * (1 + h // 2))
                    at(pe, c_h1s, i, 2, h)
                    pe.matmul(bank[0][:, :], A1, ef[:, h % 2, :], start=True, stop=True).then_inc(c_h1.sem, 1)

                def product2(i, h):
                    at(pe, c_h1s, i, 2, h + 1)
                    at(pe, c_h2s, i, 2, h)
                    pe.matmul(bank[1][:, :], A2, H1[:, h % 2, :], start=True, stop=True).then_inc(c_h2.sem, 1)

                def product3(i, q):
                    h, j = q // 2, q % 2
                    hid = slice(j * HID, (j + 1) * HID)
                    at(pe, c_h2s, i, 2, h + 1)
                    at(pe, c_msg, i, QUADS, q - 1)
                    for t in range(QUAD):
                        ins = pe.matmul(bank[2 + j][:, t * P:(t + 1) * P], H2[hid, h % 2, t * P:(t + 1) * P], A3[hid, :], start=True, stop=True)
                    ins.then_inc(c_tp.sem, 1)

                def sum_up(i, q):
                    at(pe, c_msg, i, QUADS, q + 1)
                    at(pe, c_onehot, i, QUADS, q + 1)
                    at(pe, c_added, i, SLOTS, (q - 1) * QUAD)
                    for s in range(q * QUAD, (q + 1) * QUAD):
                        for part in range(2):
                            o = bank[4 + 2 * (q % 2) + (s % QUAD) // 2][:, ((s % 2) * 2 + part) * P:((s % 2) * 2 + part + 1) * P]
                            ins = pe.matmul(o, msg[:, s, part * D:(part + 1) * D], OH[:, s, :], start=True, stop=True)
                    ins.then_inc(c_rows.sem, 1)

                product1(0, 0)
                product2(0, 0)
                product3(0, 0)
                product3(0, 1)
                product1(0, 1)

                def turn(i, last):
                    product2(i, 1)
                    sum_up(i, 0)
                    product3(i, 2)
                    if not last:
                        product1(i, 2)
                    sum_up(i, 1)
                    product3(i, 3)
                    if not last:
                        product2(i, 2)
                    sum_up(i, 2)
                    if not last:
                        product3(i, 4)
                        product1(i, 3)
                    sum_up(i, 3)
                    if not last:
                        product3(i, 5)
                turns(pe, turn)

            @block.vector
            def _(_e):
                def messages(i, q):
                    j, h, turn_q, q = q % 2, q % QUADS // 2, q, q % QUADS
                    at(dve, c_rows, i, QUADS, turn_q + 1 - QUADS)
                    for s in range(q * QUAD, (q + 1) * QUAD):
                        at(dve, c_gather[s], i, 16, 16 * (1 + turn_q // QUADS))
                    if q % 2 == 0:
                        at(dve, c_ea[h], i, 16, 16 * (1 + turn_q // QUADS))
                    at(dve, c_tp, i, QUADS, turn_q + 1)
                    w = bank[2 + j][:, :].rearrange("p (s g u) -> p s g u", s=QUAD, g=4)
                    g = G[:, q * QUAD:(q + 1) * QUAD, 0:D].rearrange("p s (g u) -> p s g u", g=4)
                    y = ea[:, h, (q % 2) * QUAD:(q % 2 + 1) * QUAD, :]
                    mq = msg[:, q * QUAD:(q + 1) * QUAD, :]
                    ys = y[:, :, 0:1].to_broadcast([P, QUAD, MUL])
                    yv = y[:, :, 1:4].unsqueeze(3).to_broadcast([P, QUAD, 3, MUL])
                    n = QUAD * MUL
                    ss_w0, ss_w1, ys_w2, dot = (tmp[:, (8 * j + k) * n:(8 * j + k + 1) * n].rearrange("p (s u) -> p s u", u=MUL) for k in range(4))
                    prod = tmp[:, (8 * j + 4) * n:(8 * j + 7) * n].rearrange("p (s i u) -> p s i u", s=QUAD, i=3)
                    v1 = mq[:, :, 2 * MUL:].rearrange("p s (i k u) -> p s i k u", i=3, k=2)
                    dve.tensor_tensor(ss_w0, g[:, :, 0, :], w[:, :, 0, :], ALU.mult)
                    dve.tensor_tensor(ss_w1, g[:, :, 0, :], w[:, :, 1, :], ALU.mult)
                    dve.tensor_tensor(ys_w2, ys, w[:, :, 2, :], ALU.mult)
                    dve.tensor_tensor(prod, g[:, :, 1:4, :], yv, ALU.mult).then_inc(c_step.sem, 1)
                    at(dve, c_step, i, 3 * QUADS, 3 * turn_q + 1)
                    dve.tensor_tensor(dot, prod[:, :, 0, :], prod[:, :, 1, :], ALU.add).then_inc(c_step.sem, 1)
                    dve.tensor_tensor(mq[:, :, 0:MUL], ss_w0, ys, ALU.mult)
                    at(dve, c_step, i, 3 * QUADS, 3 * turn_q + 2)
                    dve.tensor_tensor(dot, dot, prod[:, :, 2, :], ALU.add).then_inc(c_step.sem, 1)
                    dve.tensor_tensor(v1[:, :, :, 0, :], ss_w1.unsqueeze(2).to_broadcast([P, QUAD, 3, MUL]), yv, ALU.mult)
                    dve.tensor_tensor(v1[:, :, :, 1, :], g[:, :, 1:4, :], ys_w2.unsqueeze(2).to_broadcast([P, QUAD, 3, MUL]), ALU.mult)
                    at(dve, c_step, i, 3 * QUADS, 3 * turn_q + 3)
                    dve.scalar_tensor_tensor(mq[:, :, MUL:2 * MUL], dot, float(3.0 ** -0.5), w[:, :, 3, :], ALU.mult, ALU.mult).then_inc(c_msg.sem, 1)

                def add_pairs(i, q):
                    windows = windows_of(DVE, i, q)
                    at(dve, c_rows, i, QUADS, q + 1)
                    for k in range(QUAD):
                        w = sums[:, :, bass.ds(windows[k], P)]
                        o = bank[4 + 2 * (q % 2) + k // 2][:, (k % 2) * 2 * P:((k % 2) * 2 + 2) * P].rearrange("p (k n) -> p k n", k=2)
                        at(dve, c_added, i, SLOTS, q * QUAD + k)
                        dve.tensor_tensor(w, w, o, ALU.add).then_inc(c_added.sem, 1)

                messages(0, 0)

                def turn(i, last):
                    for q in range(QUADS):
                        if not last or q + 1 < QUADS:
                            messages(i, q + 1)
                        add_pairs(i, q)
                turns(dve, turn)
        finish([(c, 16 * TURNS) for c in c_gather + c_ef + c_ea] + [(c_idx, QUADS * (TURNS + 1)), (c_added, SLOTS * TURNS)])
        pr.barrier()
        nextN = hT[:].rearrange("p (b d) -> p b d", d=D)
        m = layer_norm(nextN, [(xT, ident[:]), (aggT, wout[0]), (spare, wout[1])], None)
        wait("sp", m)
        dma("sp", out.rearrange("(b p) d -> p b d", p=P), nextN)
        pr.all_dmas("sp")


def kernel(**inputs):
    import concourse.bacc as bacc
    from concourse.bass_utils import run_bass_kernel_spmd

    x = {k: np.asarray(v) for k, v in inputs.items()}

    def padded(v, rows, fill=0):
        return np.concatenate([v, np.full((rows - v.shape[0],) + v.shape[1:], fill, v.dtype)])

    def tiles(v):
        return np.swapaxes(v.reshape((TILES, P) + v.shape[1:]), 0, 1)

    src, dst = padded(x["src"], EP), padded(x["dst"], EP, NO_NODE)
    up_v = np.zeros((3, D, MUL), np.float32)
    for i in range(3):
        up_v[i, MUL + i::3, :] = x["L3_gnn_W_up_v"]
    arrays = {
        "x": padded(x["x"], NP),
        "src_tile": np.concatenate([tiles(src), np.zeros((P, SLOTS), src.dtype)], axis=1),
        "dst_tile": tiles(dst),
        "dst_first": dst[::P],
        "dst_line": np.concatenate([np.full(1, -1, dst.dtype), dst, np.full(1, 2 * NO_NODE, dst.dtype)]),
        "edge_attrs": tiles(padded(x["edge_attr_4"], EP)).reshape(P, TILES * 4),
        "edge_feats": padded(x["edge_attr_8"], EP).reshape(2 * TURNS, 2, QUAD * P, FEATS)
        .transpose(1, 3, 0, 2).reshape(2 * FEATS, 2 * TURNS * QUAD * P),
        "W_msg": x["L0_gnn_W_msg"], "W_att": x["L0_gnn_W_att"],
        "b_msg": x["L0_gnn_b_msg"].reshape(1, D), "b_att": x["L0_gnn_b_att"].reshape(1, 1),
        "W_ih": x["L0_gnn_W_ih"].T, "W_hh": x["L0_gnn_W_hh"].T,
        "b_ih": x["L0_gnn_b_ih"].reshape(3, D).T, "b_hh": x["L0_gnn_b_hh"].reshape(3, D).T,
        "bn": np.stack([x["L0_gnn_gamma"], x["L0_gnn_beta"]], axis=1), "beta": x["L0_gnn_beta"].reshape(1, D),
        "Wq": x["L1_gnn_Wq"], "Wk": x["L1_gnn_Wk"], "Wv": x["L1_gnn_Wv"], "Ws": x["L1_gnn_Ws"],
        "bq": x["L1_gnn_bq"].reshape(HEADS_L1, D, 1), "bk": x["L1_gnn_bk"], "bv": x["L1_gnn_bv"], "bs": x["L1_gnn_bs"], "bs_col": x["L1_gnn_bs"].reshape(HEADS_L1, D, 1),
        "b_sage": np.stack([x[f"L2_gnn_b{l}"] for l in range(3)]),
        "b_sage_col": np.stack([x[f"L2_gnn_b{l}"] for l in range(3)]).reshape(3, D, 1),
        "W_up_s": x["L3_gnn_W_up_s"], "W_up_v": up_v,
        "A1": x["L3_gnn_A1"], "A2": x["L3_gnn_A2"], "A3": x["L3_gnn_A3"],
        "b1": x["L3_gnn_b1"].reshape(HID, 1), "b2": x["L3_gnn_b2"].reshape(HID, 1),
        "W_out_s": x["L3_gnn_W_out_s"], "W_out_v": x["L3_gnn_W_out_v"],
    }
    for l in range(3):
        arrays[f"W_l{l}"], arrays[f"W_r{l}"] = x[f"L2_gnn_W_l{l}"], x[f"L2_gnn_W_r{l}"]
    arrays = {f"in_{k}": np.ascontiguousarray(v) for k, v in arrays.items()}

    nc = bacc.Bacc("TRN2", target_bir_lowering=False, num_devices=1)
    drams = {k[3:]: nc.dram_tensor(k, v.shape, mybir.dt.from_np(v.dtype), kind="ExternalInput").ap() for k, v in arrays.items()}
    out = nc.dram_tensor("out", (NP, D), F32, kind="ExternalOutput").ap()
    build_program(nc, drams, out)
    result = run_bass_kernel_spmd(nc, [arrays], core_ids=[0])
    return result.results[0]["out"][:NODES]
```

```python
from contextlib import ExitStack

import numpy as np

import concourse.bass as bass
from concourse import mybir

F32 = mybir.dt.float32
I32 = mybir.dt.int32
ALU = mybir.AluOpType
ACT = mybir.ActivationFunctionType
AX = mybir.AxisListType

DVE, PE = mybir.EngineType.DVE, mybir.EngineType.PE
P = 128
NODES = 6250
EDGES = 106250
D = 128
BLOCKS = -(-NODES // P)
NP = BLOCKS * P
NW = NP + P
SLOTS = 16
QUAD = 4
QUADS = SLOTS // QUAD
HALF = SLOTS // 2
TURNS = -(-EDGES // (P * SLOTS))
TILES = TURNS * SLOTS
EP = TILES * P
LINES = EP // (8 * P)
LINE = EP // LINES
PIECE_TURNS = 4
PIECES = TURNS // PIECE_TURNS
PT = PIECE_TURNS * SLOTS
LAG = PIECE_TURNS + 3
CHUNK = NP // 14
TRANSFORMERS = 3
MUL = 32
HID = 64
FEATS = 8
NO_NODE = 1 << 20
EPS = 1e-5
BIG = 1e38

assert CHUNK * 14 == NP and CHUNK <= 512 and LINE == 8 * P and LINES <= P and TILES % 8 == 0
assert PIECES * PIECE_TURNS == TURNS and PT <= P and PIECES <= 14


class Count:

    def __init__(self, sem, value=0):
        self.sem, self.value = sem, value


class Program:
    def __init__(self, nc, ctx):
        self.nc, self.ctx = nc, ctx
        self.engines = {"pe": nc.tensor, "act": nc.scalar, "dve": nc.vector, "pool": nc.gpsimd, "sp": nc.sync}
        self.done = {k: self.count(f"done_{k}") for k in self.engines}
        self.lanes = [self.count(f"lane{i}") for i in range(8)]
        self.lane_at = 0

    def sbuf(self, name, shape, dt=F32):
        return self.ctx.enter_context(self.nc.sbuf_tensor(name, shape, dt))

    def count(self, name):
        return Count(self.ctx.enter_context(self.nc.semaphore(name)))

    def wait(self, engine, *marks):
        for m in marks:
            if m is not None:
                self.engines[engine].wait_ge(m[0].sem, m[1])

    def mark(self, engine, instruction):
        c = self.done[engine]
        c.value += 1
        instruction.then_inc(c.sem, 1)
        return c, c.value

    def dma(self, engine, out, in_):
        lane = self.lanes[self.lane_at % len(self.lanes)]
        self.lane_at += 1
        if lane.value:
            self.engines[engine].wait_ge(lane.sem, lane.value)
        lane.value += 16
        self.engines[engine].dma_start(out, in_).then_inc(lane.sem, 16)
        return lane, lane.value

    def so_far(self, *engines):
        return [(self.done[e], self.done[e].value) for e in engines]

    def all_dmas(self, engine):
        for lane in self.lanes:
            if lane.value:
                self.engines[engine].wait_ge(lane.sem, lane.value)

    def barrier(self):
        self.all_dmas("sp")
        self.nc.all_engine_barrier()


def build_program(nc, a, out):
    with ExitStack() as ctx:
        pr = Program(nc, ctx)
        sb, wait, mark, dma = pr.sbuf, pr.wait, pr.mark, pr.dma
        pe, act, dve, pool, sp = nc.tensor, nc.scalar, nc.vector, nc.gpsimd, nc.sync
        bank = [ctx.enter_context(nc.psum_tensor(f"bank{i}", [P, 512], F32)) for i in range(8)]

        def dram(name, shape):
            return nc.dram_tensor(name, shape, F32, kind="Internal").ap()

        table_gated = dram("table_gated", (NP, D + 1))
        table_kv = dram("table_kv", (NP, 2 * D))
        table = [dram(f"table_h{i}", (NP, D)) for i in range(2)]
        stash = dram("stash", (2 * TURNS, P, HALF * D))

        ident = sb("ident", [P, P])
        ramp = sb("ramp", [P, P])
        ones = sb("ones", [P, P])
        src_idx = sb("src_idx", [P, TILES + SLOTS], I32)
        start = sb("start", [P, TILES], I32)
        place = sb("place", [P, TILES])
        same_prev = sb("same_prev", [PT, PIECES * P])
        same_next = sb("same_next", [PT, PIECES * P])
        rows = sb("rows", [1, 6, P])
        cols = sb("cols", [P, 8])
        xT = sb("xT", [P, NP])
        hT = sb("hT", [P, NP])
        qT = sb("qT", [P, NW])
        sums = sb("sums", [P, 2, NW])
        aggT = sums[:, 0, :]
        spare = sums[:, 1, :]
        inv_degree = sb("inv_degree", [P, TILES])
        weight = sb("weight", [P, TILES])
        wts = sb("wts", [P, 6 * D])
        bias_rows = sb("bias_rows", [P, 2 * D])
        biasc = sb("biasc", [P, 8])
        small = sb("small", [P, 16])

        G = sb("G", [P, SLOTS, 2 * D])
        OH = sb("OH", [P, SLOTS, P])
        KT = sb("KT", [P, SLOTS, P])
        idx = sb("idx", [P, SLOTS], I32)
        per_slot = sb("per_slot", [P, 3, SLOTS])
        stats = sb("stats", [P, BLOCKS, 6])
        moments = sb("moments", [P, BLOCKS, 2])

        m_in = [dma("sp", src_idx[:], a["src_tile"]), dma("sp", start[:], a["dst_first"].rearrange("(a t) -> a t", a=1).to_broadcast([P, TILES]))]
        dst_i = inv_degree[:].bitcast(I32)
        m_dst = dma("sp", dst_i, a["dst_tile"])
        lines = [spare[0:LINES, k * LINE:(k + 1) * LINE].bitcast(I32) for k in range(3)]
        m_lines = [dma("sp", lines[k], a["dst_line"][k:k + EP].rearrange("(i r) -> i r", i=LINES)) for k in range(3)]
        m_x = []
        xN = hT[:].rearrange("p (b d) -> p b d", d=D)
        for b0 in range(0, BLOCKS, 7):
            m_x.append(dma("act", xN[:, b0:b0 + 7, :], a["x"].rearrange("(b p) d -> p b d", p=P)[:, b0:b0 + 7, :]))
        mark("pool", pool.iota(ramp[:], [[1, P]], base=0, channel_multiplier=0, allow_small_or_imprecise_dtypes=True))
        m = mark("pool", pool.memset(ident[:], 0.0))
        wait("pool", m)
        m_ident = mark("pool", pool.affine_select(out=ident[:], in_=ident[:], compare_op=ALU.not_equal, fill=1.0, base=0, pattern=[[-1, P]], channel_multiplier=1))
        m_ones = mark("dve", dve.memset(ones[:], 1.0))
        wait("dve", *m_in, m_dst)
        m1 = mark("dve", dve.tensor_scalar(start[:], start[:], float(NODES - 1), None, ALU.min))
        m2 = mark("dve", dve.tensor_copy(weight[:], dst_i))
        wait("dve", m1, m2)
        m3 = mark("dve", dve.tensor_tensor(place[:], weight[:], start[:], ALU.subtract))
        free = [None] * 8

        def chunk_of(b):
            return ((b + 1) * P - 1) // CHUNK

        def transposed(source, ready, n, done):
            for g, b0 in enumerate(range(0, n, QUAD)):
                nb = min(QUAD, n - b0)
                k = g % 8
                wait("pe", free[k], *ready(b0 + nb - 1))
                for j in range(nb):
                    m = pe.transpose(bank[k][:, j * P:(j + 1) * P], source(b0 + j), ident[:])
                free[k] = done(b0, nb, k, mark("pe", m))

        def to_T(dstT, srcN, ready):
            def done(b0, nb, k, m):
                who, e = (("act", act.copy), ("dve", dve.tensor_copy))[b0 // QUAD % 2]
                wait(who, m)
                return mark(who, e(dstT[:, b0 * P:(b0 + nb) * P], bank[k][:, 0:nb * P]))
            transposed(lambda b: srcN[:, b, :], ready, BLOCKS, done)

        def product_T(terms, done, banks=range(8), between=lambda: None):
            marks = []
            for c in range(14):
                k = banks[c % len(banks)]
                cut = slice(c * CHUNK, (c + 1) * CHUNK)
                wait("pe", free[k])
                for n, (w, nodesT) in enumerate(terms):
                    m = pe.matmul(bank[k][:, 0:CHUNK], w, nodesT[:, cut], start=n == 0, stop=n == len(terms) - 1)
                free[k] = done(cut, bank[k][:, 0:CHUNK], mark("pe", m))
                marks.append(free[k])
                between()
            return marks

        def nodes_T(dstT, terms, func, bias, **more):
            def done(cut, psum, m):
                wait("act", m)
                return mark("act", act.activation(dstT[:, cut], psum, func, bias=bias))
            return product_T(terms, done, **more)

        stage_at = [0]
        stage_free = [None] * 8
        stage = G[:].rearrange("p s d -> p (s d)").rearrange("p (s d) -> p s d", d=512)

        def send(dst, b0, nb, width, evacuate):
            s = stage_at[0] % 8
            stage_at[0] += 1
            piece = stage[:, s, 0:nb * width]
            m, r = evacuate(piece, stage_free[s])
            wait("sp", m)
            stage_free[s] = dma("sp", dst[b0 * P:(b0 + nb) * P, :].rearrange("(b p) d -> p b d", p=P), piece.rearrange("p (b d) -> p b d", d=width))
            return r

        def make_table(dst, srcT, w, width, bias=None, scale=1.0, ready=None):
            per = 512 // width
            for g, b0 in enumerate(range(0, BLOCKS, per)):
                nb = min(per, BLOCKS - b0)
                k = g % 8
                wait("pe", free[k], *([ready[chunk_of(b0 + nb - 1)]] if ready else []))
                for j in range(nb):
                    m = pe.matmul(bank[k][:, j * width:(j + 1) * width], srcT[:, (b0 + j) * P:(b0 + j + 1) * P], w, start=True, stop=True)
                m = mark("pe", m)

                def evacuate(piece, piece_free):
                    psum = bank[k][:, 0:nb * width]
                    if bias is None:
                        wait("act", m, piece_free)
                        r = mark("act", act.activation(piece, psum, ACT.Copy, scale=scale))
                    else:
                        wait("dve", m, piece_free)
                        r = mark("dve", dve.tensor_tensor(piece.rearrange("p (b d) -> p b d", d=width), psum.rearrange("p (b d) -> p b d", d=width),
                                                          bias.unsqueeze(1).to_broadcast([P, nb, width]), ALU.add))
                    return r, r
                free[k] = send(dst, b0, nb, width, evacuate)

        def table_of(dst, srcT, ready):
            def done(b0, nb, k, m):
                def evacuate(piece, piece_free):
                    wait("dve", m, piece_free)
                    r = mark("dve", dve.tensor_copy(piece, bank[k][:, 0:nb * P]))
                    return r, r
                return send(dst, b0, nb, D, evacuate)
            transposed(lambda b: srcT[:, b * P:(b + 1) * P], lambda b: [ready[chunk_of(b)]], BLOCKS, done)

        def layer_norm(dstN, yT, ready, rows_to):
            def done(b0, nb, k, m):
                wait("dve", m)
                for j in range(nb):
                    s = mark("dve", dve.bn_stats(stats[:, b0 + j, :], bank[k][:, j * P:(j + 1) * P]))
                wait("act", s)
                return mark("act", act.copy(dstN[:, b0:b0 + nb, :].rearrange("p b d -> p (b d)"), bank[k][:, 0:nb * P]))
            transposed(lambda b: yT[:, b * P:(b + 1) * P], lambda b: [ready[chunk_of(b)]], BLOCKS, done)
            copied = pr.so_far("act")
            wait("dve", *pr.so_far("dve"))
            for b in range(BLOCKS):
                m = mark("dve", dve.bn_aggr(moments[:, b, :], stats[:, b, :]))
            wait("dve", m)
            mean, var, shift = moments[:, :, 0], moments[:, :, 1], stats[:, :, 0]
            m = mark("dve", dve.tensor_scalar(var, var, EPS, None, ALU.add))
            wait("act", m)
            m = mark("act", act.activation(var, var, ACT.Sqrt))
            wait("dve", m)
            m = mark("dve", dve.reciprocal(var, var))
            wait("dve", m)
            m = mark("dve", dve.scalar_tensor_tensor(shift, mean, -1.0, var, ALU.mult, ALU.mult))
            wait("act", m)
            wait("dve", *copied)
            blocks_ready = [None] * BLOCKS
            for g in range(0, BLOCKS, 7):
                for b in range(g, g + 7):
                    if b % 2:
                        blocks_ready[b] = [mark("act", act.activation(dstN[:, b, :], dstN[:, b, :], ACT.Identity, bias=shift[:, b:b + 1], scale=var[:, b:b + 1]))]
                    else:
                        blocks_ready[b] = [mark("dve", dve.tensor_scalar(dstN[:, b, :], dstN[:, b, :], mean[:, b:b + 1], var[:, b:b + 1], ALU.subtract, ALU.mult))]
                if rows_to is not None:
                    wait("sp", *blocks_ready[g + 5], *blocks_ready[g + 6])
                    dma("sp", rows_to[g * P:(g + 7) * P, :].rearrange("(b p) d -> p b d", p=P), dstN[:, g:g + 7, :])
            return blocks_ready

        def back_to_T(dstT, srcN, blocks_ready):
            to_T(dstT, srcN, lambda b: [m for i in range(max(0, b - 3), b + 1) for m in blocks_ready[i]])

        def load_weights(parts):
            return [dma("sp", o, i) for o, i in parts]

        def zero_sums(whole=False):
            return mark("dve", dve.memset(sums[:, :, :] if whole else aggT, 0.0))

        DEGREE_BANKS = (0, 2, 3, 4, 5)

        def degrees():
            wait("dve", *m_lines)
            before, here, after = lines
            eq_next = spare[0:LINES, 3 * LINE:4 * LINE]
            line_same, line_next, fwd, back = (hT[0:LINES, k * LINE:(k + 1) * LINE] for k in range(4))
            m4 = mark("dve", dve.tensor_tensor(line_same, here, before, ALU.is_equal))
            m5 = mark("dve", dve.tensor_tensor(eq_next, here, after, ALU.is_equal))
            wait("dve", m4, m5)
            m6 = mark("dve", dve.tensor_scalar(line_next, eq_next, 2 * BIG, -BIG, ALU.mult, ALU.add))
            wait("dve", m6)
            dve.tensor_reduce(cols[0:LINES, 0:1], line_same, AX.X, ALU.min)
            m7 = mark("dve", dve.tensor_reduce(cols[0:LINES, 1:2], line_next, AX.X, ALU.min))
            yield
            wait("pe", m7)
            for k in range(2):
                m8 = mark("pe", pe.matmul(bank[0][0:1, k * P:k * P + LINES], cols[0:LINES, k:k + 1], ident[0:LINES, 0:LINES], start=True, stop=True))
            wait("dve", m8)
            for k in range(2):
                m9 = mark("dve", dve.tensor_copy(rows[0:1, k, 0:LINES], bank[0][0:1, k * P:k * P + LINES]))
            ROW_SAME, ROW_NEXT, ROW_END, ROW_CARRY = range(4)

            def carried(row_keep, end, reverse, lowest, op_keep, op_take, m_end):
                yield
                wait("pe", m_end)
                m = mark("pe", pe.matmul(bank[2][0:1, 0:LINES], end, ident[0:LINES, 0:LINES], start=True, stop=True))
                wait("dve", m)
                m = mark("dve", dve.tensor_copy(rows[0:1, ROW_END, 0:LINES], bank[2][0:1, 0:LINES]))
                carry = rows[0:1, ROW_CARRY, :]
                m0 = mark("dve", dve.memset(carry, lowest))
                wait("dve", m, m0)
                k, x = rows[0:1, row_keep, 0:LINES], rows[0:1, ROW_END, 0:LINES]
                if reverse:
                    m = mark("dve", dve.tensor_tensor_scan(carry[:, 0:LINES - 1][:, ::-1], k[:, 1:][:, ::-1], x[:, 1:][:, ::-1], lowest, op_keep, op_take))
                else:
                    m = mark("dve", dve.tensor_tensor_scan(carry[:, 1:LINES], k[:, 0:LINES - 1], x[:, 0:LINES - 1], lowest, op_keep, op_take))
                yield
                wait("pe", m)
                m = mark("pe", pe.matmul(bank[3][0:LINES, 0:1], carry[:, 0:LINES], ones[0:1, 0:1], start=True, stop=True))
                wait("dve", m)
                m = mark("dve", dve.tensor_copy(cols[0:LINES, 3:4], bank[3][0:LINES, 0:1]))
                wait("dve", m)

            each = spare[0:LINES, 0:LINE]
            m = mark("dve", dve.memset(each, 1.0))
            wait("dve", m, m9)
            m = mark("dve", dve.tensor_tensor_scan(fwd, line_same, each, 0.0, ALU.mult, ALU.add))
            yield from carried(ROW_SAME, fwd[:, LINE - 1:LINE], False, 0.0, ALU.mult, ALU.add, m)
            m = mark("dve", dve.tensor_tensor_scan(fwd, line_same, each, cols[0:LINES, 3:4], ALU.mult, ALU.add))
            wait("dve", m)
            m = mark("dve", dve.tensor_tensor_scan(back[:, ::-1], line_next[:, ::-1], fwd[:, ::-1], -BIG, ALU.min, ALU.max))
            yield from carried(ROW_NEXT, back[:, 0:1], True, -BIG, ALU.min, ALU.max, m)
            m = mark("dve", dve.tensor_tensor_scan(back[:, ::-1], line_next[:, ::-1], fwd[:, ::-1], cols[0:LINES, 3:4], ALU.min, ALU.max))
            yield
            wait("pe", m)
            for j in range(8):
                m = mark("pe", pe.transpose(bank[4 + j // 4][:, (j % 4) * P:(j % 4) * P + LINES], back[:, j * P:(j + 1) * P], ident[0:LINES, 0:LINES]))
            degree = inv_degree[:].rearrange("p (i j) -> p j i", j=8)
            wait("dve", m)
            for h in range(2):
                m = mark("dve", dve.tensor_scalar(degree[:, 4 * h:4 * h + 4, :], bank[4 + h][:, :].rearrange("p (j i) -> p j i", j=4)[:, :, 0:LINES], 1.0, None, ALU.max))
            wait("dve", m)
            m_degree = mark("dve", dve.reciprocal(inv_degree[:], inv_degree[:]))
            for k in DEGREE_BANKS:
                free[k] = m_degree

        v_rows = spare[:, 0:SLOTS * D].rearrange("p (s d) -> p s d", d=D)
        scratch = spare[:, SLOTS * D:(SLOTS + QUAD) * D].rearrange("p (s d) -> p s d", d=D)
        SOFTMAX_AT = (SLOTS + QUAD) * D
        fwd, back, expo, clamp_prev, clamp_next = (spare[:, SOFTMAX_AT + k * P:SOFTMAX_AT + (k + 1) * P] for k in range(5))
        picked = spare[:, SOFTMAX_AT + 5 * P:SOFTMAX_AT + 6 * P]
        row_at = SOFTMAX_AT + 6 * P
        same_row, clamp_row, clamp_next_row = (spare[0:1, row_at + k * TILES:row_at + (k + 1) * TILES] for k in range(3))
        max_row, behind_row, sum_row, whole_row, carry, next_row = (rows[0:1, k, :] for k in range(6))
        rescale = cols[:, 7:8]

        c_gather = [pr.count(f"gather{s}") for s in range(SLOTS)]
        c_idx = pr.count("idx_ready")
        c_issue = pr.count("pool_issue")
        c_sp_issue = pr.count("sp_issue")
        c_rows = pr.count("rows_used")
        c_added = pr.count("added")
        c_onehot = pr.count("onehot_ready")
        c_z = pr.count("gate_in")
        c_gate = pr.count("gate_ready")
        c_bd = pr.count("dst_part")
        c_turned = pr.count("turned")
        c_kt = pr.count("kt_ready")
        c_scores = pr.count("scores")
        c_picked = pr.count("picked")
        c_stored = [pr.count(f"stored{h}") for h in range(2)]
        c_loaded = [pr.count(f"loaded{q}") for q in range(QUADS)]
        c_link = pr.count("softmax_link")
        c_hop = pr.count("softmax_hop")
        c_exp = pr.count("softmax_exp")
        c_ef = [pr.count(f"ef{h}") for h in range(2)]
        c_h1 = pr.count("h1_psum")
        c_h1s = pr.count("h1_ready")
        c_h2 = pr.count("h2_psum")
        c_h2s = pr.count("h2_ready")
        c_tp = pr.count("tp_psum")
        c_far = pr.count("distance")
        c_step = pr.count("msg_step")
        c_msg = pr.count("msg_ready")
        sp.sem_inc(c_rows.sem, QUADS)
        sp.sem_inc(c_added.sem, SLOTS)
        sp.sem_inc(c_turned.sem, QUADS)
        sp.sem_inc(c_scores.sem, QUADS)
        sp.sem_inc(c_kt.sem, QUADS)
        sp.sem_inc(c_picked.sem, QUADS)
        for h in range(2):
            sp.sem_inc(c_stored[h].sem, 16)
            c_stored[h].value = 16
        c_rows.value = c_turned.value = c_scores.value = c_kt.value = c_picked.value = QUADS
        c_added.value = SLOTS
        for c in (c_h1s, c_h2s, c_tp, c_h1, c_h2, c_msg):
            sp.sem_inc(c.sem, QUADS)
            c.value = QUADS

        def at(eng, c, turn, per_turn, n):
            eng.wait_ge(c.sem, turn * per_turn + (c.value + n))

        def quad(buf, q):
            return buf[:, q * QUAD:(q + 1) * QUAD]

        def first_idx():
            act.copy(idx[:], src_idx[:, 0:SLOTS]).then_inc(c_idx.sem, QUADS)

        def load_idx_loop(c_free):
            def quad_idx(i, q):
                at(act, c_free, i, QUADS, q + 1)
                act.copy(quad(idx, q), src_idx[:, bass.ds((i + 1) * SLOTS + q * QUAD, QUAD)]).then_inc(c_idx.sem, 1)
            return quad_idx

        def gather_loop(tab, width, stashed=False):
            with pool.Fori(0, TURNS) as i:
                for q in range(QUADS):
                    at(pool, c_idx, i, QUADS, q + 1)
                    if stashed:
                        at(pool, c_stored[q // 2], i, 16, 0)
                    pool.sem_inc(c_issue.sem, 1)
                    for s in range(q * QUAD, (q + 1) * QUAD):
                        pool.indirect_dma_start(G[:, s, 0:width], None, tab,
                                                bass.IndirectOffsetOnAxis(ap=idx[:, s:s + 1], axis=0)).then_inc(c_gather[s].sem, 16)

        def finish(counts):
            for c, n in counts:
                c.value += n
            free[:] = [None] * 8

        def windows_of(kind, i, q, n=QUAD):
            _, values = nc.values_load_multi_w_load_instructions(
                start[0:1, bass.ds(i * SLOTS + q * QUAD, n)], engines=(kind,), min_val=0, max_val=NODES - 1,
                skip_runtime_bounds_check_because="starts are dst values, clamped to the nodes")
            return values

        def turns(engine, body):
            with engine.Fori(0, TURNS - 1) as i:
                body(i, False)
            body(TURNS - 1, True)

        def slots_of(q):
            return [q % QUADS * QUAD + k for k in range(QUAD)]

        def onehot_and_add(i, q_onehot, weights, q_add, c_weights=None, banks=range(4), between=lambda: None):
            windows = windows_of(DVE, i, q_add) if q_add is not None else None
            for k in range(QUAD):
                if q_onehot is not None:
                    s = slots_of(q_onehot)[k]
                    tile = bass.ds(i * SLOTS + (q_onehot * QUAD + k), 1)
                    if k == 0:
                        if c_weights is not None:
                            at(dve, c_weights, i, QUADS, q_onehot + 1)
                        at(dve, c_rows, i, QUADS, q_onehot + 1 - QUADS)
                    w = weights[:, tile] if weights.shape[1] == TILES else weights[:, s:s + 1]
                    ins = dve.tensor_scalar(OH[:, s, :], ramp[:], place[:, tile], w, ALU.is_equal, ALU.mult)
                    if k == QUAD - 1:
                        ins.then_inc(c_onehot.sem, 1)
                between()
                if q_add is not None:
                    if k == 0:
                        at(dve, c_rows, i, QUADS, q_add + 1)
                    w = aggT[:, bass.ds(windows[k], P)]
                    at(dve, c_added, i, SLOTS, q_add * QUAD + k)
                    dve.tensor_tensor(w, w, bank[banks[q_add % len(banks)]][:, k * P:(k + 1) * P], ALU.add).then_inc(c_added.sem, 1)
                between()

        def pe_sums(i, q, rows_ready, view, banks=range(4)):
            at(pe, c_onehot, i, QUADS, q + 1)
            at(pe, c_added, i, SLOTS, (q + 1 - len(banks)) * QUAD)
            for s in range(q * QUAD, (q + 1) * QUAD):
                rows_ready(i, s)
                ins = pe.matmul(bank[banks[q % len(banks)]][:, (s % QUAD) * P:(s % QUAD + 1) * P], view[:, s, :], OH[:, s, :], start=True, stop=True)
            ins.then_inc(c_rows.sem, 1)

        def slot_landed(i, s):
            at(pe, c_gather[s], i, 16, 16)

        def quad_loaded(i, s):
            if s % QUAD == 0:
                at(pe, c_loaded[s // QUAD], i, 16, 16)

        def aggregate(tab, weights):
            with nc.Block() as block:
                @block.gpsimd
                def _(_e):
                    gather_loop(tab, D)

                @block.scalar
                def _(_e):
                    quad_idx = load_idx_loop(c_rows)
                    with act.Fori(0, TURNS) as i:
                        for q in range(QUADS):
                            quad_idx(i, q)

                @block.tensor
                def _(_e):
                    with pe.Fori(0, TURNS) as i:
                        for q in range(QUADS):
                            pe_sums(i, q, slot_landed, G[:, :, 0:D])

                @block.vector
                def _(_e):
                    for q in range(2):
                        onehot_and_add(0, q, weights, None)

                    def turn(i, last):
                        for q in range(QUADS):
                            onehot_and_add(i, None if last and q + 2 >= QUADS else q + 2, weights, q)
                    turns(dve, turn)
            finish([(c, 16 * TURNS) for c in c_gather] + [(c_idx, QUADS * (TURNS + 1))])
            finish([(c_rows, QUADS * TURNS), (c_onehot, QUADS * TURNS), (c_added, SLOTS * TURNS)])

        def aggregate_gated():
            dst_part, gate_in, gate = (per_slot[:, k, :] for k in range(3))
            with nc.Block() as block:
                @block.gpsimd
                def _(_e):
                    gather_loop(table_gated, D + 1)

                @block.scalar
                def _(_e):
                    quad_idx = load_idx_loop(c_rows)
                    act.activation(small[:, 3:4], ones[:, 0:1], ACT.Sigmoid)

                    def sigmoid(i, q):
                        at(act, c_z, i, QUADS, q + 1)
                        act.activation(quad(gate, q % QUADS), quad(gate_in, q % QUADS), ACT.Sigmoid).then_inc(c_gate.sem, 1)

                    sigmoid(0, 0)
                    sigmoid(0, 1)

                    def turn(i, last):
                        for q in range(QUADS):
                            if not last or q + 2 < QUADS:
                                sigmoid(i, q + 2)
                            quad_idx(i, q)
                    turns(act, turn)

                @block.tensor
                def _(_e):
                    with pe.Fori(0, TURNS) as i:
                        for q in range(QUADS):
                            pe_sums(i, q, slot_landed, G[:, :, 0:D])

                @block.vector
                def _(_e):
                    def dst_parts(i, q):
                        windows = windows_of(DVE, i, q)
                        for k, s in enumerate(slots_of(q)):
                            ins = dve.scalar_tensor_tensor(KT[:, s, :], ramp[:], place[:, bass.ds(i * SLOTS + (q * QUAD + k), 1)],
                                                           qT[:, bass.ds(windows[k], P)],
                                                           ALU.is_equal, ALU.mult, accum_out=dst_part[:, s:s + 1])
                        ins.then_inc(c_bd.sem, 1)

                    def gate_inputs(i, q):
                        for s in slots_of(q):
                            at(dve, c_gather[s], i, 16, 16 * (1 + q // QUADS))
                        at(dve, c_bd, i, QUADS, q + 1)
                        a, b = slots_of(q)[0], slots_of(q)[-1] + 1
                        dve.tensor_tensor(gate_in[:, a:b], dst_part[:, a:b], G[:, a:b, D], ALU.add).then_inc(c_z.sem, 1)

                    for q in range(2):
                        dst_parts(0, q)
                        gate_inputs(0, q)
                    onehot_and_add(0, 0, gate, None, c_gate)

                    def turn(i, last):
                        for q in range(QUADS):
                            ahead = not last or q + 2 < QUADS
                            if ahead:
                                dst_parts(i, q + 2)
                            onehot_and_add(i, q + 1 if not last or q + 1 < QUADS else None, gate, q, c_gate)
                            if ahead:
                                gate_inputs(i, q + 2)
                    turns(dve, turn)
            finish([(c, 16 * TURNS) for c in c_gather] + [(c_idx, QUADS * (TURNS + 1))])
            finish([(c, QUADS * TURNS) for c in (c_rows, c_onehot, c_z, c_gate, c_bd)] + [(c_added, SLOTS * TURNS)])

        order = [hT[0:PT, k * PIECES * P:(k + 1) * PIECES * P].bitcast(I32) for k in range(3)]

        def load_order():
            return [dma("sp", order[k].rearrange("t (c p) -> t c p", p=P), a["dst_line"][k:k + EP].rearrange("(c t p) -> t c p", t=PT, p=P)) for k in range(3)]

        def prepare_softmax(loaded):
            m0 = mark("dve", dve.memset(spare[:, SOFTMAX_AT:], 0.0))
            wait("dve", *loaded, m0)
            m1 = mark("dve", dve.tensor_tensor(same_prev[:], order[1], order[0], ALU.is_equal))
            m2 = mark("dve", dve.tensor_tensor(same_next[:], order[1], order[2], ALU.is_equal))
            wait("dve", m1, m2)
            whole = picked[0:PT, 0:2 * PIECES].rearrange("p (k c) -> p k c", k=2)
            for k, same in enumerate((same_prev, same_next)):
                m = mark("dve", dve.tensor_reduce(whole[:, k, :], same[:].rearrange("t (c p) -> t c p", p=P), AX.X, ALU.min))
            yield
            wait("pe", m)
            for k in range(2):
                for c in range(PIECES):
                    b, col = 2 * k + c // 7, c % 7 * PT
                    m = mark("pe", pe.matmul(bank[b][0:1, col:col + PT], picked[:, k * PIECES + c:k * PIECES + c + 1], ident[:, 0:PT], start=True, stop=True))
            wait("dve", m)
            for b, (lo, hi) in enumerate(((0, 7 * PT), (7 * PT, TILES))):
                m = mark("dve", dve.tensor_copy(same_row[:, lo:hi], bank[b][0:1, 0:hi - lo]))
                m = mark("dve", dve.tensor_scalar(clamp_row[:, lo:hi], bank[b][0:1, 0:hi - lo], 2 * BIG, -BIG, ALU.mult, ALU.add))
                m = mark("dve", dve.tensor_scalar(clamp_next_row[:, lo:hi], bank[2 + b][0:1, 0:hi - lo], 2 * BIG, -BIG, ALU.mult, ALU.add))
            free[0:4] = [m] * 4

        DVE_LINKS = (2, 2, 5, 3, 3, 7, 4, 1)
        LINKS_TO = [sum(DVE_LINKS[:k + 1]) for k in range(len(DVE_LINKS))]
        LINKS, HOPS, EXPS = LINKS_TO[-1], 6, 2
        STAGES_AT = {k: k for k in range(7)}
        HOPS_AT = {1: 0, 2: 1, 3: 2, 5: 3, 6: 4, 7: 5}

        def attention(skip_terms, skip_bias):
            m0 = mark("dve", dve.memset(rows[:], 0.0))
            wait("dve", m0)
            dve.memset(max_row[:, 0:1], -BIG)
            m0 = mark("dve", dve.memset(behind_row[:, PT - 1:PT], -BIG))
            wait("dve", m0)
            scale = float(D) ** -0.5
            assert PIECE_TURNS * QUADS >= 14
            m_skip = [(pr.done["pe"], pr.done["pe"].value + n + 1) for n in range(14)]
            m_kept = [(pr.done["act"], pr.done["act"].value + n + 1) for n in range(14)]

            def phases(c, j):
                t = c * PIECE_TURNS + j
                if isinstance(c, int):
                    return t, t < TURNS, 0 <= t - LAG < TURNS, 1 <= c <= PIECES
                return t, True, True, True

            def pieces(engine, body):
                body(0)
                body(1)
                with engine.Fori(0, PIECES - 2) as i:
                    body(i + 2)
                body(PIECES)
                body(PIECES + 1)

            with nc.Block() as block:
                @block.gpsimd
                def _(_e):
                    gather_loop(table_kv, 2 * D, stashed=True)

                @block.sync
                def _(_e):
                    def store(t, h):
                        at(sp, c_turned, t, QUADS, 2 * h + 2)
                        sp.sem_inc(c_sp_issue.sem, 1)
                        sp.dma_start(stash[bass.ds(t * 2 + h, 1)].rearrange("a p (s d) -> (a p) s d", d=D),
                                     G[:, h * HALF:(h + 1) * HALF, D:2 * D]).then_inc(c_stored[h].sem, 16)

                    def load(t, q):
                        at(sp, c_stored[q // 2], t, 16, 16)
                        sp.sem_inc(c_sp_issue.sem, 1)
                        at(sp, c_rows, t, QUADS, q + 1 - QUADS)
                        sp.sem_inc(c_sp_issue.sem, 1)
                        part = q % 2 * QUAD * D
                        sp.dma_start(v_rows[:, q * QUAD:(q + 1) * QUAD, :].rearrange("p s d -> p (s d)"),
                                     stash[bass.ds(t * 2 + q // 2, 1), :, part:part + QUAD * D].rearrange("a p d -> (a p) d")).then_inc(c_loaded[q].sem, 16)

                    with sp.Fori(0, LAG - 1) as i:
                        store(i, 0)
                        store(i, 1)
                    with sp.Fori(0, TURNS - LAG + 1) as i:
                        for q in range(QUADS):
                            if q % 2:
                                store(i + (LAG - 1), q // 2)
                            load(i, q)
                    with sp.Fori(0, LAG - 1) as i:
                        for q in range(QUADS):
                            load(i + (TURNS - LAG + 1), q)

                @block.scalar
                def _(_e):
                    quad_idx = load_idx_loop(c_turned)

                    def piece(c):
                        for j in range(PIECE_TURNS):
                            t, scores_on, _, softmax_on = phases(c, j)
                            if softmax_on and j == 0:
                                if not isinstance(c, int) or c > 1:
                                    at(act, c_link, c - 2, LINKS, LINKS)
                                act.copy(next_row[:, 0:PT], clamp_next_row[:, bass.ds((c - 1) * PT, PT)])
                                edges = bass.ds((c - 1) * P, P)
                                act.activation(clamp_prev[0:PT, :], same_prev[:, edges], ACT.Copy, bias=-BIG, scale=2 * BIG)
                                act.activation(clamp_next[0:PT, :], same_next[:, edges], ACT.Copy, bias=-BIG, scale=2 * BIG).then_inc(c_exp.sem, 1)
                            for q in range(QUADS):
                                if scores_on:
                                    at(act, c_turned, t, QUADS, q + 1)
                                    at(act, c_scores, t, QUADS, q + 1 - QUADS)
                                    act.copy(quad(KT, q).rearrange("p s d -> p (s d)"), bank[q % 2][:, :]).then_inc(c_kt.sem, 1)
                                    quad_idx(t, q)
                                n = j * QUADS + q
                                if isinstance(c, int) and c == 0 and n < 14:
                                    wait("act", m_skip[n])
                                    mark("act", act.activation(hT[:, n * CHUNK:(n + 1) * CHUNK], bank[4 + n % 2][:, 0:CHUNK], ACT.Identity, bias=skip_bias))
                                if softmax_on and j == 0 and q == 3:
                                    at(act, c_link, c - 1, LINKS, LINKS_TO[2])
                                    act.activation(expo[0:PT, :], fwd[0:PT, :], ACT.Exp, scale=scale)
                                    act.activation(carry[:, 1:2], carry[:, 0:1], ACT.Exp, scale=scale).then_inc(c_exp.sem, 1)
                    pieces(act, piece)

                @block.tensor
                def _(_e):
                    def turn(t, q):
                        at(pe, c_kt, t, QUADS, q - 1)
                        for s in range(q * QUAD, (q + 1) * QUAD):
                            slot_landed(t, s)
                            ins = pe.transpose(bank[q % 2][:, (s % QUAD) * P:(s % QUAD + 1) * P], G[:, s, 0:D], ident[:])
                        ins.then_inc(c_turned.sem, 1)

                    def scores(t, q):
                        windows = windows_of(PE, t, q)
                        at(pe, c_kt, t, QUADS, q + 1)
                        at(pe, c_picked, t, QUADS, q - 1)
                        for s in range(q * QUAD, (q + 1) * QUAD):
                            w = qT[:, bass.ds(windows[s % QUAD], P)]
                            ins = pe.matmul(bank[2 + q % 2][:, (s % QUAD) * P:(s % QUAD + 1) * P], KT[:, s, :], w, start=True, stop=True)
                        ins.then_inc(c_scores.sem, 1)

                    def hop(c, k):
                        if k == 0:
                            at(pe, c_picked, c * PIECE_TURNS, QUADS, 0)
                            ins = pe.transpose(bank[6][:, 0:P], picked, ident[:])
                        else:
                            at(pe, c_link, c - 1, LINKS, LINKS_TO[k - 1 if k < 3 else k])
                            if k in (1, 3):
                                pe.matmul(bank[7][0:1, 0:PT], back[:, P - 1:P], ident[:, 0:PT], start=True, stop=True)
                                ins = pe.matmul(bank[7][0:1, PT:2 * PT], back[:, 0:1], ident[:, 0:PT], start=True, stop=True)
                            elif k in (2, 4):
                                pe.matmul(bank[7][0:PT, P:P + 1], (max_row if k == 2 else sum_row)[:, 0:PT], ones[0:1, 0:1], start=True, stop=True)
                                ins = pe.matmul(bank[7][0:PT, P + 1:P + 2], behind_row[:, 0:PT], ones[0:1, 0:1], start=True, stop=True)
                            else:
                                pe.transpose(bank[6][:, 0:P], fwd, ident[:])
                                ins = pe.matmul(bank[7][:, P + 2:P + 3], ones[0:1, :], carry[:, 2:3], start=True, stop=True)
                        ins.then_inc(c_hop.sem, 1)

                    def piece(c):
                        for j in range(PIECE_TURNS):
                            t, scores_on, sums_on, softmax_on = phases(c, j)
                            if isinstance(c, int) and t == LAG:
                                wait("pe", m_kept[-1])
                            for q in range(QUADS):
                                n = j * QUADS + q
                                if isinstance(c, int) and c == 0 and n < 14:
                                    wait("pe", m_kept[n - 2] if n > 1 else None)
                                    for k, (w, nodesT) in enumerate(skip_terms):
                                        ins = pe.matmul(bank[4 + n % 2][:, 0:CHUNK], w, nodesT[:, n * CHUNK:(n + 1) * CHUNK], start=k == 0, stop=k == len(skip_terms) - 1)
                                    mark("pe", ins)
                                if scores_on:
                                    turn(t, q)
                                if q and scores_on:
                                    scores(t, q - 1)
                                elif not q and phases(c, j - 1)[1] and (not isinstance(c, int) or t > 0):
                                    scores(t - 1, QUADS - 1)
                                if softmax_on and j * QUADS + q in HOPS_AT:
                                    hop(c, HOPS_AT[j * QUADS + q])
                                if sums_on:
                                    pe_sums(t - LAG, q, quad_loaded, v_rows, (4, 5))
                    pieces(pe, piece)

                @block.vector
                def _(_e):
                    def pick(c, j, q):
                        t = phases(c, j)[0]
                        at(dve, c_scores, t, QUADS, q + 1)
                        at(dve, c_picked, t, QUADS, q)
                        if j == 0 and q == 0 and (not isinstance(c, int) or c > 0):
                            at(dve, c_hop, c - 1, HOPS, 1)
                        for s in range(q * QUAD, (q + 1) * QUAD):
                            ins = dve.scalar_tensor_tensor(scratch[:, s % QUAD, :], ramp[:], place[:, bass.ds(t * SLOTS + s, 1)],
                                                           bank[2 + q % 2][:, (s % QUAD) * P:(s % QUAD + 1) * P],
                                                           ALU.is_equal, ALU.mult, accum_out=picked[:, j * SLOTS + s:j * SLOTS + s + 1])
                        ins.then_inc(c_picked.sem, 1)

                    def softmax(c):
                        taken = [0]
                        now = bass.ds((c - 1) * PT, PT)
                        edges = bass.ds((c - 1) * P, P)

                        def link(ins):
                            taken[0] += 1
                            ins.then_inc(c_link.sem, 1)

                        def linked():
                            at(dve, c_link, c - 1, LINKS, taken[0])

                        def hopped(k):
                            at(dve, c_hop, c - 1, HOPS, k + 1)

                        def forward(keep, values, first, ops):
                            link(dve.tensor_tensor_scan(fwd[0:PT, :], keep, values, first, *ops))

                        def backward(first):
                            linked()
                            link(dve.tensor_tensor_scan(back[0:PT, ::-1], clamp_next[0:PT, ::-1], fwd[0:PT, ::-1], first, ALU.min, ALU.max))

                        def carries_behind(values):
                            link(dve.tensor_tensor_scan(behind_row[:, 0:PT - 1][:, ::-1], next_row[:, 1:PT][:, ::-1],
                                                        values[:, 1:PT][:, ::-1], -BIG, ALU.min, ALU.max))

                        top, add = (ALU.min, ALU.max), (ALU.mult, ALU.add)
                        logits = bank[6][0:PT, 0:P]
                        ends, begins = bank[7][0:1, 0:PT], bank[7][0:1, PT:2 * PT]

                        hopped(0)
                        at(dve, c_exp, c - 1, EXPS, 1)
                        forward(clamp_prev[0:PT, :], logits, -BIG, top)
                        yield
                        backward(-BIG)
                        yield
                        hopped(1)
                        link(dve.tensor_tensor_scan(max_row[:, 1:PT + 1], clamp_row[:, now], ends, max_row[:, 0:1], *top))
                        yield
                        carries_behind(begins)
                        yield
                        hopped(2)
                        link(dve.tensor_copy(cols[0:PT, 0:2], bank[7][0:PT, P:P + 2]))
                        yield
                        linked()
                        forward(clamp_prev[0:PT, :], back[0:PT, :], cols[0:PT, 0:1], top)
                        yield
                        backward(cols[0:PT, 1:2])
                        yield
                        linked()
                        link(dve.tensor_tensor(fwd[0:PT, :], logits, back[0:PT, :], ALU.subtract))
                        yield
                        link(dve.tensor_scalar(carry[:, 0:1], max_row[:, 0:1], back[0:1, 0:1], 0.0, ALU.subtract, ALU.min))
                        yield
                        at(dve, c_exp, c - 1, EXPS, 2)
                        link(dve.tensor_tensor(sum_row[:, 0:1], sum_row[:, 0:1], carry[:, 1:2], ALU.mult))
                        yield
                        forward(same_prev[:, edges], expo[0:PT, :], 0.0, add)
                        yield
                        backward(-BIG)
                        yield
                        hopped(3)
                        link(dve.tensor_tensor_scan(sum_row[:, 1:PT + 1], same_row[:, now], ends, sum_row[:, 0:1], *add))
                        yield
                        linked()
                        link(dve.tensor_tensor(whole_row[:, 0:PT], begins, sum_row[:, 0:PT], ALU.add))
                        yield
                        linked()
                        carries_behind(whole_row)
                        yield
                        hopped(4)
                        link(dve.tensor_copy(cols[0:PT, 0:2], bank[7][0:PT, P:P + 2]))
                        yield
                        linked()
                        forward(same_prev[:, edges], expo[0:PT, :], cols[0:PT, 0:1], add)
                        yield
                        backward(cols[0:PT, 1:2])
                        yield
                        linked()
                        link(dve.tensor_scalar(back[0:PT, :], back[0:PT, :], 1e-16, None, ALU.max))
                        yield
                        linked()
                        link(dve.reciprocal(back[0:PT, :], back[0:PT, :]))
                        yield
                        linked()
                        link(dve.tensor_tensor(fwd[0:PT, :], expo[0:PT, :], back[0:PT, :], ALU.mult))
                        yield
                        link(dve.tensor_tensor(carry[:, 2:3], sum_row[:, 0:1], back[0:1, 0:1], ALU.mult))
                        yield
                        hopped(5)
                        link(dve.tensor_copy(weight[:, now], bank[6][:, 0:PT]))
                        yield
                        link(dve.tensor_copy(rescale, bank[7][:, P + 2:P + 3]))
                        yield
                        link(dve.tensor_copy(max_row[:, 0:1], max_row[:, PT:PT + 1]))
                        yield
                        link(dve.tensor_copy(sum_row[:, 0:1], sum_row[:, PT:PT + 1]))
                        yield
                        windows = windows_of(DVE, (c - 1) * PIECE_TURNS, 0, 1)
                        at(dve, c_added, (c - 1) * PIECE_TURNS, SLOTS, 0)
                        column = aggT[:, bass.ds(windows[0], 1)]
                        link(dve.tensor_scalar(column, column, rescale, None, ALU.mult))
                        assert taken[0] == LINKS

                    def piece(c):
                        links = softmax(c)
                        taken, wait_for = [0], [0]

                        def take(to):
                            wait_for[0] -= 1
                            if taken[0] < to and wait_for[0] < 0:
                                taken[0] += 1
                                next(links, None)

                        for j in range(PIECE_TURNS):
                            t, scores_on, _, softmax_on = phases(c, j)
                            i = t - LAG
                            for q in range(QUADS):
                                if softmax_on and j == 3 and q == 0:
                                    take(LINKS)
                                if softmax_on and (j, q) in ((1, 3), (3, 0)):
                                    at(dve, c_link, c - 1, LINKS, taken[0])
                                if scores_on:
                                    pick(c, j, q)
                                to = LINKS_TO[STAGES_AT[j * QUADS + q]] if softmax_on and j * QUADS + q in STAGES_AT else 0
                                wait_for[0] = 3
                                q_onehot, q_add = q + 2, q
                                if isinstance(c, int):
                                    q_onehot = q_onehot if 0 <= i * QUADS + q_onehot < TURNS * QUADS else None
                                    q_add = q_add if 0 <= i < TURNS else None
                                if q_onehot is not None or q_add is not None:
                                    onehot_and_add(i, q_onehot, weight, q_add, banks=(4, 5), between=lambda: take(to))
                                while taken[0] < to:
                                    take(to)
                    pieces(dve, piece)
            finish([(c, 16 * TURNS) for c in c_gather + c_stored + c_loaded] + [(c_idx, QUADS * (TURNS + 1)), (c_added, SLOTS * TURNS)])
            finish([(c, QUADS * TURNS) for c in (c_turned, c_kt, c_scores, c_picked, c_rows, c_onehot)])
            finish([(c_link, LINKS * PIECES), (c_hop, HOPS * PIECES), (c_exp, EXPS * PIECES)])

        wm = wts[:, 0:D + 1]
        wrep = wts[:, 2 * D:3 * D]
        ws = load_weights([(wm[:, 0:D], a["W_msg"]), (wm[:, D:D + 1], a["W_att"][0:D, :]), (small[:, 0:1], a["W_att"][D:2 * D, :]),
                           (bias_rows[:, 0:D], a["b_msg"].to_broadcast([P, D])), (bias_rows[:, D:D + 1], a["b_att"].to_broadcast([P, 1])),
                           (biasc[:, 0:3], a["b_ih"]), (biasc[:, 3:6], a["b_hh"]), (small[:, 1:3], a["bn"])])
        to_T(xT, xN, lambda b: m_x[:b // 7 + 1] + [m_ident])
        wait("dve", *ws, m_ones)
        mark("dve", dve.tensor_scalar(wrep, ones[:], small[:, 0:1], None, ALU.mult))
        mark("dve", dve.tensor_tensor(small[:, 4:6], biasc[:, 0:2], biasc[:, 3:5], ALU.add))
        wait("pe", *ws, *free)
        make_table(table_gated, xT, wm, D + 1, bias=bias_rows[:, 0:D + 1])
        pr.barrier()
        first_idx()
        mark("dve", dve.memset(qT[:, NP:NW], 0.0))
        zero_sums()
        steps = degrees()
        ms = nodes_T(qT, [(wrep, xT)], ACT.Identity, 0.0, banks=(1, 6, 7), between=lambda: next(steps, None))
        for _ in steps:
            pass
        wait("dve", ms[-1])
        wait("sp", *pr.so_far("pe"))
        load_weights([(wts[:, 0:3 * D], a["W_ih"]), (wts[:, 3 * D:6 * D], a["W_hh"])])
        aggregate_gated()

        w_ih, w_hh = wts[:, 0:3 * D], wts[:, 3 * D:6 * D]
        pr.barrier()
        BN = 250
        assert NODES % BN == 0 and NODES // BN <= BLOCKS
        gate_r, gate_z, mix = (spare[:, k * 2 * CHUNK:(k + 1) * 2 * CHUNK].rearrange("p (j c) -> p j c", j=2) for k in range(3))
        for c in range(14):
            j, k = c % 2, 4 * (c % 2)
            cut = slice(c * CHUNK, (c + 1) * CHUNK)
            r_p, z_p, in_p, hn_p = (bank[k + n][:, 0:CHUNK] for n in range(4))
            wait("pe", free[k], free[k + 3])
            for o, g in ((r_p, 0), (z_p, 1)):
                pe.matmul(o, w_ih[:, g * D:(g + 1) * D], aggT[:, cut], start=True, stop=False)
                pe.matmul(o, w_hh[:, g * D:(g + 1) * D], xT[:, cut], start=False, stop=True)
            pe.matmul(in_p, w_ih[:, 2 * D:3 * D], aggT[:, cut], start=True, stop=True)
            m = mark("pe", pe.matmul(hn_p, w_hh[:, 2 * D:3 * D], xT[:, cut], start=True, stop=True))
            wait("act", m)
            m_r = mark("act", act.activation(gate_r[:, j, :], r_p, ACT.Sigmoid, bias=small[:, 4:5]))
            m_z = mark("act", act.activation(gate_z[:, j, :], z_p, ACT.Sigmoid, bias=small[:, 5:6]))
            wait("dve", m_r)
            m = mark("dve", dve.scalar_tensor_tensor(mix[:, j, :], hn_p, biasc[:, 5:6], gate_r[:, j, :], ALU.add, ALU.mult))
            wait("dve", m)
            m = mark("dve", dve.tensor_tensor(mix[:, j, :], mix[:, j, :], in_p, ALU.add))
            wait("act", m)
            m = mark("act", act.activation(mix[:, j, :], mix[:, j, :], ACT.Tanh, bias=biasc[:, 2:3]))
            wait("dve", m, m_z)
            m = mark("dve", dve.tensor_tensor(gate_r[:, j, :], xT[:, cut], mix[:, j, :], ALU.subtract))
            wait("dve", m)
            m = mark("dve", dve.tensor_tensor(gate_r[:, j, :], gate_r[:, j, :], gate_z[:, j, :], ALU.mult))
            wait("dve", m)
            m = mark("dve", dve.tensor_tensor(hT[:, cut], gate_r[:, j, :], mix[:, j, :], ALU.add))
            free[k] = free[k + 3] = m
            wait("dve", m)
            for n in range(c * CHUNK // BN, min((c + 1) * CHUNK, NODES) // BN):
                m = mark("dve", dve.bn_stats(stats[:, n, :], hT[:, n * BN:(n + 1) * BN]))
        wait("dve", m)
        m = mark("dve", dve.bn_aggr(moments[:, 0, :], stats[:, 0:NODES // BN, :].rearrange("p c s -> p (c s)")))
        wait("dve", m)
        m = mark("dve", dve.tensor_scalar(small[:, 6:7], moments[:, 0, 1:2], EPS, None, ALU.add))
        wait("act", m)
        m = mark("act", act.activation(small[:, 6:7], small[:, 6:7], ACT.Sqrt))
        wait("dve", m)
        m = mark("dve", dve.reciprocal(small[:, 6:7], small[:, 6:7]))
        wait("dve", m)
        m = mark("dve", dve.tensor_scalar(small[:, 6:7], small[:, 6:7], small[:, 1:2], None, ALU.mult))
        wait("dve", m)
        m = mark("dve", dve.scalar_tensor_tensor(small[:, 7:8], moments[:, 0, 0:1], small[:, 6:7], small[:, 2:3], ALU.mult, ALU.subtract))
        wait("dve", m)
        m = mark("dve", dve.tensor_scalar(small[:, 7:8], small[:, 7:8], -1.0, None, ALU.mult))
        wait("act", m)
        marks = []
        for c in range(14):
            part = slice(c * CHUNK, (c + 1) * CHUNK)
            m = mark("act", act.activation(hT[:, part], hT[:, part], ACT.Identity, bias=small[:, 7:8], scale=small[:, 6:7]))
            wait("dve", m)
            marks.append(mark("dve", dve.tensor_tensor(hT[:, part], hT[:, part], xT[:, part], ALU.add)))
        nextN = qT[:, 0:NP].rearrange("p (b d) -> p b d", d=D)
        free[:] = [marks[0]] * 8
        blocks_ready = layer_norm(nextN, hT, marks, None)
        wait("sp", *pr.so_far("pe", "act", "dve"))

        wq, wkv = wts[:, 0:D], wts[:, D:3 * D]
        wskip = [wts[:, (3 + k) * D:(4 + k) * D] for k in range(2)]

        def load_attention(l):
            return load_weights([(wq, a["Wq"][l]), (wkv[:, 0:D], a["Wk"][l]), (wkv[:, D:2 * D], a["Wv"][l]), (wskip[l % 2], a["Ws"][l]),
                                 (biasc[:, 0:1], a["bq"][l]), (biasc[:, 1 + l % 2:2 + l % 2], a["bs_col"][l]),
                                 (bias_rows[:, 0:D], a["bk"][l:l + 1, :].to_broadcast([P, D])), (bias_rows[:, D:2 * D], a["bv"][l:l + 1, :].to_broadcast([P, D]))])

        m_order = load_order()
        ws = load_attention(0)
        back_to_T(xT, nextN, blocks_ready)
        wait("pe", *ws)
        wait("act", *ws)
        wait("dve", *ws)
        marks = None
        for l in range(TRANSFORMERS):
            inT = xT if l == 0 else hT
            make_table(table_kv, inT, wkv, 2 * D, bias=bias_rows[:], ready=marks)
            pr.barrier()
            first_idx()
            if l == 0:
                mark("dve", dve.memset(qT[:, NP:NW], 0.0))
                steps = prepare_softmax(m_order)
                next(steps)
            zero_sums()
            ms = nodes_T(qT, [(wq, inT)], ACT.Identity, biasc[:, 0:1], banks=range(4, 8))
            if l == 0:
                next(steps, None)
                wait("pe", free[0])
            wait("pe", ms[-1])
            if l + 1 < TRANSFORMERS:
                wait("sp", ms[-1])
                load_attention(l + 1)
            last = l + 1 == TRANSFORMERS
            attention([(wskip[l % 2], inT)] + ([(ident[:], xT)] if last else []), biasc[:, 1 + l % 2:2 + l % 2])
            pr.barrier()
            marks = []
            for c in range(14):
                part = hT[:, c * CHUNK:(c + 1) * CHUNK]
                m = mark("dve", dve.tensor_tensor(part, part, aggT[:, c * CHUNK:(c + 1) * CHUNK], ALU.add))
                if not last:
                    wait("act", m)
                    m = mark("act", act.activation(part, part, ACT.Relu))
                marks.append(m)
        blocks_ready = layer_norm(nextN, hT, marks, table[0])

        sage = [(wts[:, 2 * k * D:(2 * k + 1) * D], wts[:, (2 * k + 1) * D:(2 * k + 2) * D], biasc[:, k:k + 1]) for k in range(2)]

        def load_sage(l):
            wl, wr, bias = sage[l % 2]
            return load_weights([(wl, a[f"W_l{l}"]), (wr, a[f"W_r{l}"]), (bias, a["b_sage_col"][l])])

        ws = load_sage(0)
        back_to_T(xT, nextN, blocks_ready)
        pr.barrier()
        for l in range(3):
            inT = (xT, hT, qT)[l]
            outT = (hT, qT, None)[l]
            first_idx()
            zero_sums()
            wl, wr, bias = sage[l % 2]
            wait("pe", *ws)
            wait("act", *ws)
            own = outT if l < 2 else qT
            nodes_T(own, [(wr, inT)], ACT.Identity, bias, banks=range(4, 8))
            aggregate(table[l % 2], inv_degree)
            pr.barrier()

            def with_own(cut, psum, m):
                wait("dve", m)
                m = r = mark("dve", dve.tensor_tensor(own[:, cut], psum, own[:, cut], ALU.add))
                if l < 2:
                    wait("act", m)
                    m = mark("act", act.activation(own[:, cut], own[:, cut], ACT.Relu))
                else:
                    wait("dve", m)
                    m = mark("dve", dve.tensor_tensor(own[:, cut], own[:, cut], xT[:, cut], ALU.add))
                marks.append(m)
                return r
            marks = []
            product_T([(wl, aggT)], with_own)
            if l < 2:
                ws = load_sage(l + 1)
                table_of(table[(l + 1) % 2], own, marks)
                pr.barrier()

        nextN = hT[:].rearrange("p (b d) -> p b d", d=D)
        back_to_T(xT, nextN, layer_norm(nextN, qT, marks, None))
        pr.barrier()

        wup = wts[:, 0:D]
        wout = [wts[:, D:2 * D], wts[:, 2 * D:3 * D]]
        A3, A2, A1 = wts[:, 3 * D:4 * D], wts[:, 4 * D:5 * D], wts[0:2 * FEATS, 5 * D:6 * D]
        m = mark("dve", dve.memset(wts[:], 0.0))
        wait("sp", m)
        up = wup.rearrange("p (g w) -> p g w", g=4)
        parts = [(up[0:MUL, 0, :], a["W_up_s"])]
        for k in range(2):
            hid = slice(k * HID, (k + 1) * HID)
            parts += [(A1[k * FEATS:(k + 1) * FEATS, hid], a["A1"]), (A2[hid, hid], a["A2"]), (A3[hid, :], a["A3"]),
                      (biasc[hid, 0:1], a["b1"]), (biasc[hid, 1:2], a["b2"])]
        for i in range(3):
            parts.append((up[:, 1 + i, :], a["W_up_v"][i]))
        outv = [w[:, MUL:D].rearrange("p (w i) -> p i w", i=3) for w in wout]
        parts.append((wout[0][0:2 * MUL, 0:MUL], a["W_out_s"]))
        vec = sb("vec", [P, MUL])
        parts.append((vec[0:2 * MUL, :], a["W_out_v"]))
        parts.append((vec[2 * MUL:P, :], a["W_out_v"]))
        ws = load_weights(parts)
        wait("dve", *ws)
        scale_out = 0.1 * float(2 * MUL) ** -0.5
        m = mark("dve", dve.tensor_scalar(wout[0][0:2 * MUL, 0:MUL], wout[0][0:2 * MUL, 0:MUL], scale_out, None, ALU.mult))
        for w, axis_lo, axis_hi in ((outv[0], None, 0), (outv[1], 1, 2)):
            if axis_lo is not None:
                m = mark("dve", dve.tensor_scalar(w[0:2 * MUL, axis_lo, :], vec[0:2 * MUL, :], scale_out, None, ALU.mult))
            m = mark("dve", dve.tensor_scalar(w[2 * MUL:P, axis_hi, :], vec[2 * MUL:P, :], scale_out, None, ALU.mult))
        wait("pe", *ws)
        make_table(table[0], xT, wup, D, scale=float(MUL) ** -0.5)
        pr.barrier()
        first_idx()
        zero_sums(whole=True)
        msg = qT[:, 0:SLOTS * 2 * D].rearrange("p (s m) -> p s m", m=2 * D)
        PAIR = 2 * QUAD * P // 2
        ef = hT[0:2 * FEATS, 0:2 * PAIR].rearrange("p (h e) -> p h e", h=2)
        H1, H2 = (hT[:, (2 + 2 * k) * PAIR:(4 + 2 * k) * PAIR].rearrange("p (h e) -> p h e", h=2) for k in range(2))
        tmp = KT[:].rearrange("p s d -> p (s d)")
        ea = qT[:, SLOTS * 2 * D:SLOTS * 2 * D + 2 * HALF * 4].rearrange("p (h s c) -> p h s c", h=2, c=4)
        c_ea = c_loaded[0:2]
        with nc.Block() as block:
            @block.gpsimd
            def _(_e):
                gather_loop(table[0], D)

            @block.sync
            def _(_e):
                def features(h, column):
                    sp.dma_start(ef[:, h, :], a["edge_feats"][:, bass.ds(column, PAIR)]).then_inc(c_ef[h].sem, 16)

                features(0, 0)
                features(1, PAIR)

                def turn(i, last):
                    for h in range(2):
                        at(sp, c_msg, i, QUADS, 2 * h + 2 - QUADS)
                        sp.dma_start(ea[:, h, :, :].rearrange("p s c -> p (s c)"),
                                     a["edge_attrs"][:, bass.ds(i * SLOTS * 4 + h * HALF * 4, HALF * 4)]).then_inc(c_ea[h].sem, 16)
                        if not last:
                            at(sp, c_h1, i, 2, h + 1)
                            features(h, (i * 2 + (h + 2)) * PAIR)
                turns(sp, turn)

            @block.scalar
            def _(_e):
                quad_idx = load_idx_loop(c_msg)

                def layer1(i, h):
                    at(act, c_h1, i, 2, h + 1)
                    at(act, c_h2, i, 2, h - 1)
                    act.activation(H1[:, h % 2, :], bank[0][:, :], ACT.Silu, bias=biasc[:, 0:1]).then_inc(c_h1s.sem, 1)

                def layer2(i, h):
                    at(act, c_h2, i, 2, h + 1)
                    at(act, c_tp, i, QUADS, 2 * h - 2)
                    act.activation(H2[:, h % 2, :], bank[1][:, :], ACT.Silu, bias=biasc[:, 1:2]).then_inc(c_h2s.sem, 1)

                def onehot(i, q):
                    at(act, c_rows, i, QUADS, q + 1 - QUADS)
                    for k, s in enumerate(slots_of(q)):
                        ins = act.activation(OH[:, s, :], ramp[:], ACT.Abs, bias=place[:, bass.ds(i * SLOTS + (q * QUAD + k), 1)], scale=-1.0)
                    ins.then_inc(c_far.sem, 1)
                    at(act, c_far, i, QUADS, q + 1)
                    act.activation(quad(OH, q % QUADS), quad(OH, q % QUADS), ACT.Relu, bias=1.0, scale=-1.0).then_inc(c_onehot.sem, 1)

                layer1(0, 0)
                layer2(0, 0)
                onehot(0, 0)
                onehot(0, 1)

                layer1(0, 1)

                def turn(i, last):
                    layer2(i, 1)
                    quad_idx(i, 0)
                    onehot(i, 2)
                    if not last:
                        layer1(i, 2)
                    quad_idx(i, 1)
                    onehot(i, 3)
                    if not last:
                        layer2(i, 2)
                    quad_idx(i, 2)
                    if not last:
                        onehot(i, 4)
                        layer1(i, 3)
                    quad_idx(i, 3)
                    if not last:
                        onehot(i, 5)
                turns(act, turn)

            @block.tensor
            def _(_e):
                def product1(i, h):
                    at(pe, c_ef[h % 2], i, 16, 16 * (1 + h // 2))
                    at(pe, c_h1s, i, 2, h)
                    pe.matmul(bank[0][:, :], A1, ef[:, h % 2, :], start=True, stop=True).then_inc(c_h1.sem, 1)

                def product2(i, h):
                    at(pe, c_h1s, i, 2, h + 1)
                    at(pe, c_h2s, i, 2, h)
                    pe.matmul(bank[1][:, :], A2, H1[:, h % 2, :], start=True, stop=True).then_inc(c_h2.sem, 1)

                def product3(i, q):
                    h, j = q // 2, q % 2
                    hid = slice(j * HID, (j + 1) * HID)
                    at(pe, c_h2s, i, 2, h + 1)
                    at(pe, c_msg, i, QUADS, q - 1)
                    for t in range(QUAD):
                        ins = pe.matmul(bank[2 + j][:, t * P:(t + 1) * P], H2[hid, h % 2, t * P:(t + 1) * P], A3[hid, :], start=True, stop=True)
                    ins.then_inc(c_tp.sem, 1)

                def sum_up(i, q):
                    at(pe, c_msg, i, QUADS, q + 1)
                    at(pe, c_onehot, i, QUADS, q + 1)
                    at(pe, c_added, i, SLOTS, (q - 1) * QUAD)
                    for s in range(q * QUAD, (q + 1) * QUAD):
                        for part in range(2):
                            o = bank[4 + 2 * (q % 2) + (s % QUAD) // 2][:, ((s % 2) * 2 + part) * P:((s % 2) * 2 + part + 1) * P]
                            ins = pe.matmul(o, msg[:, s, part * D:(part + 1) * D], OH[:, s, :], start=True, stop=True)
                    ins.then_inc(c_rows.sem, 1)

                product1(0, 0)
                product2(0, 0)
                product3(0, 0)
                product3(0, 1)
                product1(0, 1)

                def turn(i, last):
                    product2(i, 1)
                    sum_up(i, 0)
                    product3(i, 2)
                    if not last:
                        product1(i, 2)
                    sum_up(i, 1)
                    product3(i, 3)
                    if not last:
                        product2(i, 2)
                    sum_up(i, 2)
                    if not last:
                        product3(i, 4)
                        product1(i, 3)
                    sum_up(i, 3)
                    if not last:
                        product3(i, 5)
                turns(pe, turn)

            @block.vector
            def _(_e):
                def messages(i, q):
                    j, h, turn_q, q = q % 2, q % QUADS // 2, q, q % QUADS
                    at(dve, c_rows, i, QUADS, turn_q + 1 - QUADS)
                    for s in range(q * QUAD, (q + 1) * QUAD):
                        at(dve, c_gather[s], i, 16, 16 * (1 + turn_q // QUADS))
                    if q % 2 == 0:
                        at(dve, c_ea[h], i, 16, 16 * (1 + turn_q // QUADS))
                    at(dve, c_tp, i, QUADS, turn_q + 1)
                    w = bank[2 + j][:, :].rearrange("p (s g u) -> p s g u", s=QUAD, g=4)
                    g = G[:, q * QUAD:(q + 1) * QUAD, 0:D].rearrange("p s (g u) -> p s g u", g=4)
                    y = ea[:, h, (q % 2) * QUAD:(q % 2 + 1) * QUAD, :]
                    mq = msg[:, q * QUAD:(q + 1) * QUAD, :]
                    ys = y[:, :, 0:1].to_broadcast([P, QUAD, MUL])
                    yv = y[:, :, 1:4].unsqueeze(3).to_broadcast([P, QUAD, 3, MUL])
                    n = QUAD * MUL
                    ss_w0, ss_w1, ys_w2, dot = (tmp[:, (8 * j + k) * n:(8 * j + k + 1) * n].rearrange("p (s u) -> p s u", u=MUL) for k in range(4))
                    prod = tmp[:, (8 * j + 4) * n:(8 * j + 7) * n].rearrange("p (s i u) -> p s i u", s=QUAD, i=3)
                    v1 = mq[:, :, 2 * MUL:].rearrange("p s (i k u) -> p s i k u", i=3, k=2)
                    dve.tensor_tensor(ss_w0, g[:, :, 0, :], w[:, :, 0, :], ALU.mult)
                    yield
                    dve.tensor_tensor(ss_w1, g[:, :, 0, :], w[:, :, 1, :], ALU.mult)
                    dve.tensor_tensor(prod, g[:, :, 1:4, :], yv, ALU.mult).then_inc(c_step.sem, 1)
                    yield
                    dve.tensor_tensor(ys_w2, ys, w[:, :, 2, :], ALU.mult)
                    at(dve, c_step, i, 3 * QUADS, 3 * turn_q + 1)
                    dve.tensor_tensor(dot, prod[:, :, 0, :], prod[:, :, 1, :], ALU.add).then_inc(c_step.sem, 1)
                    yield
                    dve.tensor_tensor(mq[:, :, 0:MUL], ss_w0, ys, ALU.mult)
                    at(dve, c_step, i, 3 * QUADS, 3 * turn_q + 2)
                    dve.tensor_tensor(dot, dot, prod[:, :, 2, :], ALU.add).then_inc(c_step.sem, 1)
                    dve.tensor_tensor(v1[:, :, :, 0, :], ss_w1.unsqueeze(2).to_broadcast([P, QUAD, 3, MUL]), yv, ALU.mult)
                    dve.tensor_tensor(v1[:, :, :, 1, :], g[:, :, 1:4, :], ys_w2.unsqueeze(2).to_broadcast([P, QUAD, 3, MUL]), ALU.mult)
                    at(dve, c_step, i, 3 * QUADS, 3 * turn_q + 3)
                    dve.scalar_tensor_tensor(mq[:, :, MUL:2 * MUL], dot, float(3.0 ** -0.5), w[:, :, 3, :], ALU.mult, ALU.mult).then_inc(c_msg.sem, 1)

                def messages_and_adds(i, q_messages, q_add):
                    steps = messages(i, q_messages) if q_messages is not None else iter(())
                    next(steps, None)
                    if q_add is not None:
                        windows = windows_of(DVE, i, q_add)
                        for k in range(QUAD):
                            if k == 0:
                                at(dve, c_rows, i, QUADS, q_add + 1)
                            at(dve, c_added, i, SLOTS, q_add * QUAD + k)
                            w = sums[:, :, bass.ds(windows[k], P)]
                            o = bank[4 + 2 * (q_add % 2) + k // 2][:, (k % 2) * 2 * P:((k % 2) * 2 + 2) * P].rearrange("p (k n) -> p k n", k=2)
                            dve.tensor_tensor(w, w, o, ALU.add).then_inc(c_added.sem, 1)
                            next(steps, None)
                    for _ in steps:
                        pass

                def turn(i, first, last):
                    for q in range(QUADS):
                        messages_and_adds(i, None if last and q + 1 == QUADS else q + 1, None if first and q == 0 else q - 1)

                messages_and_adds(0, 0, None)
                turn(0, True, False)
                with dve.Fori(0, TURNS - 2) as i:
                    turn(i + 1, False, False)
                turn(TURNS - 1, False, True)
                messages_and_adds(TURNS - 1, None, QUADS - 1)
        finish([(c, 16 * TURNS) for c in c_gather + c_ef + c_ea] + [(c_idx, QUADS * (TURNS + 1)), (c_added, SLOTS * TURNS)])
        pr.barrier()
        nextN = hT[:].rearrange("p (b d) -> p b d", d=D)

        def with_residual(cut, psum, m):
            wait("dve", m)
            return mark("dve", dve.tensor_tensor(aggT[:, cut], psum, xT[:, cut], ALU.add))
        layer_norm(nextN, aggT, product_T([(wout[0], aggT), (wout[1], spare)], with_residual), out)
        pr.all_dmas("sp")


def kernel(**inputs):
    import concourse.bacc as bacc
    from concourse.bass_utils import run_bass_kernel_spmd

    x = {k: np.asarray(v) for k, v in inputs.items()}

    def padded(v, rows, fill=0):
        return np.concatenate([v, np.full((rows - v.shape[0],) + v.shape[1:], fill, v.dtype)])

    def tiles(v):
        return np.swapaxes(v.reshape((TILES, P) + v.shape[1:]), 0, 1)

    src, dst = padded(x["src"], EP), padded(x["dst"], EP, NO_NODE)
    up_v = np.zeros((3, D, MUL), np.float32)
    for i in range(3):
        up_v[i, MUL + i::3, :] = x["L3_gnn_W_up_v"]
    arrays = {
        "x": padded(x["x"], NP),
        "src_tile": np.concatenate([tiles(src), np.zeros((P, SLOTS), src.dtype)], axis=1),
        "dst_tile": tiles(dst),
        "dst_first": dst[::P],
        "dst_line": np.concatenate([np.full(1, -1, dst.dtype), dst, np.full(1, 2 * NO_NODE, dst.dtype)]),
        "edge_attrs": tiles(padded(x["edge_attr_4"], EP)).reshape(P, TILES * 4),
        "edge_feats": padded(x["edge_attr_8"], EP).reshape(2 * TURNS, 2, QUAD * P, FEATS)
        .transpose(1, 3, 0, 2).reshape(2 * FEATS, 2 * TURNS * QUAD * P),
        "W_msg": x["L0_gnn_W_msg"], "W_att": x["L0_gnn_W_att"],
        "b_msg": x["L0_gnn_b_msg"].reshape(1, D), "b_att": x["L0_gnn_b_att"].reshape(1, 1),
        "W_ih": x["L0_gnn_W_ih"].T, "W_hh": x["L0_gnn_W_hh"].T,
        "b_ih": x["L0_gnn_b_ih"].reshape(3, D).T, "b_hh": x["L0_gnn_b_hh"].reshape(3, D).T,
        "bn": np.stack([x["L0_gnn_gamma"], x["L0_gnn_beta"]], axis=1),
        "Wq": x["L1_gnn_Wq"], "Wk": x["L1_gnn_Wk"], "Wv": x["L1_gnn_Wv"], "Ws": x["L1_gnn_Ws"],
        "bq": x["L1_gnn_bq"].reshape(TRANSFORMERS, D, 1), "bk": x["L1_gnn_bk"], "bv": x["L1_gnn_bv"], "bs_col": x["L1_gnn_bs"].reshape(TRANSFORMERS, D, 1),
        "b_sage_col": np.stack([x[f"L2_gnn_b{l}"] for l in range(3)]).reshape(3, D, 1),
        "W_up_s": x["L3_gnn_W_up_s"], "W_up_v": up_v,
        "A1": x["L3_gnn_A1"], "A2": x["L3_gnn_A2"], "A3": x["L3_gnn_A3"],
        "b1": x["L3_gnn_b1"].reshape(HID, 1), "b2": x["L3_gnn_b2"].reshape(HID, 1),
        "W_out_s": x["L3_gnn_W_out_s"], "W_out_v": x["L3_gnn_W_out_v"],
    }
    for l in range(3):
        arrays[f"W_l{l}"], arrays[f"W_r{l}"] = x[f"L2_gnn_W_l{l}"], x[f"L2_gnn_W_r{l}"]
    arrays = {f"in_{k}": np.ascontiguousarray(v) for k, v in arrays.items()}

    nc = bacc.Bacc("TRN2", target_bir_lowering=False, num_devices=1)
    drams = {k[3:]: nc.dram_tensor(k, v.shape, mybir.dt.from_np(v.dtype), kind="ExternalInput").ap() for k, v in arrays.items()}
    out = nc.dram_tensor("out", (NP, D), F32, kind="ExternalOutput").ap()
    build_program(nc, drams, out)
    result = run_bass_kernel_spmd(nc, [arrays], core_ids=[0])
    return result.results[0]["out"][:NODES]
```
